# Optimizing a Trainium2 kernel written in Bass

```python
import numpy as np
import jax
import jax.numpy as jnp

def _softmax(x, axis=-1):
    return jax.nn.softmax(x, axis=axis)

def _gelu(x):
    return jax.nn.gelu(x, approximate=True)

def _silu(x):
    return jax.nn.silu(x)

def _sigmoid(x):
    return jax.nn.sigmoid(x)

def _layernorm(x, axis=-1, eps=1e-05):
    m = jnp.mean(x, axis=axis, keepdims=True)
    v = jnp.var(x, axis=axis, keepdims=True)
    return (x - m) / jnp.sqrt(v + eps)

def _scatter_add(tgt, idx, src, axis=0):
    return tgt.at[idx].add(src)

def _segment_sum(src, seg, n):
    return jax.ops.segment_sum(src, seg, n)
kernel_name = 'mk_decoder_postln_d2_seqx_r4_feedb4'

def setup_inputs(seed: int=0):
    np.random.seed(seed)
    _w = jnp.asarray

    def _rec_inputs():
        import jax
        import jax.numpy as jnp
        _rk = jax.random.key(seed)
        x = -0.0003929 + 0.9999 * jax.random.normal(jax.random.fold_in(_rk, 1), (4, 1024, 256), jnp.float32)
        _lenS = 1024 - jax.random.randint(jax.random.fold_in(_rk, 7), (4,), 0, max(1, 1024 // 4) + 1, jnp.int32)
        _lenS2 = 77 - jax.random.randint(jax.random.fold_in(_rk, 8), (4,), 0, max(1, 77 // 4) + 1, jnp.int32)
        _ctx_1024P = jax.random.normal(jax.random.fold_in(_rk, 11), (4, 16, 256), jnp.float32)
        _ctx_1024c = jax.random.dirichlet(jax.random.fold_in(_rk, 511), 0.3 * jnp.ones((16,), jnp.float32), (4, 77))
        _ctx_1024t = jnp.einsum('bsk,bkd->bsd', _ctx_1024c, _ctx_1024P)
        _ctx_1024t = _ctx_1024t * jax.lax.rsqrt(jnp.mean(jnp.square(_ctx_1024t)) + 1e-12) * 0.953939
        ctx_1024 = 2.81802e-05 + 1.00001 * (_ctx_1024t + 0.3 * jax.random.normal(jax.random.fold_in(_rk, 611), (4, 77, 256), jnp.float32))
        return (x, ctx_1024)
    x, ctx_1024 = _rec_inputs()

    def _L0_attn_setup():
        import jax, jax.numpy as jnp
        import numpy as np
        N_HEADS = 16
        INPUT_DIM = 256
        EMBED_DIM = 256
        KEY_DIM = EMBED_DIM // N_HEADS
        BATCH = 4
        SEQ = 512

        def _uniform(key, shape, bound):
            return jax.random.uniform(key, shape, jnp.float32, -bound, bound)
        key = jax.random.key(seed)
        kq, k1, k2, k3, k4 = jax.random.split(key, 5)
        stdv_k = 1.0 / np.sqrt(KEY_DIM)
        stdv_e = 1.0 / np.sqrt(EMBED_DIM)
        return {'q': jax.random.normal(kq, (BATCH, SEQ, INPUT_DIM), jnp.float32), 'W_query': _uniform(k1, (N_HEADS, INPUT_DIM, KEY_DIM), stdv_k), 'W_key': _uniform(k2, (N_HEADS, INPUT_DIM, KEY_DIM), stdv_k), 'W_val': _uniform(k3, (N_HEADS, INPUT_DIM, KEY_DIM), stdv_k), 'W_out': _uniform(k4, (N_HEADS, KEY_DIM, EMBED_DIM), stdv_e)}
    _L0_attn_all = _L0_attn_setup()
    _L0_attn_in = {k: v for k, v in _L0_attn_all.items() if k in ('W_query', 'W_key', 'W_val', 'W_out')}
    del _L0_attn_all

    def _L0_xattn_setup():
        import jax, jax.numpy as jnp
        import numpy as np
        DIM = 256
        SCALE_DIM = 4
        QK_DIM = DIM // SCALE_DIM
        B, S = (4, 1024)
        key = jax.random.key(seed)
        ks = jax.random.split(key, 8)
        std = 1.0 / np.sqrt(DIM)
        return {'q': jax.random.normal(ks[0], (B, S, DIM), jnp.float32), 'k': jax.random.normal(ks[1], (B, S, DIM), jnp.float32), 'v': jax.random.normal(ks[2], (B, S, DIM), jnp.float32), 'Wq': jax.random.normal(ks[3], (QK_DIM, DIM), jnp.float32) * std, 'bq': jnp.zeros((QK_DIM,), jnp.float32), 'Wk': jax.random.normal(ks[4], (QK_DIM, DIM), jnp.float32) * std, 'bk': jnp.zeros((QK_DIM,), jnp.float32), 'Wv': jax.random.normal(ks[5], (DIM, DIM), jnp.float32) * std, 'bv': jnp.zeros((DIM,), jnp.float32)}
    _L0_xattn_all = _L0_xattn_setup()
    _L0_xattn_in = {k: v for k, v in _L0_xattn_all.items() if k in ('Wq', 'bq', 'Wk', 'bk', 'Wv', 'bv')}
    del _L0_xattn_all

    def _L0_ffn_setup():
        import jax, jax.numpy as jnp
        import numpy as np
        B, T, D = (2, 512, 256)
        DCD = 1024
        RET = 128
        NEXP = 1024
        NKEYS = 64
        H = 4
        KPH = 8
        key = jax.random.key(seed)
        ks = jax.random.split(key, 10)
        s = lambda k, shape, scale: jax.random.normal(k, shape, jnp.float32) * scale
        return {'hidden_states': jax.random.normal(ks[0], (B, T, D), jnp.float32), 'Wg': s(ks[1], (D, DCD), 0.02), 'bg': jnp.zeros((DCD,), jnp.float32), 'Wu': s(ks[2], (D, DCD), 0.02), 'bu': jnp.zeros((DCD,), jnp.float32), 'Wd': s(ks[3], (DCD, D), 0.02), 'bd': jnp.zeros((D,), jnp.float32), 'Wq': s(ks[4], (D, RET * H), 0.02), 'keys': s(ks[5], (H, NKEYS, 2, RET // 2), 0.02), 'down_embed': s(ks[6], (NEXP, D), 0.02), 'up_embed': s(ks[7], (NEXP, D), 0.02)}
    _L0_ffn_all = _L0_ffn_setup()
    _L0_ffn_in = {k: v for k, v in _L0_ffn_all.items() if k in ('Wg', 'bg', 'Wu', 'bu', 'Wd', 'bd', 'Wq', 'keys', 'down_embed', 'up_embed')}
    del _L0_ffn_all

    def _L1_attn_setup():
        import jax, jax.numpy as jnp
        import numpy as np
        DIM = 256
        HEADS = 16
        EPS = 1e-12
        key = jax.random.key(seed)
        ks = jax.random.split(key, 6)
        b, n, dim, h = (2, 512, DIM, HEADS)
        x = jax.random.normal(ks[0], (b, n, dim), dtype=jnp.float32)
        w_qkv = jax.random.normal(ks[1], (3 * dim, dim), dtype=jnp.float32) / np.sqrt(dim)
        w_out = jax.random.normal(ks[2], (dim, dim), dtype=jnp.float32) / np.sqrt(dim)
        b_out = jax.random.normal(ks[3], (dim,), dtype=jnp.float32) * 0.02
        norm_g = jnp.ones((1, h, 1, 1), dtype=jnp.float32)
        norm_b = jnp.zeros((1, h, 1, 1), dtype=jnp.float32)
        return {'x': x, 'w_qkv': w_qkv, 'w_out': w_out, 'b_out': b_out, 'norm_g': norm_g, 'norm_b': norm_b}
    _L1_attn_all = _L1_attn_setup()
    _L1_attn_in = {k: v for k, v in _L1_attn_all.items() if k in ('w_qkv', 'w_out', 'b_out', 'norm_g', 'norm_b')}
    del _L1_attn_all

    def _L1_xattn_setup():
        import jax, jax.numpy as jnp
        import numpy as np
        B, N, D, K = (4, 1024, 256, 128)
        key = jax.random.key(seed)
        ks = jax.random.split(key, 5)
        q = jax.random.normal(ks[0], (B, N, D), dtype=jnp.float32)
        k = jax.random.normal(ks[1], (B, N, D), dtype=jnp.float32)
        weight = jax.random.normal(ks[2], (D, K), dtype=jnp.float32)
        kp_w = jax.random.normal(ks[3], (D, D), dtype=jnp.float32) * (1.0 / np.sqrt(D))
        kp_b = jax.random.normal(ks[4], (D,), dtype=jnp.float32) * 0.01
        return {'q': q, 'k': k, 'weight': weight, 'kp_w': kp_w, 'kp_b': kp_b}
    _L1_xattn_all = _L1_xattn_setup()
    _L1_xattn_in = {k: v for k, v in _L1_xattn_all.items() if k in ('weight', 'kp_w', 'kp_b')}
    del _L1_xattn_all

    def _L1_ffn_setup():
        import jax, jax.numpy as jnp
        import numpy as np
        D_MODEL = 256
        D1, D2 = (32, 32)
        F1, F2 = (64, 64)
        E = 64
        TOP_K = 2

        def kmoe(x_flat, W_router, A, B, scale, bias, d_in1, d_in2, d_out1, d_out2, top_k):
            logits = x_flat @ W_router.T
            vals, idx = jax.lax.top_k(logits, top_k)
            probs = jax.nn.softmax(vals, axis=-1)
            xs = x_flat.reshape(-1, d_in1, d_in2)
            Ag = A[idx]
            Bg = B[idx]
            Y = jnp.einsum('nkoi,nij,nkpj->nkop', Ag, xs, Bg)
            out = jnp.einsum('nkop,nk->nop', Y, probs).reshape(-1, d_out1 * d_out2)
            return out * scale + bias
        key = jax.random.key(seed)
        ks = jax.random.split(key, 12)
        s = 0.02
        return {'x': jax.random.normal(ks[0], (4, 512, D_MODEL), dtype=jnp.float32), 'W_up': jax.random.normal(ks[1], (E, D1 * D2), dtype=jnp.float32) * s, 'A_up': jax.random.normal(ks[2], (E, F1, D1), dtype=jnp.float32) * s, 'B_up': jax.random.normal(ks[3], (E, F2, D2), dtype=jnp.float32) * s, 'scale_up': jnp.ones((1,), dtype=jnp.float32), 'bias_up': jnp.zeros((F1 * F2,), dtype=jnp.float32), 'W_down': jax.random.normal(ks[4], (E, F1 * F2), dtype=jnp.float32) * s, 'A_down': jax.random.normal(ks[5], (E, D1, F1), dtype=jnp.float32) * s, 'B_down': jax.random.normal(ks[6], (E, D2, F2), dtype=jnp.float32) * s, 'scale_down': jnp.ones((1,), dtype=jnp.float32), 'bias_down': jnp.zeros((D1 * D2,), dtype=jnp.float32)}
    _L1_ffn_all = _L1_ffn_setup()
    _L1_ffn_in = {k: v for k, v in _L1_ffn_all.items() if k in ('W_up', 'A_up', 'B_up', 'scale_up', 'bias_up', 'W_down', 'A_down', 'B_down', 'scale_down', 'bias_down')}
    del _L1_ffn_all
    return {'x': x, 'ctx_1024': ctx_1024, 'L0_attn_W_query': _L0_attn_in['W_query'], 'L0_attn_W_key': _L0_attn_in['W_key'], 'L0_attn_W_val': _L0_attn_in['W_val'], 'L0_attn_W_out': _L0_attn_in['W_out'], 'L0_xattn_Wq': _L0_xattn_in['Wq'], 'L0_xattn_bq': _L0_xattn_in['bq'], 'L0_xattn_Wk': _L0_xattn_in['Wk'], 'L0_xattn_bk': _L0_xattn_in['bk'], 'L0_xattn_Wv': _L0_xattn_in['Wv'], 'L0_xattn_bv': _L0_xattn_in['bv'], 'L0_ffn_Wg': _L0_ffn_in['Wg'], 'L0_ffn_bg': _L0_ffn_in['bg'], 'L0_ffn_Wu': _L0_ffn_in['Wu'], 'L0_ffn_bu': _L0_ffn_in['bu'], 'L0_ffn_Wd': _L0_ffn_in['Wd'], 'L0_ffn_bd': _L0_ffn_in['bd'], 'L0_ffn_Wq': _L0_ffn_in['Wq'], 'L0_ffn_keys': _L0_ffn_in['keys'], 'L0_ffn_down_embed': _L0_ffn_in['down_embed'], 'L0_ffn_up_embed': _L0_ffn_in['up_embed'], 'L1_attn_w_qkv': _L1_attn_in['w_qkv'], 'L1_attn_w_out': _L1_attn_in['w_out'], 'L1_attn_b_out': _L1_attn_in['b_out'], 'L1_attn_norm_g': _L1_attn_in['norm_g'], 'L1_attn_norm_b': _L1_attn_in['norm_b'], 'L1_xattn_weight': _L1_xattn_in['weight'], 'L1_xattn_kp_w': _L1_xattn_in['kp_w'], 'L1_xattn_kp_b': _L1_xattn_in['kp_b'], 'L1_ffn_W_up': _L1_ffn_in['W_up'], 'L1_ffn_A_up': _L1_ffn_in['A_up'], 'L1_ffn_B_up': _L1_ffn_in['B_up'], 'L1_ffn_scale_up': _L1_ffn_in['scale_up'], 'L1_ffn_bias_up': _L1_ffn_in['bias_up'], 'L1_ffn_W_down': _L1_ffn_in['W_down'], 'L1_ffn_A_down': _L1_ffn_in['A_down'], 'L1_ffn_B_down': _L1_ffn_in['B_down'], 'L1_ffn_scale_down': _L1_ffn_in['scale_down'], 'L1_ffn_bias_down': _L1_ffn_in['bias_down']}

def reference(x, ctx_1024, L0_attn_W_query, L0_attn_W_key, L0_attn_W_val, L0_attn_W_out, L0_xattn_Wq, L0_xattn_bq, L0_xattn_Wk, L0_xattn_bk, L0_xattn_Wv, L0_xattn_bv, L0_ffn_Wg, L0_ffn_bg, L0_ffn_Wu, L0_ffn_bu, L0_ffn_Wd, L0_ffn_bd, L0_ffn_Wq, L0_ffn_keys, L0_ffn_down_embed, L0_ffn_up_embed, L1_attn_w_qkv, L1_attn_w_out, L1_attn_b_out, L1_attn_norm_g, L1_attn_norm_b, L1_xattn_weight, L1_xattn_kp_w, L1_xattn_kp_b, L1_ffn_W_up, L1_ffn_A_up, L1_ffn_B_up, L1_ffn_scale_up, L1_ffn_bias_up, L1_ffn_W_down, L1_ffn_A_down, L1_ffn_B_down, L1_ffn_scale_down, L1_ffn_bias_down):
    import jax
    import jax.numpy as jnp

    def _L0_attn_ref(q, W_query, W_key, W_val, W_out):
        import jax, jax.numpy as jnp
        import numpy as np
        N_HEADS = 16
        INPUT_DIM = 256
        EMBED_DIM = 256
        KEY_DIM = EMBED_DIM // N_HEADS
        BATCH = 4
        SEQ = 512

        def _uniform(key, shape, bound):
            return jax.random.uniform(key, shape, jnp.float32, -bound, bound)
        norm = 1.0 / np.sqrt(KEY_DIM)
        Q = jnp.einsum('bsd,hdk->hbsk', q, W_query)
        K = jnp.einsum('bsd,hdk->hbsk', q, W_key)
        V = jnp.einsum('bsd,hdv->hbsv', q, W_val)
        scores = norm * jnp.einsum('hbqk,hbnk->hbqn', Q, K)
        attn = jax.nn.softmax(scores, axis=-1)
        heads = jnp.einsum('hbqn,hbnv->hbqv', attn, V)
        out = jnp.einsum('hbqv,hve->bqe', heads, W_out)
        return out

    def _L0_xattn_ref(q, k, v, Wq, bq, Wk, bk, Wv, bv):
        import jax, jax.numpy as jnp
        import numpy as np
        DIM = 256
        SCALE_DIM = 4
        QK_DIM = DIM // SCALE_DIM
        B, S = (4, 1024)
        scale = jnp.asarray(np.sqrt(QK_DIM), q.dtype)
        qp = jnp.einsum('bsd,ed->bse', q, Wq) + bq
        kp = jnp.einsum('bsd,ed->bse', k, Wk) + bk
        vp = jnp.einsum('bsd,ed->bse', v, Wv) + bv
        z = jnp.einsum('bqe,bke->bqk', qp, kp)
        z = jax.nn.sigmoid(z / scale)
        return jnp.einsum('bqk,bkd->bqd', z, vp)

    def _L0_ffn_ref(hidden_states, Wg, bg, Wu, bu, Wd, bd, Wq, keys, down_embed, up_embed):
        import jax, jax.numpy as jnp
        import numpy as np
        B, T, D = (2, 512, 256)
        DCD = 1024
        RET = 128
        NEXP = 1024
        NKEYS = 64
        H = 4
        KPH = 8
        b, t, d = hidden_states.shape
        q = (hidden_states @ Wq).reshape(b, t, 2, H, RET // 2)
        sim = jnp.einsum('btphn,hkpn->pbthk', q, keys)
        sc, ix = jax.lax.top_k(sim, KPH)
        sx, sy = (sc[0], sc[1])
        ixx, ixy = (ix[0], ix[1])
        all_sc = (sx[..., :, None] + sy[..., None, :]).reshape(b, t, H, KPH * KPH)
        all_ix = (ixx[..., :, None] * NKEYS + ixy[..., None, :]).reshape(b, t, H, KPH * KPH)
        scores, pk = jax.lax.top_k(all_sc, KPH)
        idx = jnp.take_along_axis(all_ix, pk, axis=-1)
        de = down_embed[idx]
        ue = up_embed[idx]
        w = jnp.einsum('btd,bthkd->bthk', hidden_states, de)
        w = jax.nn.silu(w) * jax.nn.softmax(scores, axis=-1)
        experts_states = jnp.einsum('bthk,bthkd->btd', w, ue)
        mlp = jax.nn.silu(hidden_states @ Wg + bg) * (hidden_states @ Wu + bu) @ Wd + bd
        return mlp + experts_states

    def _L1_attn_ref(x, w_qkv, w_out, b_out, norm_g, norm_b):
        import jax, jax.numpy as jnp
        import numpy as np
        DIM = 256
        HEADS = 16
        EPS = 1e-12
        b, n, dim = x.shape
        h = HEADS
        d = dim // h
        qkv = jnp.einsum('bnm,om->bno', x, w_qkv)
        qkv = qkv.reshape(b, n, 3, h, d)
        q, k, v = [jnp.transpose(qkv[:, :, i], (0, 2, 1, 3)) for i in range(3)]
        dots = jnp.einsum('bhid,bhjd->bhij', q, k)
        norm = jnp.sqrt(jnp.sum(dots * dots, axis=-1, keepdims=True))
        attn = dots / jnp.maximum(norm, EPS) * norm_g + norm_b
        out = jnp.einsum('bhij,bhjd->bhid', attn, v)
        out = jnp.transpose(out, (0, 2, 1, 3)).reshape(b, n, dim)
        return jnp.einsum('bnm,om->bno', out, w_out) + b_out

    def _L1_xattn_ref(q, k, weight, kp_w, kp_b):
        import jax, jax.numpy as jnp
        import numpy as np
        B, N, D, K = (4, 1024, 256, 128)
        n = q.shape[1]
        k_mod = k.mean(axis=1) @ kp_w.T + kp_b
        dynamic_weight = weight[None, :, :] * k_mod[:, :, None]
        q_f = jnp.fft.rfft(q, axis=1)
        w_f = jnp.fft.rfft(dynamic_weight, n=n, axis=2)
        y_f = q_f * jnp.transpose(w_f, (0, 2, 1))
        y = jnp.fft.irfft(y_f, n=n, axis=1)
        return y.astype(q.dtype)

    def _L1_ffn_ref(x, W_up, A_up, B_up, scale_up, bias_up, W_down, A_down, B_down, scale_down, bias_down):
        import jax, jax.numpy as jnp
        import numpy as np
        D_MODEL = 256
        D1, D2 = (32, 32)
        F1, F2 = (64, 64)
        E = 64
        TOP_K = 2

        def kmoe(x_flat, W_router, A, B, scale, bias, d_in1, d_in2, d_out1, d_out2, top_k):
            logits = x_flat @ W_router.T
            vals, idx = jax.lax.top_k(logits, top_k)
            probs = jax.nn.softmax(vals, axis=-1)
            xs = x_flat.reshape(-1, d_in1, d_in2)
            Ag = A[idx]
            Bg = B[idx]
            Y = jnp.einsum('nkoi,nij,nkpj->nkop', Ag, xs, Bg)
            out = jnp.einsum('nkop,nk->nop', Y, probs).reshape(-1, d_out1 * d_out2)
            return out * scale + bias
        orig_shape = x.shape
        x_flat = x.reshape(-1, D1 * D2)
        h = kmoe(x_flat, W_up, A_up, B_up, scale_up, bias_up, D1, D2, F1, F2, TOP_K)
        h = jax.nn.gelu(h, approximate=False)
        y = kmoe(h, W_down, A_down, B_down, scale_down, bias_down, F1, F2, D1, D2, TOP_K)
        return y.reshape(*orig_shape[:-1], D_MODEL)
    x = _layernorm(x + _L0_attn_ref(x, L0_attn_W_query, L0_attn_W_key, L0_attn_W_val, L0_attn_W_out), axis=-1)
    x = _layernorm(x + _L0_xattn_ref(x, ctx_1024, ctx_1024, L0_xattn_Wq, L0_xattn_bq, L0_xattn_Wk, L0_xattn_bk, L0_xattn_Wv, L0_xattn_bv), axis=-1)
    x = _layernorm(x + _L0_ffn_ref(x, L0_ffn_Wg, L0_ffn_bg, L0_ffn_Wu, L0_ffn_bu, L0_ffn_Wd, L0_ffn_bd, L0_ffn_Wq, L0_ffn_keys, L0_ffn_down_embed, L0_ffn_up_embed), axis=-1)
    x = _layernorm(x + _L1_attn_ref(x, L1_attn_w_qkv, L1_attn_w_out, L1_attn_b_out, L1_attn_norm_g, L1_attn_norm_b), axis=-1)
    x = _layernorm(x + _L1_xattn_ref(x, ctx_1024, L1_xattn_weight, L1_xattn_kp_w, L1_xattn_kp_b), axis=-1)
    x = _layernorm(x + _L1_ffn_ref(x, L1_ffn_W_up, L1_ffn_A_up, L1_ffn_B_up, L1_ffn_scale_up, L1_ffn_bias_up, L1_ffn_W_down, L1_ffn_A_down, L1_ffn_B_down, L1_ffn_scale_down, L1_ffn_bias_down), axis=-1)
    return x

_drawn_inputs = setup_inputs


def setup_inputs(seed=0):
    import zlib

    import numpy as np

    out = dict(_drawn_inputs(seed))
    spreads = {'L0_xattn_bq': (0.0, 0.418),
     'L0_xattn_bk': (0.0, 0.8),
     'L0_xattn_bv': (0.0, 0.1),
     'L0_ffn_bg': (0.0, 0.648),
     'L0_ffn_bu': (0.0, 0.522),
     'L0_ffn_bd': (0.0, 0.1),
     'L1_attn_norm_g': (1.0, 0.2),
     'L1_attn_norm_b': (0.0, 0.1),
     'L1_ffn_bias_up': (0.0, 0.8),
     'L1_ffn_bias_down': (0.0, 0.1)}
    factors = {'L0_ffn_Wq': 8.0,
     'L0_ffn_keys': 8.0,
     'L0_ffn_down_embed': 2.957,
     'L0_ffn_up_embed': 3.388,
     'L1_attn_b_out': 8.0,
     'L1_xattn_kp_b': 3.238,
     'L1_ffn_W_up': 8.0,
     'L1_ffn_A_up': 8.0,
     'L1_ffn_B_up': 8.0,
     'L1_ffn_W_down': 8.0,
     'L1_ffn_A_down': 8.0,
     'L1_ffn_B_down': 8.0}
    for name, (base, spread) in spreads.items():
        noise = np.random.default_rng([zlib.crc32(name.encode()), seed]).standard_normal(out[name].shape)
        drawn = base * np.exp(spread * noise) if base else spread * noise
        out[name] = jnp.asarray(drawn.astype(out[name].dtype))
    for name, factor in factors.items():
        out[name] = (out[name] * factor).astype(out[name].dtype)
    return out
```

```python
from contextlib import ExitStack

import numpy as np

import concourse.bass as bass
from concourse import mybir

F32 = mybir.dt.float32
BF16 = mybir.dt.bfloat16
I32 = mybir.dt.int32
U32 = mybir.dt.uint32
ALU = mybir.AluOpType
ACT = mybir.ActivationFunctionType
AX = mybir.AxisListType
ds = bass.ds

P = 128
B, S, D = 4, 1024, 256
N = B * S
NT = N // P
DT = D // P
CH = 512
NC = N // CH
TPC = CH // P
H0, HD = 16, 16
HG = 4
NG = H0 // HG
KB = S // P
CTX = 77
FF = 1024
NH, NK, TOPK = 4, 64, 8
NX = FF // NK
E = 64
LN_EPS = 1e-5
DEPTH = 2


class Mem:

    def __init__(self, nc, ctx):
        self.nc, self.ctx, self.sems = nc, ctx, []
        ctx.callback(self.release)

    def release(self):
        if self.sems:
            self.nc.clear_and_free_semaphores(self.sems)
            self.nc.all_engine_barrier()

    def sb(self, name, shape, dt=F32):
        return self.ctx.enter_context(self.nc.sbuf_tensor(name, shape, dt))

    def ps(self, name, shape, dt=F32):
        return self.ctx.enter_context(self.nc.psum_tensor(name, shape, dt))

    def sem(self, name):
        self.sems.append(self.nc.alloc_semaphore(name))
        return self.sems[-1]


class Chain:

    def __init__(self, eng, sem, base=0):
        self.eng, self.sem, self.base, self.n = eng, sem, base, 0

    def step(self, ins):
        self.n += 1
        ins.then_inc(self.sem, 1)

    def settle(self):
        self.eng.wait_ge(self.sem, self.base + self.n)

    def link(self, ins):
        self.step(ins)
        self.settle()


def load_tokens(nc, x, X, ident_d, ident, XT):
    with ExitStack() as ctx:
        m = Mem(nc, ctx)
        xstage = m.sb("xstage", [P, DEPTH, D])
        warm = m.sb("warm_in", [P, 1])
        tp = m.ps("tp_in", [P, DEPTH, 512])
        x_landed, id_landed = m.sem("x_landed"), m.sem("id_landed")
        staged, turned, turned_out = m.sem("in_staged"), m.sem("in_turned"), m.sem("in_turned_out")
        block = ctx.enter_context(nc.Block())

        @block.sync
        def _(sp):
            sp.dma_start(ident[:, :], ident_d).then_inc(id_landed, 16)
            sp.dma_start(X[:, :, :], x.rearrange("b (t p) d -> p (b t) d", p=P)).then_inc(x_landed, 16)

        @block.vector
        def _(dve):
            dve.wait_ge(x_landed, 16)
            with dve.Fori(0, NT // DEPTH) as j:
                for s in range(DEPTH):
                    dve.wait_ge(turned, j * DEPTH + s + 1)
                    dve.tensor_copy(xstage[:, s, :], X[:, ds(j * DEPTH + s, 1), :]).then_inc(staged, 1)

        @block.tensor
        def _(pe):
            pe.sem_inc(turned, DEPTH)
            pe.wait_ge(id_landed, 16)
            with pe.Fori(0, NT // DEPTH) as j:
                for s in range(DEPTH):
                    pe.wait_ge(staged, j * DEPTH + s + 1)
                    pe.wait_ge(turned_out, j * DEPTH + s + 1)
                    for k in range(DT):
                        t = pe.transpose(tp[:, s, k * P:(k + 1) * P], xstage[:, s, k * P:(k + 1) * P], ident[:, :])
                    t.then_inc(turned, 1)

        @block.scalar
        def _(act):
            act.wait_ge(id_landed, 16)
            act.activation(warm[:, :], ident[:, 0:1], ACT.Identity)
            act.sem_inc(turned_out, DEPTH)
            with act.Fori(0, NT // DEPTH) as j:
                for s in range(DEPTH):
                    act.wait_ge(turned, j * DEPTH + s + 1 + DEPTH)
                    act.copy(XT[:, :, ds(j * DEPTH * P + s * P, P)],
                             tp[:, s, 0:D].rearrange("p (k t) -> p k t", k=DT)).then_inc(turned_out, 1)


def layer_norm(nc, tag, X, XT, ident):
    with ExitStack() as ctx:
        m = Mem(nc, ctx)
        stats = m.sb("stats" + tag, [P, NT, 6])
        total = m.sb("total" + tag, [P, NT])
        diff = m.sb("diff" + tag, [P, NT])
        var4 = m.sb("var4" + tag, [P, NT])
        std = m.sb("std" + tag, [P, NT])
        rstd = m.sb("rstd" + tag, [P, NT])
        shift = m.sb("shift" + tag, [P, NT])
        eps = m.sb("eps" + tag, [P, 1])
        y = m.sb("y" + tag, [P, DEPTH, D])
        tp = m.ps("tp" + tag, [P, DEPTH, 512])
        stats_done, dve_steps = m.sem("stats_done" + tag), m.sem("ln_steps" + tag)
        var_ready, std_ready = m.sem("var_ready" + tag), m.sem("std_ready" + tag)
        y_ready, turned = m.sem("y_ready" + tag), m.sem("turned" + tag)
        turned_out = m.sem("turned_out" + tag)
        block = ctx.enter_context(nc.Block())

        @block.vector
        def _(dve):
            chain = Chain(dve, dve_steps)
            dve.memset(eps[:, :], LN_EPS).then_inc(var_ready, 1)
            with dve.Fori(0, NT // TPC) as c:
                for t in range(TPC):
                    last = dve.bn_stats(stats[:, ds(c * TPC + t, 1), :], X[:, ds(c * TPC + t, 1), :])
                last.then_inc(stats_done, 1)
            dve.wait_ge(stats_done, NT // TPC)
            chain.step(dve.tensor_tensor(total[:, :], stats[:, :, 1], stats[:, :, 4], ALU.add))
            chain.step(dve.tensor_tensor(diff[:, :], stats[:, :, 1], stats[:, :, 4], ALU.subtract))
            chain.link(dve.tensor_tensor(var4[:, :], stats[:, :, 2], stats[:, :, 5], ALU.add))
            chain.link(dve.tensor_tensor(diff[:, :], diff[:, :], diff[:, :], ALU.mult))
            dve.scalar_tensor_tensor(var4[:, :], var4[:, :], 4.0 / D, diff[:, :], ALU.mult, ALU.add).then_inc(var_ready, 1)
            dve.wait_ge(std_ready, 1)
            chain.link(dve.reciprocal(rstd[:, :], std[:, :]))
            chain.link(dve.scalar_tensor_tensor(shift[:, :], total[:, :], -0.5, rstd[:, :], ALU.mult, ALU.mult))
            with dve.Fori(0, NT // DEPTH) as j:
                for s in range(DEPTH):
                    i = j * DEPTH + s
                    if XT is not None:
                        dve.wait_ge(turned, i + 1)
                        dve.tensor_scalar(y[:, s, :], X[:, ds(i, 1), :], rstd[:, ds(i, 1)], shift[:, ds(i, 1)],
                                          ALU.mult, ALU.add).then_inc(y_ready, 1)
                    dve.tensor_scalar(X[:, ds(i, 1), :], X[:, ds(i, 1), :], rstd[:, ds(i, 1)], shift[:, ds(i, 1)],
                                      ALU.mult, ALU.add)

        @block.scalar
        def _(act):
            if XT is not None:
                act.sem_inc(turned_out, DEPTH)
            act.wait_ge(var_ready, 2)
            act.activation(std[:, :], var4[:, :], ACT.Sqrt, bias=eps[:, 0:1], scale=0.25).then_inc(std_ready, 1)
            if XT is not None:
                with act.Fori(0, NT // DEPTH) as j:
                    for s in range(DEPTH):
                        act.wait_ge(turned, j * DEPTH + s + 1 + DEPTH)
                        act.copy(XT[:, :, ds(j * DEPTH * P + s * P, P)],
                                 tp[:, s, 0:D].rearrange("p (k t) -> p k t", k=DT)).then_inc(turned_out, 1)

        if XT is not None:
            @block.tensor
            def _(pe):
                pe.sem_inc(turned, DEPTH)
                with pe.Fori(0, NT // DEPTH) as j:
                    for s in range(DEPTH):
                        pe.wait_ge(y_ready, j * DEPTH + s + 1)
                        pe.wait_ge(turned_out, j * DEPTH + s + 1)
                        for k in range(DT):
                            t = pe.transpose(tp[:, s, k * P:(k + 1) * P], y[:, s, k * P:(k + 1) * P], ident[:, :])
                        t.then_inc(turned, 1)


def store_tokens(nc, X, out):
    with ExitStack() as ctx:
        m = Mem(nc, ctx)
        stored = m.sem("stored")
        block = ctx.enter_context(nc.Block())

        @block.sync
        def _(sp):
            sp.dma_start(out.rearrange("b (t p) d -> p (b t) d", p=P), X[:, :, :]).then_inc(stored, 16)
            sp.wait_ge(stored, 16)


STACK = 6 * HD
ROWS = STACK + 3
PAIRS = [(0, 0), (1, 0), (2, 0), (0, 1), (1, 1), (0, 2)]


def attention_project(nc, a, XT, q_parts, k_parts, v_rows):
    with ExitStack() as ctx:
        m = Mem(nc, ctx)
        wqk = m.sb("wqk", [P, 2, DT, D])
        wv = m.sb("wv", [P, DT, D])
        xs = m.sb("xs_p0", [P, DEPTH, DT, CH])
        parts = m.sb("parts", [P, DEPTH, 3, CH], BF16)
        rest = m.sb("rest", [P, DEPTH, CH])
        v_out = m.sb("v_out", [P, DEPTH, 2, H0, 2, HD])
        warm = m.sb("warm_p0", [P, 1])
        pp = m.ps("pp", [P, DEPTH, CH])
        pv = m.ps("pv", [P, DEPTH, 2, D])
        w_landed, xs_ready = m.sem("w_landed_p0"), m.sem("xs_ready_p0")
        p_ready, high_ready, rest_ready = m.sem("p_ready"), m.sem("high_ready"), m.sem("rest_ready")
        mid_ready, low_ready = m.sem("mid_ready"), m.sem("low_ready")
        parts_kept = [m.sem(f"parts_kept{s}") for s in range(DEPTH)]
        v_kept = [m.sem(f"v_kept{s}") for s in range(DEPTH)]
        v_ready, v_copied = m.sem("v_ready"), m.sem("v_copied")
        PER = 2 * DT
        block = ctx.enter_context(nc.Block())

        @block.sync
        def _(sp):
            sp.dma_start(wqk[:, 0, :, :], a["wq0"].rearrange("(k p) f -> p k f", p=P)).then_inc(w_landed, 16)
            sp.dma_start(wqk[:, 1, :, :], a["wk0"].rearrange("(k p) f -> p k f", p=P)).then_inc(w_landed, 16)
            sp.dma_start(wv[:, :, :], a["wv0"].rearrange("(k p) f -> p k f", p=P)).then_inc(w_landed, 16)
            for s in range(DEPTH):
                sp.sem_inc(parts_kept[s], 16)
                sp.sem_inc(v_kept[s], 32)
            with sp.Fori(0, B) as b:
                for half in range(S // CH):
                    c = b * (S // CH) + half
                    for o in range(PER):
                        dst = (q_parts, k_parts)[o // DT][:, ds(b * D + (o % DT) * P, P), half * CH:(half + 1) * CH]
                        sp.wait_ge(low_ready, c * PER + o + 1)
                        sp.dma_start(dst.rearrange("l f t -> f l t"),
                                     parts[:, o % DEPTH, :, :]).then_inc(parts_kept[o % DEPTH], 16)
                    for s in range(DEPTH):
                        for t in range(2):
                            sp.wait_ge(v_copied, c * DEPTH + s + 1 + DEPTH)
                            row = half * CH + (s * 2 + t) * P
                            sp.dma_start(v_rows[ds(b * NG, NG), row:row + P, :].rearrange("g p f -> p g f"),
                                         v_out[:, s, t, :, :, :].rearrange("p (g h) o w -> p g (h o w)", g=NG)
                                         ).then_inc(v_kept[s], 16)
            for s in range(DEPTH):
                sp.wait_ge(parts_kept[s], 16 * (1 + NC * PER // DEPTH))
                sp.wait_ge(v_kept[s], 32 * (1 + NC))

        @block.gpsimd
        def _(pool):
            with pool.Fori(0, NC // DEPTH) as j:
                for s in range(DEPTH):
                    pool.wait_ge(v_ready, (j * DEPTH + s + 1) * DEPTH)
                    pool.tensor_copy(xs[:, s, :, :], XT[:, :, ds((j * DEPTH + s) * CH, CH)]).then_inc(xs_ready, 1)

        @block.tensor
        def _(pe):
            pe.sem_inc(v_ready, DEPTH * DEPTH)
            pe.wait_ge(w_landed, 48)
            with pe.Fori(0, NC // DEPTH) as j:
                for s in range(DEPTH):
                    c = j * DEPTH + s
                    for o in range(PER):
                        pe.wait_ge(rest_ready, c * PER + o + 1)
                        for k in range(DT):
                            mm = pe.matmul(pp[:, o % DEPTH, :], wqk[:, o // DT, k, (o % DT) * P:(o % DT + 1) * P],
                                           XT[:, k, ds(c * CH, CH)], start=(k == 0), stop=(k == DT - 1))
                        mm.then_inc(p_ready, 1)
                    pe.wait_ge(xs_ready, c + 1)
                    for t in range(TPC):
                        if t % 2 == 0:
                            pe.wait_ge(v_copied, c * DEPTH + t // 2 + 1)
                        for k in range(DT):
                            mm = pe.matmul(pv[:, t // 2, t % 2, :], xs[:, s, k, t * P:(t + 1) * P], wv[:, k, :],
                                           start=(k == 0), stop=(k == DT - 1))
                        if t % 2 == 1 and t < TPC - 1:
                            mm.then_inc(v_ready, 1)
                    mm.then_inc(v_ready, 1)

        @block.scalar
        def _(act):
            act.wait_ge(w_landed, 48)
            act.activation(warm[:, :], wv[:, 0, 0:1], ACT.Identity)
            with act.Fori(0, NC) as c:
                for o in range(PER):
                    act.wait_ge(p_ready, c * PER + o + 1)
                    act.wait_ge(parts_kept[o % DEPTH], (c * (PER // DEPTH) + o // DEPTH + 1) * 16)
                    act.copy(parts[:, o % DEPTH, 0, :], pp[:, o % DEPTH, :]).then_inc(high_ready, 1)
                    act.wait_ge(rest_ready, c * PER + o + 1 + DEPTH)
                    act.copy(parts[:, o % DEPTH, 1, :], rest[:, o % DEPTH, :]).then_inc(mid_ready, 1)

        @block.vector
        def _(dve):
            dve.sem_inc(rest_ready, DEPTH)
            for s in range(DEPTH):
                ones = dve.memset(v_out[:, s, :, :, 1, :], 1.0)
            ones.then_inc(v_copied, DEPTH)
            with dve.Fori(0, NC) as c:
                for o in range(PER):
                    dve.wait_ge(high_ready, c * PER + o + 1)
                    dve.tensor_tensor(rest[:, o % DEPTH, :], pp[:, o % DEPTH, :], parts[:, o % DEPTH, 0, :],
                                      ALU.subtract).then_inc(rest_ready, 1)
                    dve.wait_ge(mid_ready, c * PER + o + 1)
                    dve.tensor_tensor(parts[:, o % DEPTH, 2, :], rest[:, o % DEPTH, :], parts[:, o % DEPTH, 1, :],
                                      ALU.subtract).then_inc(low_ready, 1)
                for s in range(DEPTH):
                    dve.wait_ge(v_ready, c * DEPTH + s + 1 + DEPTH * DEPTH)
                    dve.wait_ge(v_kept[s], (c + 1) * 32)
                    for t in range(2):
                        last = dve.tensor_copy(v_out[:, s, t, :, 0, :], pv[:, s, t, :].rearrange("p (h w) -> p h w", h=H0))
                    last.then_inc(v_copied, 1)



def attention(nc, a, q_parts, k_parts, v_rows, heads, ident):
    UNITS = B * NG
    SLOTS = 4
    QT = S // P
    QH = S // CH
    STEPS = QH * KB
    BANKS = HG * QT * 2
    PER_STEP = 5
    TOP = 4
    with ExitStack() as ctx:
        m = Mem(nc, ctx)
        qs = m.sb("qs", [P, SLOTS, HG, S], BF16)
        ks = m.sb("ks", [P, SLOTS, HG, S], BF16)
        va = m.sb("va", [P, SLOTS, KB, HG, 2 * HD])
        half_max = m.sb("half_max", [P, HG * QT, 2])
        top = m.sb("top", [P, HG * QT])
        top_rest = m.sb("top_rest", [P, HG * QT])
        top_parts = m.sb("top_parts", [P, 3, HG * QT], BF16)
        top_rows = m.sb("top_rows", [3 * HG * QT, P], BF16)
        identb = m.sb("identb", [P, P], BF16)
        probs = m.sb("probs", [P, DEPTH, HG, CH])
        o_sb = m.sb("o_sb", [P, CH])
        z_inv = m.sb("z_inv", [P, TPC, HG])
        scores = m.ps("scores", [P, 2, CH])
        scores_t = m.ps("scores_t", [P, HG, CH])
        acc = m.ps("acc", [P, CH])
        misc = m.ps("misc", [P, CH])
        miscb = misc[:, :].bitcast(BF16)
        ones_ready = m.sem("ones_ready")
        qk_landed = [m.sem(f"qk_landed{s}") for s in range(SLOTS)]
        v_landed = [m.sem(f"v_landed{s}") for s in range(SLOTS)]
        identb_ready = m.sem("identb_ready")
        s_ready, s_read = m.sem("s_ready"), m.sem("s_read")
        top_steps, parts_ready, rows_ready = m.sem("top_steps"), m.sem("top_parts_ready"), m.sem("top_rows_ready")
        rows_out, rows_landed = m.sem("top_rows_out"), m.sem("top_rows_landed")
        st_ready, p_ready, pv_done = m.sem("st_ready"), m.sem("probs_ready"), m.sem("pv_done")
        o_out, o_turned, z_ready, o_done = m.sem("o_out"), m.sem("o_turned"), m.sem("z_ready"), m.sem("o_done")
        block = ctx.enter_context(nc.Block())

        def banks_of(step):
            return range(min(PER_STEP * step, BANKS), min(PER_STEP * (step + 1), BANKS))

        def units(eng, unit):
            unit(0, 0, 0, False, True)
            with eng.Fori(0, UNITS // SLOTS - 1) as j:
                for g in range(1, SLOTS + 1):
                    unit(j * SLOTS + g, g % SLOTS, j + g // SLOTS, True, True)
            for g in range(1, SLOTS):
                unit(UNITS - SLOTS + g, g, UNITS // SLOTS - 1, True, g < SLOTS - 1)

        @block.sync
        def _(sp):
            def load(u, slot):
                rows = ds(u * HG * HD, HG * HD)
                for part, (lq, lk) in enumerate(PAIRS):
                    for dst, src, level in ((qs, q_parts, lq), (ks, k_parts, lk)):
                        sp.dma_start(dst[part * HD:(part + 1) * HD, slot, :, :],
                                     src[level, rows, :].rearrange("(h d) t -> d h t", h=HG)).then_inc(qk_landed[slot], 16)
                sp.dma_start(va[:, slot, :, :, :].rearrange("p k h d -> p k (h d)"),
                             v_rows[ds(u, 1), :, :].rearrange("u (k p) f -> p (u k) f", p=P)).then_inc(v_landed[slot], 16)

            def send_top(u, slot):
                sp.wait_ge(rows_out, u + 1)
                for part in range(3):
                    sp.dma_start(qs[STACK + part:STACK + part + 1, slot, :, :].rearrange("o h (q j) -> o (h q) j", j=P),
                                 top_rows[part * HG * QT:(part + 1) * HG * QT, :]
                                 ).then_inc(rows_landed, 16)

            def unit(u, slot, turn, has_prev, has_next, loads=True):
                if has_prev and loads:
                    sp.wait_ge(pv_done, u * STEPS + DEPTH)
                if loads:
                    load(u + SLOTS - 1, (slot + SLOTS - 1) % SLOTS)
                if has_next:
                    send_top(u + 1, (slot + 1) % SLOTS)

            for slot in range(SLOTS - 1):
                load(slot, slot)
            send_top(0, 0)
            unit(0, 0, 0, False, True)
            with sp.Fori(0, UNITS // SLOTS - 1) as j:
                for g in range(1, SLOTS + 1):
                    unit(j * SLOTS + g, g % SLOTS, None, True, True)
            for g in range(1, SLOTS):
                unit(UNITS - SLOTS + g, g, None, True, g < SLOTS - 1, loads=False)

        @block.gpsimd
        def _(pool):
            pool.memset(ks[STACK:P, :, :, :], 1.0).then_inc(ones_ready, 1)

        @block.tensor
        def _(pe):
            def top_bank(u, slot, n):
                h, q, half = n // (QT * 2), n // 2 % QT, n % 2
                pe.wait_ge(s_read, u * BANKS + n + 1)
                pe.matmul(scores[:, n % 2, :], qs[0:STACK, slot, h, q * P:(q + 1) * P],
                          ks[0:STACK, slot, h, half * CH:(half + 1) * CH], start=True, stop=True).then_inc(s_ready, 1)

            def top_turn(u, done):
                pe.wait_ge(parts_ready, u + 1)
                pe.wait_ge(o_done, done + 1)
                pe.transpose(miscb[0:3 * HG * QT, 0:P], top_parts[:, :, :].rearrange("p l r -> p (l r)"),
                             identb[:, :]).then_inc(rows_ready, 1)

            def turn_outputs(u, qh, after_top):
                pe.wait_ge(o_out, u * QH + qh + 2)
                if after_top is not None:
                    pe.wait_ge(rows_out, after_top + 1)
                else:
                    pe.wait_ge(o_done, u * QH + qh + 1)
                for t in range(TPC):
                    mm = pe.transpose(misc[:, t * P:(t + 1) * P], o_sb[:, t * P:(t + 1) * P], ident[:, :])
                mm.then_inc(o_turned, 1)

            def keys(u, slot, step, pair):
                qh, kb = step // KB, step % KB
                pe.wait_ge(p_ready, (u * STEPS + step) * 2 + pair + 1)
                for h in (2 * pair, 2 * pair + 1):
                    mm = pe.matmul(scores_t[:, h, :], ks[0:ROWS, slot, h, kb * P:(kb + 1) * P],
                                   qs[0:ROWS, slot, h, qh * CH:(qh + 1) * CH], start=True, stop=True)
                mm.then_inc(st_ready, 1)

            def values(u, slot, turn, step):
                qh, kb = step // KB, step % KB
                pe.wait_ge(p_ready, (u * STEPS + step) * 2 + 4)
                if kb == 0:
                    pe.wait_ge(o_out, u * QH + qh + 1)
                if step == 0:
                    pe.wait_ge(v_landed[slot], (turn + 1) * 16)
                for h in range(HG):
                    mm = pe.matmul(acc[h * 32:(h + 1) * 32, :], va[:, slot, kb, h, :],
                                   probs[:, step % DEPTH, h, :], start=(kb == 0), stop=(kb == KB - 1))
                mm.then_inc(pv_done, 1)

            def unit(u, slot, turn, has_prev, has_next):
                nxt, before = (slot + 1) % SLOTS, (slot + SLOTS - 1) % SLOTS
                pe.wait_ge(rows_landed, (u + 1) * 48)
                if has_next:
                    pe.wait_ge(qk_landed[nxt], (turn + 1 + (slot + 1) // SLOTS) * 16 * 2 * len(PAIRS))
                for step in range(STEPS):
                    tops = list(banks_of(step)) if has_next else []

                    def some(count):
                        for n in tops[:count]:
                            top_bank(u + 1, nxt, n)
                        del tops[:count]

                    some(1)
                    keys(u, slot, step, 0)
                    some(1)
                    keys(u, slot, step, 1)
                    some(2)
                    if step:
                        values(u, slot, turn, step - 1)
                    elif has_prev:
                        values(u - 1, before, turn, STEPS - 1)
                    some(len(tops))
                    if step == 2 and has_prev:
                        turn_outputs(u - 1, 1, u)
                    if step == KB + 2:
                        turn_outputs(u, 0, None if has_prev else 0)
                    if step == BANKS // PER_STEP + 2 and has_next:
                        top_turn(u + 1, u * QH + 1)
                if not has_next:
                    values(u, slot, turn, STEPS - 1)
                    turn_outputs(u, 1, None)

            pe.sem_inc(pv_done, DEPTH)
            pe.sem_inc(o_turned, 1)
            pe.wait_ge(identb_ready, 1)
            pe.wait_ge(ones_ready, 1)
            pe.wait_ge(qk_landed[0], 16 * 2 * len(PAIRS))
            for n in range(BANKS):
                top_bank(0, 0, n)
            top_turn(0, 0)
            units(pe, unit)

        @block.scalar
        def _(act):
            def keep_outputs(u, qh):
                act.wait_ge(pv_done, u * STEPS + (qh + 1) * KB + DEPTH)
                act.wait_ge(o_turned, u * QH + qh + 1)
                act.copy(o_sb[:, :], acc[:, :]).then_inc(o_out, 1)

            def unit(u, slot, turn, has_prev, has_next):
                for step in range(STEPS):
                    for pair in range(2):
                        n = (u * STEPS + step) * 2 + pair
                        act.wait_ge(st_ready, n + 1)
                        if pair == 0:
                            act.wait_ge(pv_done, u * STEPS + step + 1)
                        act.activation(probs[:, step % DEPTH, 2 * pair:2 * pair + 2, :],
                                       scores_t[:, 2 * pair:2 * pair + 2, :], ACT.Exp,
                                       scale=float(HD) ** -0.5).then_inc(p_ready, 1)
                    if step == 0 and has_prev:
                        keep_outputs(u - 1, 1)
                    if step == KB:
                        keep_outputs(u, 0)
                if not has_next:
                    keep_outputs(u, 1)

            act.sem_inc(p_ready, DEPTH)
            act.sem_inc(o_out, 1)
            act.wait_ge(identb_ready, 1)
            act.activation(o_sb[:, 0:1], identb[:, 0:1], ACT.Exp)
            units(act, unit)

        @block.vector
        def _(dve):
            def bank_max(u, n):
                dve.wait_ge(s_ready, u * BANKS + n + 1)
                dve.tensor_reduce(half_max[:, n // 2, n % 2:n % 2 + 1], scores[:, n % 2, :], AX.X,
                                  ALU.max).then_inc(s_read, 1)

            def split_top(u):
                chain = Chain(dve, top_steps, u * TOP)
                dve.wait_ge(s_read, (u + 1) * BANKS + DEPTH)
                chain.link(dve.tensor_reduce(top[:, :], half_max[:, :, :], AX.X, ALU.max))
                chain.link(dve.tensor_scalar(top_parts[:, 0, :], top[:, :], -1.0, None, ALU.mult))
                chain.link(dve.scalar_tensor_tensor(top_rest[:, :], top[:, :], -1.0, top_parts[:, 0, :],
                                                    ALU.mult, ALU.subtract))
                chain.link(dve.tensor_copy(top_parts[:, 1, :], top_rest[:, :]))
                dve.tensor_tensor(top_parts[:, 2, :], top_rest[:, :], top_parts[:, 1, :],
                                  ALU.subtract).then_inc(parts_ready, 1)

            def keep_top(u):
                dve.wait_ge(rows_ready, u + 1)
                dve.wait_ge(rows_landed, u * 48)
                dve.tensor_copy(top_rows[:, :], miscb[0:3 * HG * QT, 0:P]).then_inc(rows_out, 1)

            def normalise(u, qh):
                dve.wait_ge(o_turned, u * QH + qh + 2)
                o = misc[:, :].rearrange("p (t h w) -> p t h w", t=TPC, h=HG)
                dve.reciprocal(z_inv[:, :, :], o[:, :, :, HD]).then_inc(z_ready, 1)
                dve.wait_ge(z_ready, u * QH + qh + 1)
                for t in range(TPC):
                    last = dve.tensor_tensor(
                        heads[:, ds(u, 1), qh * TPC + t, :].rearrange("p u (h w) -> p (u h) w", h=HG),
                        o[:, t, :, 0:HD], z_inv[:, t, :].unsqueeze(2).to_broadcast([P, HG, HD]), ALU.mult)
                last.then_inc(o_done, 1)

            def unit(u, slot, turn, has_prev, has_next):
                for step in range(STEPS):
                    if has_next:
                        for n in banks_of(step):
                            bank_max(u + 1, n)
                        if step == BANKS // PER_STEP:
                            split_top(u + 1)
                        if step == BANKS // PER_STEP + 2:
                            keep_top(u + 1)
                    if step == 2 and has_prev:
                        normalise(u - 1, 1)
                    if step == KB + 2:
                        normalise(u, 0)
                if not has_next:
                    normalise(u, 1)

            dve.tensor_copy(identb[:, :], ident[:, :]).then_inc(identb_ready, 1)
            dve.sem_inc(s_read, DEPTH)
            dve.sem_inc(o_done, 1)
            for n in range(BANKS):
                bank_max(0, n)
            split_top(0)
            dve.wait_ge(rows_ready, 1)
            dve.tensor_copy(top_rows[:, :], miscb[0:3 * HG * QT, 0:P]).then_inc(rows_out, 1)
            units(dve, unit)


def attention_output(nc, a, X, heads, ident):
    QT = S // P
    with ExitStack() as ctx:
        m = Mem(nc, ctx)
        wo = m.sb("wo", [P, DT, D])
        hstage = m.sb("hstage", [P, DEPTH, NG, HG * HD])
        ht = m.sb("ht", [P, DEPTH, DT, P])
        warm = m.sb("warm_p2", [P, 1])
        tp = m.ps("tp_p2", [P, DEPTH, CH])
        po = m.ps("po", [P, DEPTH, CH])
        wo_landed, staged, turned, ht_ready = m.sem("wo_landed"), m.sem("hstaged"), m.sem("hturned"), m.sem("ht_ready")
        po_ready, added = m.sem("po_ready"), m.sem("added_p2")
        block = ctx.enter_context(nc.Block())

        @block.sync
        def _(sp):
            sp.dma_start(wo[:, :, :], a["wo0"].rearrange("(k p) f -> p k f", p=P)).then_inc(wo_landed, 16)

        @block.vector
        def _(dve):
            dve.sem_inc(added, DEPTH)
            with dve.Fori(0, B) as b:
                for t in range(QT + 1):
                    if t < QT:
                        dve.wait_ge(turned, b * QT + t + 1)
                        dve.tensor_copy(hstage[:, t % DEPTH, :, :], heads[:, ds(b * NG, NG), t, :]).then_inc(staged, 1)
                    if t:
                        dve.wait_ge(po_ready, b * QT + t)
                        x = X[:, ds(b * QT + t - 1, 1), :].rearrange("p o d -> p (o d)")
                        dve.tensor_tensor(x, po[:, (t - 1) % DEPTH, 0:D], x, ALU.add).then_inc(added, 1)

        @block.tensor
        def _(pe):
            pe.sem_inc(turned, DEPTH)
            pe.wait_ge(wo_landed, 16)
            with pe.Fori(0, B) as b:
                for t in range(QT + 1):
                    if t < QT:
                        pe.wait_ge(staged, b * QT + t + 1)
                        pe.wait_ge(ht_ready, b * QT + t + 1)
                        flat = hstage[:, t % DEPTH, :, :].rearrange("p g f -> p (g f)")
                        for k in range(DT):
                            mm = pe.transpose(tp[:, t % DEPTH, k * P:(k + 1) * P], flat[:, k * P:(k + 1) * P],
                                              ident[:, :])
                        mm.then_inc(turned, 1)
                    if t:
                        pe.wait_ge(ht_ready, b * QT + t + DEPTH)
                        pe.wait_ge(added, b * QT + t)
                        for k in range(DT):
                            mm = pe.matmul(po[:, (t - 1) % DEPTH, 0:D], ht[:, (t - 1) % DEPTH, k, :], wo[:, k, :],
                                           start=(k == 0), stop=(k == DT - 1))
                        mm.then_inc(po_ready, 1)

        @block.scalar
        def _(act):
            act.sem_inc(ht_ready, DEPTH)
            act.activation(warm[:, :], ident[:, 0:1], ACT.Identity)
            with act.Fori(0, B) as b:
                for t in range(QT):
                    act.wait_ge(turned, b * QT + t + 1 + DEPTH)
                    if t >= DEPTH:
                        act.wait_ge(po_ready, b * QT + t + 1 - DEPTH)
                    act.copy(ht[:, t % DEPTH, :, :], tp[:, t % DEPTH, 0:D].rearrange("p (k t) -> p k t", k=DT)
                             ).then_inc(ht_ready, 1)

def sigmoid_cross(nc, a, X, XT):
    QK = 128
    SCALE = 1.0 / float(np.sqrt(a["wq_x"].shape[1] // 2))
    HALVES = S // CH
    with ExitStack() as ctx:
        m = Mem(nc, ctx)
        wq = m.sb("wq_x", [P, DT, QK])
        wk = m.sb("wk_x", [P, DT, QK])
        wv = m.sb("wv_x", [P, DT, D])
        bq = m.sb("bq_x", [P, 1])
        bk = m.sb("bk_x", [P, 1])
        bv = m.sb("bv_x", [1, D])
        ones = m.sb("ones_x", [1, CTX])
        ct = m.sb("ct_x", [P, DT, B * CTX])
        kt = m.sb("kt_x", [P, B * CTX])
        kstage = m.sb("kstage_x", [P, CTX])
        v = m.sb("v_x", [CTX, B, D])
        qt = m.sb("qt_x", [P, DEPTH, CH])
        z = m.sb("z_x", [CTX, DEPTH, CH])
        warm = m.sb("warm_x", [P, 1])
        pk = m.ps("pk_x", [P, CH])
        pq = m.ps("pq_x", [P, CH])
        pz = m.ps("pz_x", [P, DEPTH, CH])
        po = m.ps("po_x", [P, 2, 2, D])
        landed, ones_ready, pk_ready, pk_out = m.sem("landed_x"), m.sem("ones_x"), m.sem("pk_ready_x"), m.sem("pk_out_x")
        k_staged, q_ready, q_out = m.sem("k_staged_x"), m.sem("q_ready_x"), m.sem("q_out_x")
        z_ready, z_out, o_ready, added = m.sem("z_ready_x"), m.sem("z_out_x"), m.sem("o_ready_x"), m.sem("added_x")
        LOADS = 7
        block = ctx.enter_context(nc.Block())

        @block.sync
        def _(sp):
            for dst, src in ((wq, "wq_x"), (wk, "wk_x"), (wv, "wv_x"), (ct, "ctx_t")):
                sp.dma_start(dst[:, :, :], a[src].rearrange("(k p) f -> p k f", p=P)).then_inc(landed, 16)
            for dst, src in ((bq, "bq_x"), (bk, "bk_x"), (bv, "bv_x")):
                sp.dma_start(dst[:, :], a[src]).then_inc(landed, 16)

        @block.tensor
        def _(pe):
            pe.wait_ge(landed, 16 * LOADS)
            pe.wait_ge(ones_ready, 1)
            for k in range(DT):
                mm = pe.matmul(pk[:, 0:B * CTX], wk[:, k, :], ct[:, k, :], start=(k == 0), stop=(k == DT - 1))
            mm.then_inc(pk_ready, 1)
            for b in range(B):
                dst = po[0:CTX, b // 2, b % 2, :]
                pe.matmul(dst, ones[:, :], bv[:, :], start=True, stop=False)
                for k in range(DT):
                    mm = pe.matmul(dst, ct[:, k, b * CTX:(b + 1) * CTX], wv[:, k, :], start=False, stop=(k == DT - 1))
            mm.then_inc(pk_ready, 1)
            pe.wait_ge(pk_out, 3)
            with pe.Fori(0, B) as b:
                for s in range(HALVES):
                    c = b * HALVES + s
                    pe.wait_ge(q_out, c + 1)
                    for k in range(DT):
                        mm = pe.matmul(pq[:, :], wq[:, k, :], XT[:, k, ds(c * CH, CH)], start=(k == 0), stop=(k == DT - 1))
                    mm.then_inc(q_ready, 1)
                    if s == 0:
                        pe.wait_ge(k_staged, b + 1)
                    pe.wait_ge(q_out, c + 2)
                    mm = pe.matmul(pz[0:CTX, s, :], kstage[:, :], qt[:, s, :], start=True, stop=True)
                    mm.then_inc(z_ready, 1)
                    pe.wait_ge(z_out, c + 1)
                    for t in range(TPC):
                        if t % 2 == 0:
                            pe.wait_ge(added, c * 2 + t // 2 + 1)
                        mm = pe.matmul(po[:, t // 2, t % 2, :], z[:, s, t * P:(t + 1) * P],
                                       v[:, ds(b, 1), :].rearrange("p o d -> p (o d)"), start=True, stop=True)
                        if t % 2 == 1:
                            mm.then_inc(o_ready, 1)

        @block.scalar
        def _(act):
            act.wait_ge(landed, 16 * LOADS)
            act.wait_ge(pk_ready, 1)
            act.activation(kt[:, :], pk[:, 0:B * CTX], ACT.Identity, bias=bk[:, 0:1]).then_inc(pk_out, 1)
            act.wait_ge(pk_ready, 2)
            act.copy(v[:, 0:2, :], po[0:CTX, 0, :, :]).then_inc(pk_out, 1)
            act.copy(v[:, 2:4, :], po[0:CTX, 1, :, :]).then_inc(pk_out, 1)
            act.activation(warm[:, :], ct[:, 0, 0:1], ACT.Sigmoid)
            with act.Fori(0, B) as b:
                for s in range(HALVES):
                    act.wait_ge(z_ready, b * HALVES + s + 1)
                    act.activation(z[:, s, :], pz[0:CTX, s, :], ACT.Sigmoid, scale=SCALE).then_inc(z_out, 1)

        @block.vector
        def _(dve):
            dve.memset(ones[:, :], 1.0).then_inc(ones_ready, 1)
            dve.sem_inc(q_out, 1)
            dve.sem_inc(added, 2)
            dve.wait_ge(pk_out, 3)
            with dve.Fori(0, B) as b:
                for s in range(HALVES):
                    c = b * HALVES + s
                    if s == 0:
                        dve.wait_ge(added, b * HALVES * 2 + 1)
                        dve.tensor_copy(kstage[:, :], kt[:, ds(b * CTX, CTX)]).then_inc(k_staged, 1)
                    dve.wait_ge(q_ready, c + 1)
                    dve.tensor_scalar(qt[:, s, :], pq[:, :], bq[:, 0:1], None, ALU.add).then_inc(q_out, 1)
                    for t in range(2):
                        dve.wait_ge(o_ready, c * 2 + t + 1)
                        x = X[:, ds(c * TPC + 2 * t, 2), :]
                        dve.tensor_tensor(x, po[:, t, :, :], x, ALU.add).then_inc(added, 1)


def gated_mlp(nc, a, X, XT):
    FT = FF // P
    with ExitStack() as ctx:
        m = Mem(nc, ctx)
        wg = m.sb("wg", [P, DT, FF])
        wu = m.sb("wu", [P, DT, FF])
        wd = m.sb("wd", [P, FT, D])
        bg = m.sb("bg", [P, FT])
        bu = m.sb("bu", [P, FT])
        bd = m.sb("bd", [1, D])
        ones = m.sb("ones_m", [1, P])
        sg = m.sb("sg", [P, DEPTH, CH])
        h = m.sb("h_m", [P, DEPTH, FT, CH])
        warm = m.sb("warm_m", [P, 1])
        pg = m.ps("pg", [P, DEPTH, CH])
        pu = m.ps("pu", [P, DEPTH, CH])
        po = m.ps("po_m", [P, 2, 2, D])
        landed, ones_ready = m.sem("landed_m"), m.sem("ones_ready_m")
        g_ready, u_ready, sg_ready, h_ready = m.sem("g_ready"), m.sem("u_ready"), m.sem("sg_ready"), m.sem("h_ready_m")
        o_ready, added = m.sem("o_ready_m"), m.sem("added_m")
        LOADS = 6
        block = ctx.enter_context(nc.Block())

        @block.sync
        def _(sp):
            for dst, src in ((wg, "wg"), (wu, "wu"), (wd, "wd")):
                sp.dma_start(dst[:, :, :], a[src].rearrange("(k p) f -> p k f", p=P)).then_inc(landed, 16)
            for dst, src in ((bg, "bg"), (bu, "bu"), (bd, "bd")):
                sp.dma_start(dst[:, :], a[src]).then_inc(landed, 16)

        @block.tensor
        def _(pe):
            pe.wait_ge(landed, 16 * LOADS)
            pe.wait_ge(ones_ready, 1)
            with pe.Fori(0, NC // DEPTH) as j:
                for s in range(DEPTH):
                    c = j * DEPTH + s
                    for f in range(FT):
                        n = c * FT + f
                        pe.wait_ge(h_ready, n + 1)
                        for w, dst, done in ((wg, pg, g_ready), (wu, pu, u_ready)):
                            for k in range(DT):
                                mm = pe.matmul(dst[:, f % DEPTH, :], w[:, k, f * P:(f + 1) * P], XT[:, k, ds(c * CH, CH)],
                                               start=(k == 0), stop=(k == DT - 1))
                            mm.then_inc(done, 1)
                    pe.wait_ge(h_ready, (c + 1) * FT + DEPTH)
                    for t in range(TPC):
                        if t % 2 == 0:
                            pe.wait_ge(added, c * 2 + t // 2 + 1)
                        pe.matmul(po[:, t // 2, t % 2, :], ones[:, :], bd[:, :], start=True, stop=False)
                        for f in range(FT):
                            mm = pe.matmul(po[:, t // 2, t % 2, :], h[:, s, f, t * P:(t + 1) * P], wd[:, f, :],
                                           start=False, stop=(f == FT - 1))
                        if t % 2 == 1:
                            mm.then_inc(o_ready, 1)

        @block.scalar
        def _(act):
            act.wait_ge(landed, 16 * LOADS)
            act.activation(warm[:, :], bg[:, 0:1], ACT.Silu)
            with act.Fori(0, NC) as c:
                for f in range(FT):
                    n = c * FT + f
                    act.wait_ge(g_ready, n + 1)
                    act.wait_ge(h_ready, n + 1)
                    act.activation(sg[:, f % DEPTH, :], pg[:, f % DEPTH, :], ACT.Silu, bias=bg[:, f:f + 1]).then_inc(sg_ready, 1)

        @block.vector
        def _(dve):
            dve.memset(ones[:, :], 1.0).then_inc(ones_ready, 1)
            dve.sem_inc(h_ready, DEPTH)
            dve.sem_inc(added, 2)
            dve.wait_ge(landed, 16 * LOADS)
            with dve.Fori(0, NC // DEPTH) as j:
                for s in range(DEPTH):
                    c = j * DEPTH + s
                    for f in range(FT):
                        n = c * FT + f
                        dve.wait_ge(u_ready, n + 1)
                        dve.wait_ge(sg_ready, n + 1)
                        dve.scalar_tensor_tensor(h[:, s, f, :], pu[:, f % DEPTH, :], bu[:, f:f + 1], sg[:, f % DEPTH, :],
                                                 ALU.add, ALU.mult).then_inc(h_ready, 1)
                    for t in range(2):
                        dve.wait_ge(o_ready, c * 2 + t + 1)
                        x = X[:, ds(c * TPC + 2 * t, 2), :]
                        dve.tensor_tensor(x, po[:, t, :, :], x, ALU.add).then_inc(added, 1)


def peer_gates(nc, a, XT, sim, thr, shift):
    SIM = 2 * NH * NK
    with ExitStack() as ctx:
        m = Mem(nc, ctx)
        wq_t = m.sb("wq_t", [P, SIM // P, D])
        keys = m.sb("keys", [P, SIM // P, 2 * NK])
        wsim = m.sb("wsim", [P, DT, SIM])
        xs = m.sb("xs_g", [P, DEPTH, DT, P])
        best = m.sb("best", [P, DEPTH, 2 * NH, TOPK])
        sums = m.sb("sums", [P, DEPTH, NH, TOPK * TOPK])
        picked = m.sb("picked", [P, DEPTH, NH, TOPK])
        picks = m.sb("picks", [P, NT, NH, TOPK])
        z = m.sb("z_g", [P, NT, NH])
        logz = m.sb("logz", [P, NT, NH])
        pw = m.ps("pw_g", [P, DT, SIM])
        psim = m.ps("psim", [P, DEPTH, SIM])
        landed, pw_ready, w_ready = m.sem("landed_g"), m.sem("pw_ready_g"), m.sem("w_ready_g")
        xs_ready, sim_ready, sim_kept = m.sem("xs_ready_g"), m.sem("sim_ready"), m.sem("sim_kept")
        best_ready, sums_ready, passed = m.sem("best_ready"), m.sem("sums_ready"), m.sem("passed_g")
        picked_ready, picks_kept = m.sem("picked_ready"), m.sem("picks_kept")
        tail, exp_ready, log_ready = m.sem("tail_g"), m.sem("exp_ready_g"), m.sem("log_ready_g")
        block = ctx.enter_context(nc.Block())

        @block.sync
        def _(sp):
            sp.dma_start(wq_t[:, :, :], a["peer_wq_t"].rearrange("(k p) f -> p k f", p=P)).then_inc(landed, 16)
            sp.dma_start(keys[:, :, :], a["peer_keys"].rearrange("(k p) f -> p k f", p=P)).then_inc(landed, 16)

        @block.tensor
        def _(pe):
            pe.wait_ge(landed, 32)
            for k in range(DT):
                for g in range(SIM // P):
                    mm = pe.matmul(pw[:, k, g * P:(g + 1) * P], wq_t[:, g, k * P:(k + 1) * P], keys[:, g, :],
                                   start=True, stop=True)
            mm.then_inc(pw_ready, 1)
            pe.wait_ge(w_ready, 1)
            with pe.Fori(0, NT // DEPTH) as j:
                for s in range(DEPTH):
                    i = j * DEPTH + s
                    pe.wait_ge(xs_ready, i + 1)
                    pe.wait_ge(best_ready, i + 1)
                    pe.wait_ge(sim_kept, i + 1)
                    for k in range(DT):
                        mm = pe.matmul(psim[:, s, :], xs[:, s, k, :], wsim[:, k, :], start=(k == 0), stop=(k == DT - 1))
                    mm.then_inc(sim_ready, 1)

        @block.gpsimd
        def _(pool):
            with pool.Fori(0, NT // DEPTH) as j:
                for s in range(DEPTH):
                    i = j * DEPTH + s
                    pool.wait_ge(sim_kept, i + 1)
                    pool.tensor_copy(xs[:, s, :, :], XT[:, :, ds(i * P, P)]).then_inc(xs_ready, 1)

        @block.scalar
        def _(act):
            act.wait_ge(pw_ready, 1)
            act.copy(wsim[:, :, :], pw[:, :, :]).then_inc(w_ready, 1)
            act.sem_inc(sim_kept, DEPTH)
            with act.Fori(0, NT // DEPTH) as j:
                for s in range(DEPTH):
                    i = j * DEPTH + s
                    act.wait_ge(best_ready, i + 1 + DEPTH)
                    act.copy(sim[:, ds(i, 1), :], psim[:, s, :].unsqueeze(1)).then_inc(sim_kept, 1)
            act.wait_ge(tail, 1)
            act.activation(picks[:, :, :, :], picks[:, :, :, :], ACT.Exp).then_inc(exp_ready, 1)
            act.wait_ge(tail, 2)
            act.activation(logz[:, :, :], z[:, :, :], ACT.Ln).then_inc(log_ready, 1)

        @block.vector
        def _(dve):
            dve.sem_inc(best_ready, DEPTH)
            with dve.Fori(0, NT // DEPTH) as j:
                for s in range(DEPTH):
                    i = j * DEPTH + s
                    dve.wait_ge(sim_ready, i + 1)
                    dve.sem_inc(passed, 1)
                    for g in range(2 * NH):
                        last = dve.max(best[:, s, g, :], psim[:, s, g * NK:(g + 1) * NK])
                    last.then_inc(best_ready, 1)
                    dve.wait_ge(best_ready, i + 1 + DEPTH)
                    for h in range(NH):
                        last = dve.tensor_tensor(
                            sums[:, s, h, :].rearrange("p (x y) -> p x y", x=TOPK),
                            best[:, s, h, :].unsqueeze(2).to_broadcast([P, TOPK, TOPK]),
                            best[:, s, NH + h, :].unsqueeze(1).to_broadcast([P, TOPK, TOPK]), ALU.add)
                    last.then_inc(sums_ready, 1)
                    dve.wait_ge(sums_ready, i + 1)
                    dve.sem_inc(passed, 1)
                    for h in range(NH):
                        last = dve.max(picked[:, s, h, :], sums[:, s, h, :])
                    last.then_inc(picked_ready, 1)
                    dve.wait_ge(picked_ready, i + 1)
                    dve.tensor_copy(picks[:, ds(i, 1), :, :].rearrange("p o h k -> p (o h k)"),
                                    picked[:, s, :, :].rearrange("p h k -> p (h k)")).then_inc(picks_kept, 1)
            dve.wait_ge(picks_kept, NT)
            dve.tensor_copy(thr[:, :, :], picks[:, :, :, TOPK - 1])
            dve.tensor_copy(shift[:, :, :], picks[:, :, :, 0]).then_inc(picks_kept, 1)
            dve.wait_ge(picks_kept, NT + 1)
            p3 = picks[:, :, :, :].rearrange("p t h k -> p (t h) k")
            dve.tensor_tensor(p3, p3, shift[:, :, :].rearrange("p t h -> p (t h)").unsqueeze(2).to_broadcast([P, NT * NH, TOPK]),
                              ALU.subtract).then_inc(tail, 1)
            dve.wait_ge(exp_ready, 1)
            dve.tensor_reduce(z[:, :, :].rearrange("p t h -> p (t h)"), p3, AX.X, ALU.add).then_inc(tail, 1)
            dve.wait_ge(log_ready, 1)
            dve.scalar_tensor_tensor(shift[:, :, :], shift[:, :, :], -1.0, logz[:, :, :], ALU.mult, ALU.subtract)


def peer_experts(nc, a, X, XT, sim, thr, shift, ident):
    ET = FF // P
    with ExitStack() as ctx:
        m = Mem(nc, ctx)
        down = m.sb("down_t", [P, DT, FF])
        up = m.sb("up", [P, ET, D])
        both = m.sb("both", [P, DEPTH, FF])
        expd = m.sb("expd", [P, DEPTH, FF])
        gate = m.sb("gate", [P, DEPTH, FF])
        gates = m.sb("gates", [P, DEPTH, FF])
        taken = m.sb("taken", [P, DEPTH])
        rest = m.sb("rest_e", [P, DEPTH])
        act_t = m.sb("act_t", [P, DEPTH, ET, P])
        weighted = m.sb("weighted", [P, ET, P])
        warm = m.sb("warm_e", [P, 1])
        pg = m.ps("pgt", [P, ET, P])
        pw = m.ps("pw_e", [P, ET, P])
        po = m.ps("po_e", [P, DEPTH, CH])
        landed, both_ready, exp_ready = m.sem("landed_e"), m.sem("both_ready"), m.sem("exp_ready_e")
        gate_ready, steps = m.sem("gate_ready"), m.sem("gate_steps")
        gates_ready, turned, w_ready = m.sem("gates_ready"), m.sem("gates_turned"), m.sem("w_ready_e")
        act_ready, weighted_ready = m.sem("act_ready"), m.sem("weighted_ready")
        o_ready, added = m.sem("o_ready_e"), m.sem("added_e")
        STEPS = NH - 1 + 1
        block = ctx.enter_context(nc.Block())

        @block.sync
        def _(sp):
            sp.dma_start(down[:, :, :], a["down_t"].rearrange("(k p) f -> p k f", p=P)).then_inc(landed, 16)
            sp.dma_start(up[:, :, :], a["up"].rearrange("(k p) f -> p k f", p=P)).then_inc(landed, 16)

        @block.gpsimd
        def _(pool):
            with pool.Fori(0, NT) as i:
                for h in range(NH):
                    n = i * NH + h
                    pool.wait_ge(gate_ready, n + 1)
                    xk = sim[:, ds(i, 1), h * NK:h * NK + NX].rearrange("p o k -> p (o k)")
                    yk = sim[:, ds(i, 1), (NH + h) * NK:(NH + h + 1) * NK].rearrange("p o k -> p (o k)")
                    pool.tensor_tensor(both[:, h % DEPTH, :].rearrange("p (x y) -> p x y", x=NX),
                                       xk.unsqueeze(2).to_broadcast([P, NX, NK]),
                                       yk.unsqueeze(1).to_broadcast([P, NX, NK]), ALU.add).then_inc(both_ready, 1)

        @block.scalar
        def _(act):
            act.wait_ge(landed, 32)
            act.activation(warm[:, :], down[:, 0, 0:1], ACT.Exp)
            act.sem_inc(act_ready, 1)
            with act.Fori(0, NT // DEPTH) as j:
                for s in range(DEPTH):
                    i = j * DEPTH + s
                    for h in range(NH):
                        n = i * NH + h
                        act.wait_ge(both_ready, n + 1)
                        act.wait_ge(gate_ready, n + 1)
                        act.activation(expd[:, h % DEPTH, :], both[:, h % DEPTH, :], ACT.Exp,
                                       bias=shift[:, ds(i, 1), h]).then_inc(exp_ready, 1)
                    act.wait_ge(w_ready, i + 1)
                    act.wait_ge(weighted_ready, i + 1)
                    act.activation(act_t[:, s, :, :], pw[:, :, :], ACT.Silu).then_inc(act_ready, 1)

        @block.vector
        def _(dve):
            def open_gates(i, s):
                chain = Chain(dve, steps, i * STEPS)
                for h in range(NH):
                    n = i * NH + h
                    dve.wait_ge(exp_ready, n + 1)
                    if h == 0:
                        dve.wait_ge(turned, i + 1)
                    dve.scalar_tensor_tensor(gates[:, s, :] if h == 0 else gate[:, h % DEPTH, :], both[:, h % DEPTH, :],
                                             thr[:, ds(i, 1), h], expd[:, h % DEPTH, :],
                                             ALU.is_ge, ALU.mult).then_inc(gate_ready, 1)
                    dve.wait_ge(gate_ready, n + 1 + DEPTH)
                    if h:
                        chain.link(dve.scalar_tensor_tensor(gates[:, s, :], gates[:, s, :], 1.0, gate[:, h % DEPTH, :],
                                                            ALU.mult, ALU.add,
                                                            accum_out=taken[:, s:s + 1] if h == NH - 1 else None))
                chain.link(dve.tensor_scalar(rest[:, s:s + 1], taken[:, s:s + 1], -1.0, float(NH), ALU.mult, ALU.add))
                dve.tensor_tensor(gates[:, s, FF - 1:FF], gates[:, s, FF - 1:FF], rest[:, s:s + 1],
                                  ALU.add).then_inc(gates_ready, 1)

            def weigh(i, s):
                dve.wait_ge(turned, i + 1 + DEPTH)
                dve.wait_ge(act_ready, i + 2)
                dve.wait_ge(o_ready, i + 1)
                dve.tensor_tensor(weighted[:, :, :], pg[:, :, :], act_t[:, s, :, :], ALU.mult).then_inc(weighted_ready, 1)

            def add(i, s):
                dve.wait_ge(o_ready, i + 2)
                x = X[:, ds(i, 1), :].rearrange("p o d -> p (o d)")
                dve.tensor_tensor(x, po[:, s, 0:D], x, ALU.add).then_inc(added, 1)

            dve.sem_inc(gate_ready, DEPTH)
            dve.sem_inc(weighted_ready, DEPTH)
            dve.sem_inc(added, DEPTH)
            open_gates(0, 0)
            weigh(0, 0)
            open_gates(1, 1)
            with dve.Fori(0, NT // DEPTH - 1) as j:
                for s in range(DEPTH):
                    i = j * DEPTH + s
                    weigh(i + 1, 1 - s)
                    add(i, s)
                    open_gates(i + 2, s)
            weigh(NT - 1, 1)
            add(NT - 2, 0)
            add(NT - 1, 1)

        @block.tensor
        def _(pe):
            def project(i):
                pe.wait_ge(act_ready, i + 1)
                for e in range(ET):
                    for k in range(DT):
                        mm = pe.matmul(pw[:, e, :], down[:, k, e * P:(e + 1) * P], XT[:, k, ds(i * P, P)],
                                       start=(k == 0), stop=(k == DT - 1))
                mm.then_inc(w_ready, 1)

            def turn(i, s):
                pe.wait_ge(gates_ready, i + 1)
                pe.wait_ge(weighted_ready, i + DEPTH)
                for e in range(ET):
                    mm = pe.transpose(pg[:, e, :], gates[:, s, e * P:(e + 1) * P], ident[:, :])
                mm.then_inc(turned, 1)

            def combine(i, s):
                pe.wait_ge(weighted_ready, i + 1 + DEPTH)
                pe.wait_ge(added, i + 1)
                for e in range(ET):
                    mm = pe.matmul(po[:, s, 0:D], weighted[:, e, :], up[:, e, :], start=(e == 0), stop=(e == ET - 1))
                mm.then_inc(o_ready, 1)

            pe.sem_inc(turned, DEPTH)
            pe.sem_inc(o_ready, 1)
            pe.wait_ge(landed, 32)
            project(0)
            turn(0, 0)
            with pe.Fori(0, NT // DEPTH - 1) as j:
                for s in range(DEPTH):
                    i = j * DEPTH + s
                    project(i + 1)
                    combine(i, s)
                    turn(i + 1, 1 - s)
            project(NT - 1)
            combine(NT - 2, 0)
            turn(NT - 1, 1)
            combine(NT - 1, 1)


def key_products(nc, a, XT, grams, vsum):
    QT = S // P
    with ExitStack() as ctx:
        m = Mem(nc, ctx)
        wkv = m.sb("wkv", [P, DT, 2 * D])
        mask = m.sb("mask", [P, P])
        ones = m.sb("ones_k", [P, 1])
        nb = m.sb("nb", [P, DT])
        xs = m.sb("xs_k", [P, DEPTH, DT, P])
        kv = m.sb("kv", [P, DEPTH, 2 * D])
        warm = m.sb("warm_k", [P, 1])
        pkv = m.ps("pkv", [P, DEPTH, 2 * D])
        pg = m.ps("pgram", [P, DT, 2 * D])
        pv = m.ps("pvsum", [P, DT, CH])
        landed, ones_ready = m.sem("landed_k"), m.sem("ones_ready_k")
        xs_ready, kv_ready, kv_out = m.sem("xs_ready_k"), m.sem("kv_ready"), m.sem("kv_out")
        gram_ready, gram_kept = m.sem("gram_ready"), m.sem("gram_kept")
        block = ctx.enter_context(nc.Block())

        @block.sync
        def _(sp):
            sp.dma_start(wkv[:, :, :], a["wkv1"].rearrange("(k p) f -> p k f", p=P)).then_inc(landed, 16)
            sp.dma_start(mask[:, :], a["mask"]).then_inc(landed, 16)
            sp.dma_start(nb[:, :], a["norm_b"]).then_inc(landed, 16)

        @block.scalar
        def _(act):
            act.wait_ge(landed, 48)
            act.sem_inc(kv_out, DEPTH)
            act.activation(warm[:, :], mask[:, 0:1], ACT.Identity)
            with act.Fori(0, B) as b:
                for t in range(QT):
                    act.wait_ge(kv_ready, b * QT + t + 1)
                    act.copy(kv[:, t % DEPTH, :], pkv[:, t % DEPTH, :]).then_inc(kv_out, 1)

        @block.tensor
        def _(pe):
            pe.wait_ge(landed, 48)
            pe.wait_ge(ones_ready, 1)
            with pe.Fori(0, B) as b:
                pe.wait_ge(gram_kept, b + 1)
                for t in range(QT + 1):
                    if t < QT:
                        pe.wait_ge(xs_ready, b * QT + t + 1)
                        pe.wait_ge(kv_out, b * QT + t + 1)
                        for k in range(DT):
                            mm = pe.matmul(pkv[:, t % DEPTH, :], xs[:, t % DEPTH, k, :], wkv[:, k, :],
                                           start=(k == 0), stop=(k == DT - 1))
                        mm.then_inc(kv_ready, 1)
                    if t:
                        u = t - 1
                        pe.wait_ge(kv_out, b * QT + u + 1 + DEPTH)
                        tile = kv[:, u % DEPTH, :].rearrange("p (o k f) -> p o k f", o=2, k=DT)
                        for k in range(DT):
                            pe.matmul(pg[:, k, 0:2 * P], tile[:, 0, k, :], tile[:, :, k, :],
                                      start=(u == 0), stop=(u == QT - 1))
                            mm = pe.matmul(pv[:, k, 0:1], tile[:, 1, k, :], ones[:, :],
                                           start=(u == 0), stop=(u == QT - 1))
                mm.then_inc(gram_ready, 1)

        @block.vector
        def _(dve):
            dve.memset(ones[:, :], 1.0).then_inc(ones_ready, 1)
            dve.sem_inc(gram_kept, 1)
            dve.wait_ge(landed, 48)
            with dve.Fori(0, B) as b:
                for t in range(QT):
                    dve.wait_ge(kv_ready, b * QT + t) if t else dve.wait_ge(gram_kept, b + 1)
                    dve.tensor_copy(xs[:, t % DEPTH, :, :], XT[:, :, ds(b * S + t * P, P)]).then_inc(xs_ready, 1)
                dve.wait_ge(gram_ready, b + 1)
                for k in range(DT):
                    dve.tensor_tensor(grams[:, ds(b * DT + k, 1), :, :].rearrange("p o g f -> p (o g) f"),
                                      pg[:, k, 0:2 * P].rearrange("p (g f) -> p g f", g=2),
                                      mask[:, :].unsqueeze(1).to_broadcast([P, 2, P]), ALU.mult)
                    last = dve.tensor_scalar(vsum[:, ds(b * DT + k, 1)], pv[:, k, 0:1], nb[:, k:k + 1], None, ALU.mult)
                last.then_inc(gram_kept, 1)


def normed_attention(nc, a, X, XT, grams, vsum):
    EPS = 1e-12
    HALVES = S // CH
    with ExitStack() as ctx:
        m = Mem(nc, ctx)
        wq = m.sb("wq1", [P, DT, D])
        wo = m.sb("wo1", [P, DT, D])
        bo = m.sb("bo1", [1, D])
        ng = m.sb("ng", [P, DT])
        mask = m.sb("mask_n", [P, P])
        ones = m.sb("ones_n", [1, P])
        gm = m.sb("gm", [P, DT, 2, P])
        vb = m.sb("vb", [P, DT])
        qt = m.sb("qt1", [P, DT, CH])
        prod = m.sb("prod", [P, DT, CH])
        norm = m.sb("norm1", [P, DT, CH])
        floor = m.sb("floor1", [P, DT, CH])
        inv = m.sb("inv1", [P, DT, CH])
        scaled = m.sb("scaled1", [P, DT, CH])
        o = m.sb("o1", [P, DT, CH])
        warm = m.sb("warm_n", [P, 1])
        pq = m.ps("pq1", [P, DT, CH])
        pn = m.ps("pn1", [P, DT, CH])
        pm = m.ps("pm1", [P, DT, CH])
        py = m.ps("py1", [P, 2, 2, D])
        landed, ones_ready, gm_ready = m.sem("landed_n"), m.sem("ones_ready_n"), m.sem("gm_ready")
        q_ready, q_out, g_ready, prod_ready = m.sem("q_ready_n"), m.sem("q_out_n"), m.sem("g_ready_n"), m.sem("prod_ready")
        n_ready, norm_ready, m_ready = m.sem("n_ready"), m.sem("norm_ready"), m.sem("m_ready")
        inv_steps, scaled_ready, o_ready = m.sem("inv_steps"), m.sem("scaled_ready"), m.sem("o_ready_n")
        y_ready, added = m.sem("y_ready_n"), m.sem("added_n")
        block = ctx.enter_context(nc.Block())

        @block.sync
        def _(sp):
            sp.dma_start(wq[:, :, :], a["wq1"].rearrange("(k p) f -> p k f", p=P)).then_inc(landed, 16)
            sp.dma_start(wo[:, :, :], a["wo1"].rearrange("(k p) f -> p k f", p=P)).then_inc(landed, 16)
            for dst, src in ((bo, "bo1"), (ng, "norm_g"), (mask, "mask")):
                sp.dma_start(dst[:, :], a[src]).then_inc(landed, 16)

        @block.tensor
        def _(pe):
            pe.sem_inc(y_ready, 2)
            pe.wait_ge(landed, 80)
            pe.wait_ge(ones_ready, 1)
            with pe.Fori(0, B) as b:
                for s in range(HALVES):
                    c = b * HALVES + s
                    for k in range(DT):
                        n = c * DT + k
                        for kk in range(DT):
                            mm = pe.matmul(pq[:, k, :], wq[:, kk, k * P:(k + 1) * P], XT[:, kk, ds(c * CH, CH)],
                                           start=(kk == 0), stop=(kk == DT - 1))
                        mm.then_inc(q_ready, 1)
                    if s == 0:
                        pe.wait_ge(gm_ready, b + 1)
                    for k in range(DT):
                        n = c * DT + k
                        pe.wait_ge(q_out, n + 1)
                        pe.wait_ge(scaled_ready, n + 1)
                        pe.matmul(pm[:, k, :], gm[:, k, 0, :], qt[:, k, :], start=True, stop=True).then_inc(g_ready, 1)
                    for k in range(DT):
                        n = c * DT + k
                        pe.wait_ge(prod_ready, n + 1)
                        pe.matmul(pn[:, k, :], mask[:, :], prod[:, k, :], start=True, stop=True).then_inc(n_ready, 1)
                        pe.matmul(pm[:, k, :], gm[:, k, 1, :], qt[:, k, :], start=True, stop=True).then_inc(m_ready, 1)
                    pe.wait_ge(o_ready, (c + 1) * DT)
                    for t in range(TPC):
                        if t % 2 == 0:
                            pe.wait_ge(added, c * 2 + t // 2 + 1)
                        dst = py[:, t // 2, t % 2, :]
                        pe.matmul(dst, ones[:, :], bo[:, :], start=True, stop=False)
                        for k in range(DT):
                            mm = pe.matmul(dst, o[:, k, t * P:(t + 1) * P], wo[:, k, :], start=False, stop=(k == DT - 1))
                        if t % 2 == 1:
                            mm.then_inc(y_ready, 1)

        @block.scalar
        def _(act):
            act.wait_ge(landed, 80)
            act.activation(warm[:, :], ng[:, 0:1], ACT.Sqrt)
            with act.Fori(0, B) as b:
                for s in range(HALVES):
                    c = b * HALVES + s
                    for k in range(DT):
                        act.wait_ge(q_ready, c * DT + k + 1)
                        act.wait_ge(scaled_ready, c * DT + k + 1)
                        act.copy(qt[:, k, :], pq[:, k, :]).then_inc(q_out, 1)
                    for k in range(DT):
                        n = c * DT + k
                        act.wait_ge(n_ready, n + 1)
                        act.wait_ge(scaled_ready, n + 1)
                        act.activation(norm[:, k, :], pn[:, k, :], ACT.Sqrt).then_inc(norm_ready, 1)
                    for k in range(DT):
                        n = c * DT + k
                        act.wait_ge(scaled_ready, n + 1 + DT)
                        act.wait_ge(y_ready, c * 2 + 2)
                        act.activation(o[:, k, :], scaled[:, k, :], ACT.Identity,
                                       bias=vb[:, k:k + 1]).then_inc(o_ready, 1)

        @block.vector
        def _(dve):
            dve.memset(ones[:, :], 1.0).then_inc(ones_ready, 1)
            dve.sem_inc(scaled_ready, DT)
            dve.sem_inc(added, 2)
            dve.wait_ge(landed, 80)
            with dve.Fori(0, B) as b:
                dve.tensor_copy(vb[:, :], vsum[:, ds(b * DT, DT)])
                dve.tensor_copy(gm[:, :, :, :], grams[:, ds(b * DT, DT), :, :]).then_inc(gm_ready, 1)
                for s in range(HALVES):
                    c = b * HALVES + s
                    for k in range(DT):
                        n = c * DT + k
                        dve.wait_ge(g_ready, n + 1)
                        dve.tensor_tensor(prod[:, k, :], pm[:, k, :], qt[:, k, :], ALU.mult).then_inc(prod_ready, 1)
                    for k in range(DT):
                        n = c * DT + k
                        dve.wait_ge(norm_ready, n + 1)
                        dve.tensor_scalar(floor[:, k, :], norm[:, k, :], EPS, None, ALU.max).then_inc(inv_steps, 1)
                        dve.wait_ge(inv_steps, n * 2 + 1)
                        dve.reciprocal(inv[:, k, :], floor[:, k, :]).then_inc(inv_steps, 1)
                        dve.wait_ge(inv_steps, n * 2 + 2)
                        dve.wait_ge(m_ready, n + 1)
                        dve.scalar_tensor_tensor(scaled[:, k, :], pm[:, k, :], ng[:, k:k + 1], inv[:, k, :],
                                                 ALU.mult, ALU.mult).then_inc(scaled_ready, 1)
                    for t in range(2):
                        dve.wait_ge(y_ready, c * 2 + t + 1 + 2)
                        x = X[:, ds(c * TPC + 2 * t, 2), :]
                        dve.tensor_tensor(x, py[:, t, :, :], x, ALU.add).then_inc(added, 1)


def circular_filter(nc, a, X, Z):
    PAIRS_ = KB // 2
    with ExitStack() as ctx:
        m = Mem(nc, ctx)
        fwd = m.sb("fwd", [P, 4, P])
        fw = m.sb("fw", [P, 3, P])
        inv = m.sb("inv_f", [P, 2, P])
        taps = m.sb("taps", [P, D])
        ct = m.sb("ct_f", [P, DT, B, CTX])
        kpw = m.sb("kpw", [P, DT, D])
        kpb = m.sb("kpb", [1, D])
        ones = m.sb("ones_f", [1, P])
        csum = m.sb("csum", [P, DT, B])
        cmean = m.sb("cmean", [P, DT, B, P])
        kmod = m.sb("kmod", [P, B, D])
        spec = m.sb("spec", [P, 3, B, D])
        part = m.sb("part_f", [P, DEPTH, 4, 2, D])
        yf = m.sb("yf", [P, DEPTH, 2, 2, D])
        px = m.ps("px_f", [P, DEPTH, 2, 2, D])
        py = m.ps("py_f", [P, DEPTH, 2, D])
        pk = m.ps("pk_f", [P, 2, 2, D])
        landed, ones_ready, steps = m.sem("landed_f"), m.sem("ones_ready_f"), m.sem("steps_f")
        mean_ready, k_ready, k_out, w_ready, spec_ready = (m.sem("mean_ready"), m.sem("k_ready_f"), m.sem("k_out_f"),
                                                           m.sem("w_ready_f"), m.sem("spec_ready"))
        x_ready, part_ready, yf_ready = m.sem("x_ready_f"), m.sem("part_ready"), m.sem("yf_ready")
        y_ready, z_ready = m.sem("y_ready_f"), m.sem("z_ready_f")
        block = ctx.enter_context(nc.Block())

        @block.sync
        def _(sp):
            for dst, src in ((fwd, "dft_fwd"), (fw, "dft_taps"), (inv, "dft_inv")):
                sp.dma_start(dst[:, :, :], a[src].rearrange("m p f -> p m f")).then_inc(landed, 16)
            sp.dma_start(ct[:, :, :, :].rearrange("p k b c -> p k (b c)"),
                         a["ctx_t"].rearrange("(k p) f -> p k f", p=P)).then_inc(landed, 16)
            sp.dma_start(kpw[:, :, :], a["kp_w_t"].rearrange("(k p) f -> p k f", p=P)).then_inc(landed, 16)
            sp.dma_start(taps[:, :], a["taps_t"]).then_inc(landed, 16)
            sp.dma_start(kpb[:, :], a["kp_b"]).then_inc(landed, 16)

        @block.tensor
        def _(pe):
            pe.wait_ge(landed, 16 * 7)
            pe.wait_ge(ones_ready, 1)
            pe.wait_ge(mean_ready, 1)
            for b in range(B):
                dst = pk[:, b // 2, b % 2, :]
                pe.matmul(dst, ones[:, :], kpb[:, :], start=True, stop=False)
                for k in range(DT):
                    mm = pe.matmul(dst, cmean[:, k, b, :], kpw[:, k, :], start=False, stop=(k == DT - 1))
            mm.then_inc(k_ready, 1)
            pe.wait_ge(k_out, 1)
            for w in range(3):
                mm = pe.matmul(pk[:, w // 2, w % 2, :], fw[:, w, :], taps[:, :], start=True, stop=True)
            mm.then_inc(w_ready, 1)
            with pe.Fori(0, B) as b:
                for q in range(PAIRS_ + 1):
                    if q < PAIRS_:
                        n = b * PAIRS_ + q
                        pe.wait_ge(part_ready, n + 1)
                        for o in range(2):
                            dst = px[:, q % DEPTH, o, :, :]
                            pe.matmul(dst, fwd[:, 2 * o + 1, :], X[:, ds(b * KB + 2 * q, 2), :],
                                      start=True, stop=False, skip_group_check=True)
                            if q:
                                mm = pe.matmul(dst, fwd[:, 2 * o, :], X[:, ds(b * KB + 2 * q - 1, 2), :],
                                               start=False, stop=True, skip_group_check=True)
                            else:
                                pe.matmul(dst[:, 0, :], fwd[:, 2 * o, :],
                                          X[:, ds(b * KB + KB - 1, 1), :].rearrange("p o d -> p (o d)"),
                                          start=False, stop=False, skip_group_check=True)
                                mm = pe.matmul(dst[:, 1, :], fwd[:, 2 * o, :],
                                               X[:, ds(b * KB, 1), :].rearrange("p o d -> p (o d)"),
                                               start=False, stop=True, skip_group_check=True)
                        mm.then_inc(x_ready, 1)
                    if q:
                        n = b * PAIRS_ + q - 1
                        s = (q - 1) % DEPTH
                        pe.wait_ge(yf_ready, n + 1 + DEPTH)
                        pe.wait_ge(z_ready, n + 1)
                        for o in range(2):
                            mm = pe.matmul(py[:, s, :, :], inv[:, o, :], yf[:, s, o, :, :], start=(o == 0), stop=(o == 1))
                        mm.then_inc(y_ready, 1)

        @block.scalar
        def _(act):
            act.wait_ge(k_ready, 1)
            act.copy(kmod[:, :, :].rearrange("p b d -> p (b d)"), pk[:, :, :, :].rearrange("p a c d -> p (a c d)")
                     ).then_inc(k_out, 1)

        @block.vector
        def _(dve):
            chain = Chain(dve, steps)
            dve.memset(ones[:, :], 1.0).then_inc(ones_ready, 1)
            dve.sem_inc(part_ready, DEPTH)
            dve.sem_inc(z_ready, DEPTH)
            dve.wait_ge(landed, 16 * 7)
            chain.link(dve.tensor_reduce(csum[:, :, :], ct[:, :, :, :], AX.X, ALU.add))
            chain.link(dve.tensor_scalar(csum[:, :, :], csum[:, :, :], 1.0 / CTX, None, ALU.mult))
            dve.tensor_copy(cmean[:, :, :, :], csum[:, :, :].unsqueeze(3).to_broadcast([P, DT, B, P])
                            ).then_inc(mean_ready, 1)
            dve.wait_ge(w_ready, 1)
            for w in range(3):
                for b in range(B):
                    last = dve.tensor_tensor(spec[:, w, b, :], pk[:, w // 2, w % 2, :], kmod[:, b, :], ALU.mult)
            last.then_inc(spec_ready, 1)
            dve.wait_ge(spec_ready, 1)
            with dve.Fori(0, B) as b:
                for q in range(PAIRS_ + 1):
                    if q < PAIRS_:
                        n = b * PAIRS_ + q
                        s = q % DEPTH
                        dve.wait_ge(x_ready, n + 1)
                        dve.wait_ge(yf_ready, n + 1)
                        for i, (o, w) in enumerate(((0, 0), (1, 1), (0, 1), (1, 2))):
                            last = dve.tensor_tensor(
                                part[:, s, i, :, :], px[:, s, o, :, :],
                                spec[:, w, ds(b, 1), :].to_broadcast([P, 2, D]), ALU.mult)
                        last.then_inc(part_ready, 1)
                    if q:
                        n = b * PAIRS_ + q - 1
                        dve.wait_ge(y_ready, n + 1)
                        blocks = ds(b * KB + 2 * (q - 1), 2)
                        dve.tensor_tensor(Z[:, blocks, :], py[:, (q - 1) % DEPTH, :, :], X[:, blocks, :],
                                          ALU.add).then_inc(z_ready, 1)

        @block.gpsimd
        def _(pool):
            pool.sem_inc(yf_ready, DEPTH)
            with pool.Fori(0, B) as b:
                for q in range(PAIRS_):
                    n = b * PAIRS_ + q
                    s = q % DEPTH
                    pool.wait_ge(part_ready, n + 1 + DEPTH)
                    if q >= DEPTH:
                        pool.wait_ge(y_ready, n + 1 - DEPTH)
                    pool.tensor_tensor(yf[:, s, 0, :, :], part[:, s, 0, :, :], part[:, s, 1, :, :], ALU.subtract)
                    pool.tensor_tensor(yf[:, s, 1, :, :], part[:, s, 2, :, :], part[:, s, 3, :, :],
                                       ALU.add).then_inc(yf_ready, 1)


def kronecker_experts(nc, a, X, XT, spare, ident):
    R = P
    G = 4
    GB = 4
    W1, W2 = 32, 64
    PASSES = R // (G * GB)
    GROUPS = R // G
    K2 = 2
    FB = D // W1
    TOK = 4
    with ExitStack() as ctx:
        m = Mem(nc, ctx)
        bu = m.sb("bu_t", [P, E * W2])
        au = m.sb("au_t", [P, E * W2])
        bd = m.sb("bd_t", [P, E * W1])
        ad = m.sb("ad_t", [P, E * W1])
        ru = m.sb("ru", [P, TOK * DT, E])
        rd = m.sb("rd", [W2, W2, E])
        bias_u = m.sb("bias_u", [W2, W2])
        bias_d = m.sb("bias_d", [W1, W1])
        scale_u = m.sb("scale_u", [W2, 1])
        scale_d = m.sb("scale_d", [W1, 1])
        ones = m.sb("ones_s", [P, P])
        xs = m.sb("xs_s", [P, DT, CH])
        xn = m.sb("xn", [W1, R, W1])
        h = spare[0:W2, :, :].rearrange("p t d -> p (t d)").rearrange("p (r o) -> p r o", o=W2)
        y = xn
        best = m.sb("best_s", [P, 8])
        place = m.sb("place_s", [P, 8], U32)
        start_f = m.sb("start_f", [P, K2])
        start_i = m.sb("start_i", [P, K2], I32)
        starts = m.sb("starts", [1, R, K2], I32)
        gap = m.sb("gap", [P, K2])
        gate = m.sb("gate_s", [P, K2])
        spread = m.sb("spread", [P, K2, R])
        gates = m.sb("gates_s", [P, K2, R])
        stage = m.sb("stage_s", [P, DEPTH, G, W2])
        mid = m.sb("mid_s", [P, DEPTH, G, K2, W2])
        pre = m.sb("pre_s", [W2, DEPTH, G, W2])
        warm = m.sb("warm_s", [P, 1])
        p_route = m.ps("p_route", [P, CH])
        p_mid = m.ps("p_mid", [P, DEPTH, CH])
        p_out = m.ps("p_out", [P, DEPTH, CH])
        p_turn = m.ps("p_turn", [P, DEPTH, CH])
        landed, zeroed = m.sem("landed_s"), m.sem("zeroed_s")
        xs_ready, xn_ready = m.sem("xs_ready_s"), m.sem("xn_ready_s")
        route_ready, route_steps, starts_made, starts_landed = (m.sem("route_ready"), m.sem("route_steps"),
                                                                m.sem("starts_made"), m.sem("starts_landed"))
        gap_ready, gate_ready, spread_ready = m.sem("gap_ready"), m.sem("gate_ready_s"), m.sem("spread_ready")
        spread_turned, gates_ready = m.sem("spread_turned"), m.sem("gates_ready_s")
        staged, mid_ready, mid_out = m.sem("staged_s"), m.sem("mid_ready_s"), m.sem("mid_out_s")
        out_ready, out_read, h_ready = m.sem("out_ready_s"), m.sem("out_read_s"), m.sem("h_ready_s")
        turn_ready, added = m.sem("turn_ready"), m.sem("added_s")
        passed, pe_passed = m.sem("passed_s"), m.sem("pe_passed_s")
        LOADS = 10
        LAYERS = 2
        STEPS = 3
        block = ctx.enter_context(nc.Block())

        def inner(eng, c, layer, body):
            with eng.Fori(0, PASSES) as p:
                body(lambda i: (c * LAYERS + layer) * GROUPS + p * GB + i, lambda i: p * (GB * G) + i * G,
                     lambda i: c * GROUPS + p * GB + i)

        @block.sync
        def _(sp):
            sp.wait_ge(zeroed, 1)
            for dst, src in ((bu[0:W1, :], "b_up"), (au[0:W1, :], "a_up"), (bd[0:W2, :], "b_down"), (ad[0:W2, :], "a_down")):
                sp.dma_start(dst, a[src]).then_inc(landed, 16)
            sp.dma_start(ru[:, :, :], a["route_up"].rearrange("(k p) e -> p k e", p=P)).then_inc(landed, 16)
            sp.dma_start(rd[:, :, :], a["route_down"]).then_inc(landed, 16)
            for dst, src in ((bias_u, "bias_up"), (bias_d, "bias_down")):
                sp.dma_start(dst[:, :], a[src]).then_inc(landed, 16)
            for dst, src in ((scale_u, "scale_up"), (scale_d, "scale_down")):
                sp.dma_start(dst[:, :], a[src].to_broadcast([dst.shape[0], 1])).then_inc(landed, 16)
            with sp.Fori(0, NC) as c:
                for layer in range(LAYERS):
                    sp.wait_ge(starts_made, c * LAYERS + layer + 1)
                    sp.dma_start(starts[:, :, :], start_i[:, :]).then_inc(starts_landed, 16)

        @block.tensor
        def _(pe):
            pe.sem_inc(turn_ready, DEPTH)
            pe.sem_inc(mid_ready, DEPTH)
            pe.wait_ge(landed, 16 * LOADS)
            pe.wait_ge(zeroed, 2)
            with pe.Fori(0, NC) as c:
                for layer in range(LAYERS):
                    n_in, n_out = ((W1, W2), (W2, W1))[layer]
                    if layer == 0:
                        pe.wait_ge(xs_ready, c + 1)
                        for k in range(TOK * DT):
                            mm = pe.matmul(p_route[:, 0:E], xs[:, k % DT, k // DT::TOK], ru[:, k, :],
                                           start=(k == 0), stop=(k == TOK * DT - 1))
                    else:
                        pe.wait_ge(h_ready, (c + 1) * GROUPS + DEPTH)
                        for o in range(W2):
                            mm = pe.matmul(p_route[:, 0:E], h[:, :, o], rd[:, o, :], start=(o == 0), stop=(o == W2 - 1))
                    mm.then_inc(route_ready, 1)
                    pe.wait_ge(spread_ready, c * LAYERS + layer + 1)
                    pe.matmul(p_route[:, 0:K2 * R], ones[:, :], spread[:, :, :].rearrange("p k r -> p (k r)"),
                              start=True, stop=True).then_inc(spread_turned, 1)
                    pe.wait_ge(starts_landed, (c * LAYERS + layer + 1) * 16)
                    pe.sem_inc(pe_passed, 1)

                    def body(n, row, up_n):
                        regs = {}

                        def load(i):
                            _, r = nc.values_load_multi_w_load_instructions(
                                starts[0:1, ds(row(i), 2 * G), :].rearrange("o r k -> o (r k)"), min_val=0,
                                max_val=(E - 1) * n_out, engines=[mybir.EngineType.PE],
                                skip_runtime_bounds_check_because="places among the experts, times their width")
                            regs[i], regs[i + 1] = r[:G * K2], r[G * K2:]

                        def first(i):
                            pe.wait_ge(staged, n(i) + 1)
                            pe.wait_ge(mid_out, n(i) + 1)
                            table = (bu, bd)[layer]
                            for g in range(G):
                                for k in range(K2):
                                    col = (g * K2 + k) * n_out
                                    mm = pe.matmul(p_mid[0:n_in, i % DEPTH, col:col + n_out],
                                                   stage[:, i % DEPTH, g, 0:n_in],
                                                   table[:, ds(regs[i][g * K2 + k], n_out)], start=True, stop=True)
                            mm.then_inc(mid_ready, 1)

                        def second(i):
                            pe.wait_ge(mid_out, n(i) + 1 + DEPTH)
                            pe.wait_ge(out_read, n(i) + 1)
                            table = (au, ad)[layer]
                            for g in range(G):
                                for k in range(K2):
                                    mm = pe.matmul(p_out[0:n_out, i % DEPTH, g * n_out:(g + 1) * n_out],
                                                   mid[:, i % DEPTH, g, k, 0:n_out],
                                                   table[:, ds(regs[i][g * K2 + k], n_out)],
                                                   start=(k == 0), stop=(k == K2 - 1))
                            mm.then_inc(out_ready, 1)

                        for i in range(GB + 1):
                            if i < GB:
                                if i % 2 == 0:
                                    load(i)
                                first(i)
                            if i:
                                second(i - 1)

                    inner(pe, c, layer, body)
                pe.wait_ge(out_read, (c + 1) * LAYERS * GROUPS + DEPTH)
                for t in range(TPC):
                    pe.wait_ge(added, c * TPC + t + 1)
                    pe.sem_inc(pe_passed, 1)
                    for f in range(FB):
                        tok = y[:, t * W1:(t + 1) * W1, :].rearrange("p r o -> p (r o)")[:, f::FB]
                        mm = pe.transpose(p_turn[:, t % DEPTH, f * W1:(f + 1) * W1], tok, ident[0:W1, 0:W1])
                    mm.then_inc(turn_ready, 1)

        @block.vector
        def _(dve):
            for t in (bu, au, bd, ad):
                last = dve.memset(t[:, :], 0.0)
            last.then_inc(zeroed, 1)
            dve.memset(stage[:, :, :, :], 0.0)
            dve.memset(mid[:, :, :, :, :], 0.0)
            dve.memset(ones[:, :], 1.0).then_inc(zeroed, 1)
            dve.sem_inc(mid_out, DEPTH)
            dve.sem_inc(added, DEPTH)
            dve.wait_ge(landed, 16 * LOADS)
            dve.wait_ge(zeroed, 2)
            with dve.Fori(0, NC) as c:
                dve.wait_ge(added, c * TPC + DEPTH)
                for f in range(FB):
                    q = f % (FB // DT)
                    last = dve.tensor_copy(xn[:, :, f::FB],
                                           XT[q * W1:(q + 1) * W1, f // (FB // DT), ds(c * CH, CH)]
                                           .rearrange("p (r t) -> p r t", t=TOK))
                last.then_inc(xn_ready, 1)
                for layer in range(LAYERS):
                    n_in, n_out = ((W1, W2), (W2, W1))[layer]
                    v = c * LAYERS + layer
                    chain = Chain(dve, route_steps, v * STEPS)
                    dve.wait_ge(route_ready, v + 1)
                    dve.sem_inc(passed, 1)
                    chain.link(dve.max(best[:, :], p_route[:, 0:E]))
                    dve.sem_inc(passed, 1)
                    chain.link(dve.max_index(place[:, :], best[:, :], p_route[:, 0:E]))
                    dve.tensor_tensor(gap[:, 0:1], best[:, 0:1], best[:, 1:2], ALU.subtract)
                    dve.tensor_tensor(gap[:, 1:2], best[:, 1:2], best[:, 0:1], ALU.subtract).then_inc(gap_ready, 1)
                    chain.link(dve.tensor_scalar(start_f[:, :], place[:, 0:K2], float(n_out), None, ALU.mult))
                    dve.wait_ge(starts_landed, v * 16) if layer else dve.wait_ge(added, c * TPC + DEPTH)
                    dve.tensor_copy(start_i[:, :], start_f[:, :]).then_inc(starts_made, 1)
                    dve.wait_ge(gate_ready, v + 1)
                    for k in range(K2):
                        last = dve.tensor_scalar(spread[:, k, :], ident[:, :], gate[:, k:k + 1], None, ALU.mult)
                    last.then_inc(spread_ready, 1)
                    dve.wait_ge(spread_turned, v + 1)
                    dve.tensor_copy(gates[:, :, :].rearrange("p k r -> p (k r)"), p_route[:, 0:K2 * R]
                                    ).then_inc(gates_ready, 1)
                    dve.wait_ge(gates_ready, v + 1)
                    dve.sem_inc(passed, 1)

                    def body(n, row, up_n):
                        def gated(i):
                            dve.wait_ge(mid_ready, n(i) + 1 + DEPTH)
                            for k in range(K2):
                                last = dve.tensor_tensor(
                                    mid[0:n_in, i % DEPTH, :, k, 0:n_out],
                                    p_mid[0:n_in, i % DEPTH, 0:G * K2 * n_out].rearrange(
                                        "p (g k o) -> p g k o", g=G, k=K2)[:, :, k, :],
                                    gates[0:n_in, k, ds(row(i), G)].unsqueeze(2).to_broadcast([n_in, G, n_out]), ALU.mult)
                            last.then_inc(mid_out, 1)

                        def biased(i):
                            dve.wait_ge(out_ready, n(i) + 1)
                            src = p_out[0:n_out, i % DEPTH, 0:G * n_out].rearrange("p (g o) -> p g o", g=G)
                            if layer == 0:
                                dve.wait_ge(h_ready, up_n(i) + 1)
                                dve.scalar_tensor_tensor(pre[:, i % DEPTH, :, :], src, scale_u[:, 0:1],
                                                         bias_u[:, :].unsqueeze(1).to_broadcast([W2, G, W2]),
                                                         ALU.mult, ALU.add).then_inc(out_read, 1)
                            else:
                                dve.scalar_tensor_tensor(y[:, ds(row(i), G), :], src, scale_d[:, 0:1],
                                                         bias_d[:, :].unsqueeze(1).to_broadcast([W1, G, W1]),
                                                         ALU.mult, ALU.add).then_inc(out_read, 1)

                        for i in range(GB + 1):
                            if i < GB:
                                gated(i)
                            if i:
                                biased(i - 1)

                    inner(dve, c, layer, body)
                for t in range(TPC):
                    dve.wait_ge(turn_ready, c * TPC + t + 1 + DEPTH)
                    x = X[:, ds(c * TPC + t, 1), :].rearrange("p o d -> p (o d)")
                    dve.tensor_tensor(x, p_turn[:, t % DEPTH, 0:D], x, ALU.add).then_inc(added, 1)

        @block.scalar
        def _(act):
            act.sem_inc(out_read, DEPTH)
            act.sem_inc(h_ready, DEPTH)
            act.wait_ge(landed, 16 * LOADS)
            act.wait_ge(zeroed, 2)
            with act.Fori(0, NC) as c:
                act.wait_ge(out_read, c * LAYERS * GROUPS + DEPTH)
                act.copy(xs[:, :, :], XT[:, :, ds(c * CH, CH)]).then_inc(xs_ready, 1)
                for layer in range(LAYERS):
                    n_in, n_out = ((W1, W2), (W2, W1))[layer]
                    v = c * LAYERS + layer
                    act.wait_ge(gap_ready, v + 1)
                    act.activation(gate[:, :], gap[:, :], ACT.Sigmoid).then_inc(gate_ready, 1)
                    if layer == 0:
                        act.wait_ge(xn_ready, c + 1)
                        act.activation(warm[:, :], gap[:, 0:1], ACT.Gelu)
                    else:
                        act.wait_ge(h_ready, (c + 1) * GROUPS + DEPTH)

                    def body(n, row, up_n):
                        for i in range(GB + 1):
                            if i < GB:
                                act.wait_ge(mid_ready, n(i) + 1)
                                src = xn[:, ds(row(i), G), :] if layer == 0 else h[:, ds(row(i), G), :]
                                act.copy(stage[0:n_in, i % DEPTH, :, 0:n_in], src).then_inc(staged, 1)
                            if i and layer == 0:
                                act.wait_ge(out_read, n(i - 1) + 1 + DEPTH)
                                act.activation(h[:, ds(row(i - 1), G), :], pre[:, (i - 1) % DEPTH, :, :],
                                               ACT.Gelu).then_inc(h_ready, 1)

                    inner(act, c, layer, body)



def program(nc, a, out):
    with ExitStack() as ctx:
        m = Mem(nc, ctx)
        X = m.sb("X", [P, NT, D])
        XT = m.sb("XT", [P, DT, N])
        ident = m.sb("ident", [P, P])
        load_tokens(nc, a["x"], X, a["ident"], ident, XT)
        with ExitStack() as c2:
            heads = c2.enter_context(nc.sbuf_tensor("heads", [P, B * NG, S // P, HG * HD], F32))
            q_parts = nc.dram_tensor("q_parts", (3, B * D, S), BF16).ap()
            k_parts = nc.dram_tensor("k_parts", (3, B * D, S), BF16).ap()
            v_rows = nc.dram_tensor("v_rows", (B * NG, S, HG * 2 * HD), F32).ap()
            attention_project(nc, a, XT, q_parts, k_parts, v_rows)
            attention(nc, a, q_parts, k_parts, v_rows, heads, ident)
            attention_output(nc, a, X, heads, ident)
        layer_norm(nc, "_0a", X, XT, ident)
        sigmoid_cross(nc, a, X, XT)
        layer_norm(nc, "_0x", X, XT, ident)
        gated_mlp(nc, a, X, XT)
        with ExitStack() as c2:
            sim = c2.enter_context(nc.sbuf_tensor("sim", [P, NT, 2 * NH * NK], F32))
            thr = c2.enter_context(nc.sbuf_tensor("thr", [P, NT, NH], F32))
            shift = c2.enter_context(nc.sbuf_tensor("shift", [P, NT, NH], F32))
            peer_gates(nc, a, XT, sim, thr, shift)
            peer_experts(nc, a, X, XT, sim, thr, shift, ident)
        layer_norm(nc, "_0f", X, XT, ident)
        with ExitStack() as c2:
            grams = c2.enter_context(nc.sbuf_tensor("grams", [P, B * DT, 2, P], F32))
            vsum = c2.enter_context(nc.sbuf_tensor("vsum", [P, B * DT], F32))
            key_products(nc, a, XT, grams, vsum)
            normed_attention(nc, a, X, XT, grams, vsum)
        layer_norm(nc, "_1a", X, None, ident)
        Z = m.sb("Z", [P, NT, D])
        circular_filter(nc, a, X, Z)
        layer_norm(nc, "_1x", Z, XT, ident)
        kronecker_experts(nc, a, Z, XT, X, ident)
        layer_norm(nc, "_1f", Z, None, ident)
        X = Z
        store_tokens(nc, X, out)


def kernel(**inputs):
    import concourse.bacc as _bacc
    from concourse.bass_utils import run_bass_kernel_spmd as _run

    arrays = {k: np.ascontiguousarray(v) for k, v in lay_out(inputs).items()}
    nc = _bacc.Bacc("TRN2", target_bir_lowering=False, num_devices=1)
    aps = {k: nc.dram_tensor("in_" + k, v.shape, mybir.dt.from_np(v.dtype), kind="ExternalInput").ap()
           for k, v in arrays.items()}
    out = nc.dram_tensor("out_0", (B, S, D), F32, kind="ExternalOutput").ap()
    program(nc, aps, out)
    r = _run(nc, [{"in_" + k: v for k, v in arrays.items()}], core_ids=[0])
    return r.results[0]["out_0"]


def fourier():
    L = 2 * P
    n, k = np.arange(L)[:, None], np.arange(P)[None, :]
    angle = 2 * np.pi * ((n * k) % L) / L
    last = np.where(n % 2 == 0, 1.0, -1.0)
    cos, sin = np.cos(angle), -np.sin(angle)
    sin_last = sin.copy()
    sin_last[:, :1] = last
    cos_last = cos.copy()
    cos_last[:, :1] = last
    back = np.full((P, 1), 2.0 / L)
    back[0] = 1.0 / L
    fwd = np.stack([cos[:P], cos[P:], sin_last[:P], sin_last[P:]])
    return {
        "dft_fwd": fwd.astype(np.float32),
        "dft_taps": np.stack([cos[:P], sin[:P], cos_last[:P]]).astype(np.float32),
        "dft_inv": np.stack([back * cos[P:].T, back * sin_last[P:].T]).astype(np.float32),
    }


def lay_out(inputs):
    def heads_last(w):
        return np.transpose(w, (1, 0, 2)).reshape(w.shape[1], -1)

    def table(w):
        return np.transpose(w, (2, 0, 1)).reshape(w.shape[2], -1)

    def padded(w, axis):
        shape = list(w.shape)
        shape[axis] = P
        full = np.zeros(shape, w.dtype)
        full[tuple(slice(0, n) for n in w.shape)] = w
        return full

    def peer_keys(keys):
        heads, count, halves, n = keys.shape
        full = np.zeros((halves * heads, n, 2, count), keys.dtype)
        for half in range(halves):
            for h in range(heads):
                g = half * heads + h
                full[g, :, g % 2, :] = keys[h, :, half, :].T
        return full.reshape(halves * heads * n, 2 * count)

    i = {k: np.asarray(v) for k, v in inputs.items()}
    return {
        "x": i["x"],
        "ident": np.eye(P, dtype=np.float32),
        "wq0": heads_last(i["L0_attn_W_query"]),
        "wk0": heads_last(i["L0_attn_W_key"]),
        "wv0": heads_last(i["L0_attn_W_val"]),
        "wo0": i["L0_attn_W_out"].reshape(D, D),
        "ctx_t": np.transpose(i["ctx_1024"], (2, 0, 1)).reshape(D, B * CTX),
        "wq_x": padded(i["L0_xattn_Wq"].T, 1),
        "wk_x": padded(i["L0_xattn_Wk"].T, 1),
        "wv_x": i["L0_xattn_Wv"].T,
        "bq_x": padded(i["L0_xattn_bq"][:, None], 0),
        "bk_x": padded(i["L0_xattn_bk"][:, None], 0),
        "bv_x": i["L0_xattn_bv"][None, :],
        "wg": i["L0_ffn_Wg"],
        "wu": i["L0_ffn_Wu"],
        "wd": i["L0_ffn_Wd"],
        "bg": i["L0_ffn_bg"].reshape(FF // P, P).T,
        "bu": i["L0_ffn_bu"].reshape(FF // P, P).T,
        "bd": i["L0_ffn_bd"][None, :],
        "peer_wq_t": i["L0_ffn_Wq"].T,
        "peer_keys": peer_keys(i["L0_ffn_keys"]),
        "down_t": i["L0_ffn_down_embed"].T,
        "up": i["L0_ffn_up_embed"],
        "wkv1": i["L1_attn_w_qkv"][D:, :].T,
        "wq1": i["L1_attn_w_qkv"][:D, :].T,
        "wo1": i["L1_attn_w_out"].T,
        "bo1": i["L1_attn_b_out"][None, :],
        "norm_g": np.repeat(i["L1_attn_norm_g"].reshape(H0), HD).reshape(DT, P).T,
        "norm_b": np.repeat(i["L1_attn_norm_b"].reshape(H0), HD).reshape(DT, P).T,
        "mask": np.kron(np.eye(P // HD), np.ones((HD, HD))).astype(np.float32),
        "taps_t": i["L1_xattn_weight"].T,
        "kp_w_t": i["L1_xattn_kp_w"].T,
        "kp_b": i["L1_xattn_kp_b"][None, :],
        **fourier(),
        "b_up": table(i["L1_ffn_B_up"]),
        "a_up": table(i["L1_ffn_A_up"]),
        "b_down": table(i["L1_ffn_B_down"]),
        "a_down": table(i["L1_ffn_A_down"]),
        "route_up": i["L1_ffn_W_up"].T,
        "route_down": np.transpose(i["L1_ffn_W_down"].reshape(E, 64, 64), (2, 1, 0)),
        "bias_up": i["L1_ffn_bias_up"].reshape(64, 64).T,
        "bias_down": i["L1_ffn_bias_down"].reshape(32, 32).T,
        "scale_up": i["L1_ffn_scale_up"][None, :],
        "scale_down": i["L1_ffn_scale_down"][None, :],
    }
```

```python
from contextlib import ExitStack

import numpy as np

import concourse.bass as bass
from concourse import mybir

F32 = mybir.dt.float32
BF16 = mybir.dt.bfloat16
I32 = mybir.dt.int32
U32 = mybir.dt.uint32
ALU = mybir.AluOpType
ACT = mybir.ActivationFunctionType
AX = mybir.AxisListType
ds = bass.ds

P = 128
B, S, D = 4, 1024, 256
N = B * S
NT = N // P
DT = D // P
CH = 512
NC = N // CH
TPC = CH // P
H0, HD = 16, 16
HG = 4
NG = H0 // HG
KB = S // P
CTX = 77
FF = 1024
NH, NK, TOPK = 4, 64, 8
NX = FF // NK
E = 64
LN_EPS = 1e-5
DEPTH = 2


class Mem:

    def __init__(self, nc, ctx):
        self.nc, self.ctx, self.sems = nc, ctx, []
        ctx.callback(self.release)

    def release(self):
        if self.sems:
            self.nc.clear_and_free_semaphores(self.sems)
            self.nc.all_engine_barrier()

    def sb(self, name, shape, dt=F32):
        return self.ctx.enter_context(self.nc.sbuf_tensor(name, shape, dt))

    def ps(self, name, shape, dt=F32):
        return self.ctx.enter_context(self.nc.psum_tensor(name, shape, dt))

    def sem(self, name):
        self.sems.append(self.nc.alloc_semaphore(name))
        return self.sems[-1]


class Chain:

    def __init__(self, eng, sem, base=0):
        self.eng, self.sem, self.base, self.n = eng, sem, base, 0

    def step(self, ins):
        self.n += 1
        ins.then_inc(self.sem, 1)

    def settle(self):
        self.eng.wait_ge(self.sem, self.base + self.n)

    def link(self, ins):
        self.step(ins)
        self.settle()


def load_tokens(nc, x, X, ident_d, ident, XT):
    with ExitStack() as ctx:
        m = Mem(nc, ctx)
        xstage = m.sb("xstage", [P, DEPTH, D])
        warm = m.sb("warm_in", [P, 1])
        tp = m.ps("tp_in", [P, DEPTH, 512])
        x_landed, id_landed = m.sem("x_landed"), m.sem("id_landed")
        staged, turned, turned_out = m.sem("in_staged"), m.sem("in_turned"), m.sem("in_turned_out")
        block = ctx.enter_context(nc.Block())

        @block.sync
        def _(sp):
            sp.dma_start(ident[:, :], ident_d).then_inc(id_landed, 16)
            sp.dma_start(X[:, :, :], x.rearrange("b (t p) d -> p (b t) d", p=P)).then_inc(x_landed, 16)

        @block.vector
        def _(dve):
            dve.wait_ge(x_landed, 16)
            with dve.Fori(0, NT // DEPTH) as j:
                for s in range(DEPTH):
                    dve.wait_ge(turned, j * DEPTH + s + 1)
                    dve.tensor_copy(xstage[:, s, :], X[:, ds(j * DEPTH + s, 1), :]).then_inc(staged, 1)

        @block.tensor
        def _(pe):
            pe.sem_inc(turned, DEPTH)
            pe.wait_ge(id_landed, 16)
            with pe.Fori(0, NT // DEPTH) as j:
                for s in range(DEPTH):
                    pe.wait_ge(staged, j * DEPTH + s + 1)
                    pe.wait_ge(turned_out, j * DEPTH + s + 1)
                    for k in range(DT):
                        t = pe.transpose(tp[:, s, k * P:(k + 1) * P], xstage[:, s, k * P:(k + 1) * P], ident[:, :])
                    t.then_inc(turned, 1)

        @block.scalar
        def _(act):
            act.wait_ge(id_landed, 16)
            act.activation(warm[:, :], ident[:, 0:1], ACT.Identity)
            act.sem_inc(turned_out, DEPTH)
            with act.Fori(0, NT // DEPTH) as j:
                for s in range(DEPTH):
                    act.wait_ge(turned, j * DEPTH + s + 1 + DEPTH)
                    act.copy(XT[:, :, ds(j * DEPTH * P + s * P, P)],
                             tp[:, s, 0:D].rearrange("p (k t) -> p k t", k=DT)).then_inc(turned_out, 1)


def layer_norm(nc, tag, X, XT, ident, loads=(), landed=None, blank=()):
    with ExitStack() as ctx:
        m = Mem(nc, ctx)
        stats = m.sb("stats" + tag, [P, NT, 6])
        total = m.sb("total" + tag, [P, NT])
        diff = m.sb("diff" + tag, [P, NT])
        var4 = m.sb("var4" + tag, [P, NT])
        std = m.sb("std" + tag, [P, NT])
        rstd = m.sb("rstd" + tag, [P, NT])
        shift = m.sb("shift" + tag, [P, NT])
        eps = m.sb("eps" + tag, [P, 1])
        y = m.sb("y" + tag, [P, DEPTH, D])
        tp = m.ps("tp" + tag, [P, DEPTH, 512])
        stats_done, dve_steps = m.sem("stats_done" + tag), m.sem("ln_steps" + tag)
        var_ready, std_ready = m.sem("var_ready" + tag), m.sem("std_ready" + tag)
        y_ready, turned = m.sem("y_ready" + tag), m.sem("turned" + tag)
        turned_out, blanked = m.sem("turned_out" + tag), m.sem("blanked" + tag)
        block = ctx.enter_context(nc.Block())

        if blank:
            @block.gpsimd
            def _(pool):
                for t in blank:
                    pool.memset(t, 0.0).then_inc(blanked, 1)

        if loads:
            @block.sync
            def _(sp):
                if blank:
                    sp.wait_ge(blanked, len(blank))
                for dst, src in loads:
                    sp.dma_start(dst, src).then_inc(landed, 16)

        @block.vector
        def _(dve):
            chain = Chain(dve, dve_steps)
            dve.memset(eps[:, :], LN_EPS).then_inc(var_ready, 1)
            with dve.Fori(0, NT // TPC) as c:
                for t in range(TPC):
                    last = dve.bn_stats(stats[:, ds(c * TPC + t, 1), :], X[:, ds(c * TPC + t, 1), :])
                last.then_inc(stats_done, 1)
            dve.wait_ge(stats_done, NT // TPC)
            chain.step(dve.tensor_tensor(total[:, :], stats[:, :, 1], stats[:, :, 4], ALU.add))
            chain.step(dve.tensor_tensor(diff[:, :], stats[:, :, 1], stats[:, :, 4], ALU.subtract))
            chain.link(dve.tensor_tensor(var4[:, :], stats[:, :, 2], stats[:, :, 5], ALU.add))
            chain.link(dve.tensor_tensor(diff[:, :], diff[:, :], diff[:, :], ALU.mult))
            dve.scalar_tensor_tensor(var4[:, :], var4[:, :], 4.0 / D, diff[:, :], ALU.mult, ALU.add).then_inc(var_ready, 1)
            dve.wait_ge(std_ready, 1)
            chain.link(dve.reciprocal(rstd[:, :], std[:, :]))
            chain.link(dve.scalar_tensor_tensor(shift[:, :], total[:, :], -0.5, rstd[:, :], ALU.mult, ALU.mult))
            with dve.Fori(0, NT // DEPTH) as j:
                for s in range(DEPTH):
                    i = j * DEPTH + s
                    if XT is not None:
                        dve.wait_ge(turned, i + 1)
                        dve.tensor_scalar(y[:, s, :], X[:, ds(i, 1), :], rstd[:, ds(i, 1)], shift[:, ds(i, 1)],
                                          ALU.mult, ALU.add).then_inc(y_ready, 1)
                    dve.tensor_scalar(X[:, ds(i, 1), :], X[:, ds(i, 1), :], rstd[:, ds(i, 1)], shift[:, ds(i, 1)],
                                      ALU.mult, ALU.add)

        @block.scalar
        def _(act):
            if XT is not None:
                act.sem_inc(turned_out, DEPTH)
            act.wait_ge(var_ready, 2)
            act.activation(std[:, :], var4[:, :], ACT.Sqrt, bias=eps[:, 0:1], scale=0.25).then_inc(std_ready, 1)
            if XT is not None:
                with act.Fori(0, NT // DEPTH) as j:
                    for s in range(DEPTH):
                        act.wait_ge(turned, j * DEPTH + s + 1 + DEPTH)
                        act.copy(XT[:, :, ds(j * DEPTH * P + s * P, P)],
                                 tp[:, s, 0:D].rearrange("p (k t) -> p k t", k=DT)).then_inc(turned_out, 1)

        if XT is not None:
            @block.tensor
            def _(pe):
                pe.sem_inc(turned, DEPTH)
                with pe.Fori(0, NT // DEPTH) as j:
                    for s in range(DEPTH):
                        pe.wait_ge(y_ready, j * DEPTH + s + 1)
                        pe.wait_ge(turned_out, j * DEPTH + s + 1)
                        for k in range(DT):
                            t = pe.transpose(tp[:, s, k * P:(k + 1) * P], y[:, s, k * P:(k + 1) * P], ident[:, :])
                        t.then_inc(turned, 1)


def store_tokens(nc, X, out):
    with ExitStack() as ctx:
        m = Mem(nc, ctx)
        stored = m.sem("stored")
        block = ctx.enter_context(nc.Block())

        @block.sync
        def _(sp):
            sp.dma_start(out.rearrange("b (t p) d -> p (b t) d", p=P), X[:, :, :]).then_inc(stored, 16)
            sp.wait_ge(stored, 16)


STACK = 6 * HD
ROWS = STACK + 3
PAIRS = [(0, 0), (1, 0), (2, 0), (0, 1), (1, 1), (0, 2)]


def attention_project(nc, a, XT, q_parts, k_parts, v_rows):
    with ExitStack() as ctx:
        m = Mem(nc, ctx)
        wqk = m.sb("wqk", [P, 2, DT, D])
        wv = m.sb("wv", [P, DT, D])
        xs = m.sb("xs_p0", [P, DEPTH, DT, CH])
        parts = m.sb("parts", [P, DEPTH, 3, CH], BF16)
        rest = m.sb("rest", [P, DEPTH, CH])
        v_out = m.sb("v_out", [P, DEPTH, 2, H0, 2, HD])
        warm = m.sb("warm_p0", [P, 1])
        pp = m.ps("pp", [P, DEPTH, CH])
        pv = m.ps("pv", [P, DEPTH, 2, D])
        w_landed, xs_ready = m.sem("w_landed_p0"), m.sem("xs_ready_p0")
        p_ready, high_ready, rest_ready = m.sem("p_ready"), m.sem("high_ready"), m.sem("rest_ready")
        mid_ready, low_ready = m.sem("mid_ready"), m.sem("low_ready")
        parts_kept = [m.sem(f"parts_kept{s}") for s in range(DEPTH)]
        v_kept = [m.sem(f"v_kept{s}") for s in range(DEPTH)]
        v_ready, v_copied = m.sem("v_ready"), m.sem("v_copied")
        PER = 2 * DT
        block = ctx.enter_context(nc.Block())

        @block.sync
        def _(sp):
            sp.dma_start(wqk[:, 0, :, :], a["wq0"].rearrange("(k p) f -> p k f", p=P)).then_inc(w_landed, 16)
            sp.dma_start(wqk[:, 1, :, :], a["wk0"].rearrange("(k p) f -> p k f", p=P)).then_inc(w_landed, 16)
            sp.dma_start(wv[:, :, :], a["wv0"].rearrange("(k p) f -> p k f", p=P)).then_inc(w_landed, 16)
            for s in range(DEPTH):
                sp.sem_inc(parts_kept[s], 16)
                sp.sem_inc(v_kept[s], 32)
            with sp.Fori(0, B) as b:
                for half in range(S // CH):
                    c = b * (S // CH) + half
                    for o in range(PER):
                        dst = (q_parts, k_parts)[o // DT][:, ds(b * D + (o % DT) * P, P), half * CH:(half + 1) * CH]
                        sp.wait_ge(low_ready, c * PER + o + 1)
                        sp.dma_start(dst.rearrange("l f t -> f l t"),
                                     parts[:, o % DEPTH, :, :]).then_inc(parts_kept[o % DEPTH], 16)
                    for s in range(DEPTH):
                        for t in range(2):
                            sp.wait_ge(v_copied, c * DEPTH + s + 1 + DEPTH)
                            row = half * CH + (s * 2 + t) * P
                            sp.dma_start(v_rows[ds(b * NG, NG), row:row + P, :].rearrange("g p f -> p g f"),
                                         v_out[:, s, t, :, :, :].rearrange("p (g h) o w -> p g (h o w)", g=NG)
                                         ).then_inc(v_kept[s], 16)
            for s in range(DEPTH):
                sp.wait_ge(parts_kept[s], 16 * (1 + NC * PER // DEPTH))
                sp.wait_ge(v_kept[s], 32 * (1 + NC))

        @block.gpsimd
        def _(pool):
            with pool.Fori(0, NC // DEPTH) as j:
                for s in range(DEPTH):
                    pool.wait_ge(v_ready, (j * DEPTH + s + 1) * DEPTH)
                    pool.tensor_copy(xs[:, s, :, :], XT[:, :, ds((j * DEPTH + s) * CH, CH)]).then_inc(xs_ready, 1)

        @block.tensor
        def _(pe):
            pe.sem_inc(v_ready, DEPTH * DEPTH)
            pe.wait_ge(w_landed, 48)
            with pe.Fori(0, NC // DEPTH) as j:
                for s in range(DEPTH):
                    c = j * DEPTH + s
                    for o in range(PER):
                        pe.wait_ge(rest_ready, c * PER + o + 1)
                        for k in range(DT):
                            mm = pe.matmul(pp[:, o % DEPTH, :], wqk[:, o // DT, k, (o % DT) * P:(o % DT + 1) * P],
                                           XT[:, k, ds(c * CH, CH)], start=(k == 0), stop=(k == DT - 1))
                        mm.then_inc(p_ready, 1)
                    pe.wait_ge(xs_ready, c + 1)
                    for t in range(TPC):
                        if t % 2 == 0:
                            pe.wait_ge(v_copied, c * DEPTH + t // 2 + 1)
                        for k in range(DT):
                            mm = pe.matmul(pv[:, t // 2, t % 2, :], xs[:, s, k, t * P:(t + 1) * P], wv[:, k, :],
                                           start=(k == 0), stop=(k == DT - 1))
                        if t % 2 == 1 and t < TPC - 1:
                            mm.then_inc(v_ready, 1)
                    mm.then_inc(v_ready, 1)

        @block.scalar
        def _(act):
            act.wait_ge(w_landed, 48)
            act.activation(warm[:, :], wv[:, 0, 0:1], ACT.Identity)
            with act.Fori(0, NC) as c:
                for o in range(PER):
                    act.wait_ge(p_ready, c * PER + o + 1)
                    act.wait_ge(parts_kept[o % DEPTH], (c * (PER // DEPTH) + o // DEPTH + 1) * 16)
                    act.copy(parts[:, o % DEPTH, 0, :], pp[:, o % DEPTH, :]).then_inc(high_ready, 1)
                    act.wait_ge(rest_ready, c * PER + o + 1 + DEPTH)
                    act.copy(parts[:, o % DEPTH, 1, :], rest[:, o % DEPTH, :]).then_inc(mid_ready, 1)

        @block.vector
        def _(dve):
            dve.sem_inc(rest_ready, DEPTH)
            for s in range(DEPTH):
                ones = dve.memset(v_out[:, s, :, :, 1, :], 1.0)
            ones.then_inc(v_copied, DEPTH)
            with dve.Fori(0, NC) as c:
                for o in range(PER):
                    dve.wait_ge(high_ready, c * PER + o + 1)
                    dve.tensor_tensor(rest[:, o % DEPTH, :], pp[:, o % DEPTH, :], parts[:, o % DEPTH, 0, :],
                                      ALU.subtract).then_inc(rest_ready, 1)
                    dve.wait_ge(mid_ready, c * PER + o + 1)
                    dve.tensor_tensor(parts[:, o % DEPTH, 2, :], rest[:, o % DEPTH, :], parts[:, o % DEPTH, 1, :],
                                      ALU.subtract).then_inc(low_ready, 1)
                for s in range(DEPTH):
                    dve.wait_ge(v_ready, c * DEPTH + s + 1 + DEPTH * DEPTH)
                    dve.wait_ge(v_kept[s], (c + 1) * 32)
                    for t in range(2):
                        last = dve.tensor_copy(v_out[:, s, t, :, 0, :], pv[:, s, t, :].rearrange("p (h w) -> p h w", h=H0))
                    last.then_inc(v_copied, 1)



def attention(nc, a, q_parts, k_parts, v_rows, heads, ident):
    UNITS = B * NG
    SLOTS = 4
    QT = S // P
    QH = S // CH
    STEPS = QH * KB
    BANKS = HG * QT * 2
    PER_STEP = 6
    TOP = 4
    with ExitStack() as ctx:
        m = Mem(nc, ctx)
        qs = m.sb("qs", [P, SLOTS, HG, S], BF16)
        ks = m.sb("ks", [P, SLOTS, HG, S], BF16)
        va = m.sb("va", [P, SLOTS, KB, HG, 2 * HD])
        half_max = m.sb("half_max", [P, HG * QT, 2])
        top = m.sb("top", [P, HG * QT])
        top_rest = m.sb("top_rest", [P, HG * QT])
        top_parts = m.sb("top_parts", [P, 3, HG * QT], BF16)
        top_rows = m.sb("top_rows", [3 * HG * QT, P], BF16)
        identb = m.sb("identb", [P, P], BF16)
        probs = m.sb("probs", [P, DEPTH, HG, CH])
        o_sb = m.sb("o_sb", [P, CH])
        z_inv = m.sb("z_inv", [P, TPC, HG])
        scores = m.ps("scores", [P, 2, CH])
        scores_t = m.ps("scores_t", [P, HG, CH])
        acc = m.ps("acc", [P, CH])
        misc = m.ps("misc", [P, CH])
        miscb = misc[:, :].bitcast(BF16)
        ones_ready = m.sem("ones_ready")
        qk_landed = [m.sem(f"qk_landed{s}") for s in range(SLOTS)]
        v_landed = [m.sem(f"v_landed{s}") for s in range(SLOTS)]
        identb_ready = m.sem("identb_ready")
        s_ready, s_read = m.sem("s_ready"), m.sem("s_read")
        top_steps, parts_ready, rows_ready = m.sem("top_steps"), m.sem("top_parts_ready"), m.sem("top_rows_ready")
        rows_out, rows_landed = m.sem("top_rows_out"), m.sem("top_rows_landed")
        st_ready, p_ready, pv_done = m.sem("st_ready"), m.sem("probs_ready"), m.sem("pv_done")
        o_out, o_turned, z_ready, o_done = m.sem("o_out"), m.sem("o_turned"), m.sem("z_ready"), m.sem("o_done")
        block = ctx.enter_context(nc.Block())

        def banks_of(step):
            return range(min(PER_STEP * step, BANKS), min(PER_STEP * (step + 1), BANKS))

        def units(eng, unit):
            unit(0, 0, 0, False, True)
            with eng.Fori(0, UNITS // SLOTS - 1) as j:
                for g in range(1, SLOTS + 1):
                    unit(j * SLOTS + g, g % SLOTS, j + g // SLOTS, True, True)
            for g in range(1, SLOTS):
                unit(UNITS - SLOTS + g, g, UNITS // SLOTS - 1, True, g < SLOTS - 1)

        @block.sync
        def _(sp):
            def load(u, slot):
                rows = ds(u * HG * HD, HG * HD)
                for part, (lq, lk) in enumerate(PAIRS):
                    for dst, src, level in ((qs, q_parts, lq), (ks, k_parts, lk)):
                        sp.dma_start(dst[part * HD:(part + 1) * HD, slot, :, :],
                                     src[level, rows, :].rearrange("(h d) t -> d h t", h=HG)).then_inc(qk_landed[slot], 16)
                sp.dma_start(va[:, slot, :, :, :].rearrange("p k h d -> p k (h d)"),
                             v_rows[ds(u, 1), :, :].rearrange("u (k p) f -> p (u k) f", p=P)).then_inc(v_landed[slot], 16)

            def send_top(u, slot):
                sp.wait_ge(rows_out, u + 1)
                for part in range(3):
                    sp.dma_start(qs[STACK + part:STACK + part + 1, slot, :, :].rearrange("o h (q j) -> o (h q) j", j=P),
                                 top_rows[part * HG * QT:(part + 1) * HG * QT, :]
                                 ).then_inc(rows_landed, 16)

            def unit(u, slot, turn, has_prev, has_next, loads=True):
                if has_prev and loads:
                    sp.wait_ge(pv_done, u * STEPS + DEPTH)
                if loads:
                    load(u + SLOTS - 1, (slot + SLOTS - 1) % SLOTS)
                if has_next:
                    send_top(u + 1, (slot + 1) % SLOTS)

            for slot in range(SLOTS - 1):
                load(slot, slot)
            send_top(0, 0)
            unit(0, 0, 0, False, True)
            with sp.Fori(0, UNITS // SLOTS - 1) as j:
                for g in range(1, SLOTS + 1):
                    unit(j * SLOTS + g, g % SLOTS, None, True, True)
            for g in range(1, SLOTS):
                unit(UNITS - SLOTS + g, g, None, True, g < SLOTS - 1, loads=False)

        @block.gpsimd
        def _(pool):
            pool.memset(ks[STACK:P, :, :, :], 1.0).then_inc(ones_ready, 1)

        @block.tensor
        def _(pe):
            def top_bank(u, slot, n):
                h, q, half = n // (QT * 2), n // 2 % QT, n % 2
                pe.wait_ge(s_read, u * BANKS + n + 1)
                pe.matmul(scores[:, n % 2, :], qs[0:STACK, slot, h, q * P:(q + 1) * P],
                          ks[0:STACK, slot, h, half * CH:(half + 1) * CH], start=True, stop=True).then_inc(s_ready, 1)

            def top_turn(u, done):
                pe.wait_ge(parts_ready, u + 1)
                pe.wait_ge(o_done, done + 1)
                pe.transpose(miscb[0:3 * HG * QT, 0:P], top_parts[:, :, :].rearrange("p l r -> p (l r)"),
                             identb[:, :]).then_inc(rows_ready, 1)

            def turn_outputs(u, qh, after_top):
                pe.wait_ge(o_out, u * QH + qh + 2)
                if after_top is not None:
                    pe.wait_ge(rows_out, after_top + 1)
                else:
                    pe.wait_ge(o_done, u * QH + qh + 1)
                for t in range(TPC):
                    mm = pe.transpose(misc[:, t * P:(t + 1) * P], o_sb[:, t * P:(t + 1) * P], ident[:, :])
                mm.then_inc(o_turned, 1)

            def keys(u, slot, step, pair):
                qh, kb = step // KB, step % KB
                pe.wait_ge(p_ready, (u * STEPS + step) * 2 + pair + 1)
                for h in (2 * pair, 2 * pair + 1):
                    mm = pe.matmul(scores_t[:, h, :], ks[0:ROWS, slot, h, kb * P:(kb + 1) * P],
                                   qs[0:ROWS, slot, h, qh * CH:(qh + 1) * CH], start=True, stop=True)
                mm.then_inc(st_ready, 1)

            def values(u, slot, turn, step):
                qh, kb = step // KB, step % KB
                pe.wait_ge(p_ready, (u * STEPS + step) * 2 + 4)
                if kb == 0:
                    pe.wait_ge(o_out, u * QH + qh + 1)
                if step == 0:
                    pe.wait_ge(v_landed[slot], (turn + 1) * 16)
                for h in range(HG):
                    mm = pe.matmul(acc[h * 32:(h + 1) * 32, :], va[:, slot, kb, h, :],
                                   probs[:, step % DEPTH, h, :], start=(kb == 0), stop=(kb == KB - 1))
                mm.then_inc(pv_done, 1)

            def unit(u, slot, turn, has_prev, has_next):
                nxt, before = (slot + 1) % SLOTS, (slot + SLOTS - 1) % SLOTS
                pe.wait_ge(rows_landed, (u + 1) * 48)
                if has_next:
                    pe.wait_ge(qk_landed[nxt], (turn + 1 + (slot + 1) // SLOTS) * 16 * 2 * len(PAIRS))
                for step in range(STEPS):
                    tops = list(banks_of(step)) if has_next else []

                    def some(count):
                        for n in tops[:count]:
                            top_bank(u + 1, nxt, n)
                        del tops[:count]

                    some(1)
                    keys(u, slot, step, 0)
                    some(1)
                    keys(u, slot, step, 1)
                    some(2)
                    if step:
                        values(u, slot, turn, step - 1)
                    elif has_prev:
                        values(u - 1, before, turn, STEPS - 1)
                    some(len(tops))
                    if step == 2 and has_prev:
                        turn_outputs(u - 1, 1, u)
                    if step == KB + 2:
                        turn_outputs(u, 0, None if has_prev else 0)
                    if step == BANKS // PER_STEP + 2 and has_next:
                        top_turn(u + 1, u * QH + 1)
                if not has_next:
                    values(u, slot, turn, STEPS - 1)
                    turn_outputs(u, 1, None)

            pe.sem_inc(pv_done, DEPTH)
            pe.sem_inc(o_turned, 1)
            pe.wait_ge(identb_ready, 1)
            pe.wait_ge(ones_ready, 1)
            pe.wait_ge(qk_landed[0], 16 * 2 * len(PAIRS))
            for n in range(BANKS):
                top_bank(0, 0, n)
            top_turn(0, 0)
            units(pe, unit)

        @block.scalar
        def _(act):
            def keep_outputs(u, qh):
                act.wait_ge(pv_done, u * STEPS + (qh + 1) * KB + DEPTH)
                act.wait_ge(o_turned, u * QH + qh + 1)
                act.copy(o_sb[:, :], acc[:, :]).then_inc(o_out, 1)

            def unit(u, slot, turn, has_prev, has_next):
                for step in range(STEPS):
                    for pair in range(2):
                        n = (u * STEPS + step) * 2 + pair
                        act.wait_ge(st_ready, n + 1)
                        if pair == 0:
                            act.wait_ge(pv_done, u * STEPS + step + 1)
                        act.activation(probs[:, step % DEPTH, 2 * pair:2 * pair + 2, :],
                                       scores_t[:, 2 * pair:2 * pair + 2, :], ACT.Exp,
                                       scale=float(HD) ** -0.5).then_inc(p_ready, 1)
                    if step == 0 and has_prev:
                        keep_outputs(u - 1, 1)
                    if step == KB:
                        keep_outputs(u, 0)
                if not has_next:
                    keep_outputs(u, 1)

            act.sem_inc(p_ready, DEPTH)
            act.sem_inc(o_out, 1)
            act.wait_ge(identb_ready, 1)
            act.activation(o_sb[:, 0:1], identb[:, 0:1], ACT.Exp)
            units(act, unit)

        @block.vector
        def _(dve):
            def bank_max(u, n):
                dve.wait_ge(s_ready, u * BANKS + n + 1)
                dve.tensor_reduce(half_max[:, n // 2, n % 2:n % 2 + 1], scores[:, n % 2, :], AX.X,
                                  ALU.max).then_inc(s_read, 1)

            def split_top(u):
                chain = Chain(dve, top_steps, u * TOP)
                dve.wait_ge(s_read, (u + 1) * BANKS + DEPTH)
                chain.link(dve.tensor_reduce(top[:, :], half_max[:, :, :], AX.X, ALU.max))
                chain.link(dve.tensor_scalar(top_parts[:, 0, :], top[:, :], -1.0, None, ALU.mult))
                chain.link(dve.scalar_tensor_tensor(top_rest[:, :], top[:, :], -1.0, top_parts[:, 0, :],
                                                    ALU.mult, ALU.subtract))
                chain.link(dve.tensor_copy(top_parts[:, 1, :], top_rest[:, :]))
                dve.tensor_tensor(top_parts[:, 2, :], top_rest[:, :], top_parts[:, 1, :],
                                  ALU.subtract).then_inc(parts_ready, 1)

            def keep_top(u):
                dve.wait_ge(rows_ready, u + 1)
                dve.wait_ge(rows_landed, u * 48)
                dve.tensor_copy(top_rows[:, :], miscb[0:3 * HG * QT, 0:P]).then_inc(rows_out, 1)

            def normalise(u, qh):
                dve.wait_ge(o_turned, u * QH + qh + 2)
                o = misc[:, :].rearrange("p (t h w) -> p t h w", t=TPC, h=HG)
                dve.reciprocal(z_inv[:, :, :], o[:, :, :, HD]).then_inc(z_ready, 1)
                dve.wait_ge(z_ready, u * QH + qh + 1)
                for t in range(TPC):
                    last = dve.tensor_tensor(
                        heads[:, ds(u, 1), qh * TPC + t, :].rearrange("p u (h w) -> p (u h) w", h=HG),
                        o[:, t, :, 0:HD], z_inv[:, t, :].unsqueeze(2).to_broadcast([P, HG, HD]), ALU.mult)
                last.then_inc(o_done, 1)

            def unit(u, slot, turn, has_prev, has_next):
                for step in range(STEPS):
                    if has_next:
                        for n in banks_of(step):
                            bank_max(u + 1, n)
                        if step == BANKS // PER_STEP:
                            split_top(u + 1)
                        if step == BANKS // PER_STEP + 2:
                            keep_top(u + 1)
                    if step == 2 and has_prev:
                        normalise(u - 1, 1)
                    if step == KB + 2:
                        normalise(u, 0)
                if not has_next:
                    normalise(u, 1)

            dve.tensor_copy(identb[:, :], ident[:, :]).then_inc(identb_ready, 1)
            dve.sem_inc(s_read, DEPTH)
            dve.sem_inc(o_done, 1)
            for n in range(BANKS):
                bank_max(0, n)
            split_top(0)
            dve.wait_ge(rows_ready, 1)
            dve.tensor_copy(top_rows[:, :], miscb[0:3 * HG * QT, 0:P]).then_inc(rows_out, 1)
            units(dve, unit)


def attention_output(nc, a, X, heads, ident):
    QT = S // P
    with ExitStack() as ctx:
        m = Mem(nc, ctx)
        wo = m.sb("wo", [P, DT, D])
        hstage = m.sb("hstage", [P, DEPTH, NG, HG * HD])
        ht = m.sb("ht", [P, DEPTH, DT, P])
        warm = m.sb("warm_p2", [P, 1])
        tp = m.ps("tp_p2", [P, DEPTH, CH])
        po = m.ps("po", [P, DEPTH, CH])
        wo_landed, staged, turned, ht_ready = m.sem("wo_landed"), m.sem("hstaged"), m.sem("hturned"), m.sem("ht_ready")
        po_ready, added = m.sem("po_ready"), m.sem("added_p2")
        block = ctx.enter_context(nc.Block())

        @block.sync
        def _(sp):
            sp.dma_start(wo[:, :, :], a["wo0"].rearrange("(k p) f -> p k f", p=P)).then_inc(wo_landed, 16)

        @block.vector
        def _(dve):
            dve.sem_inc(added, DEPTH)
            with dve.Fori(0, B) as b:
                for t in range(QT + 1):
                    if t < QT:
                        dve.wait_ge(turned, b * QT + t + 1)
                        dve.tensor_copy(hstage[:, t % DEPTH, :, :], heads[:, ds(b * NG, NG), t, :]).then_inc(staged, 1)
                    if t:
                        dve.wait_ge(po_ready, b * QT + t)
                        x = X[:, ds(b * QT + t - 1, 1), :].rearrange("p o d -> p (o d)")
                        dve.tensor_tensor(x, po[:, (t - 1) % DEPTH, 0:D], x, ALU.add).then_inc(added, 1)

        @block.tensor
        def _(pe):
            pe.sem_inc(turned, DEPTH)
            pe.wait_ge(wo_landed, 16)
            with pe.Fori(0, B) as b:
                for t in range(QT + 1):
                    if t < QT:
                        pe.wait_ge(staged, b * QT + t + 1)
                        pe.wait_ge(ht_ready, b * QT + t + 1)
                        flat = hstage[:, t % DEPTH, :, :].rearrange("p g f -> p (g f)")
                        for k in range(DT):
                            mm = pe.transpose(tp[:, t % DEPTH, k * P:(k + 1) * P], flat[:, k * P:(k + 1) * P],
                                              ident[:, :])
                        mm.then_inc(turned, 1)
                    if t:
                        pe.wait_ge(ht_ready, b * QT + t + DEPTH)
                        pe.wait_ge(added, b * QT + t)
                        for k in range(DT):
                            mm = pe.matmul(po[:, (t - 1) % DEPTH, 0:D], ht[:, (t - 1) % DEPTH, k, :], wo[:, k, :],
                                           start=(k == 0), stop=(k == DT - 1))
                        mm.then_inc(po_ready, 1)

        @block.scalar
        def _(act):
            act.sem_inc(ht_ready, DEPTH)
            act.activation(warm[:, :], ident[:, 0:1], ACT.Identity)
            with act.Fori(0, B) as b:
                for t in range(QT):
                    act.wait_ge(turned, b * QT + t + 1 + DEPTH)
                    if t >= DEPTH:
                        act.wait_ge(po_ready, b * QT + t + 1 - DEPTH)
                    act.copy(ht[:, t % DEPTH, :, :], tp[:, t % DEPTH, 0:D].rearrange("p (k t) -> p k t", k=DT)
                             ).then_inc(ht_ready, 1)

def cross_weights(m, a):
    QK = 128
    wq = m.sb("wq_x", [P, DT, QK])
    wk = m.sb("wk_x", [P, DT, QK])
    wv = m.sb("wv_x", [P, DT, D])
    bq = m.sb("bq_x", [P, 1])
    bk = m.sb("bk_x", [P, 1])
    bv = m.sb("bv_x", [1, D])
    ct = m.sb("ct_x", [P, DT, B * CTX])
    loads = [(dst[:, :, :], a[src].rearrange("(k p) f -> p k f", p=P))
             for dst, src in ((wq, "wq_x"), (wk, "wk_x"), (wv, "wv_x"), (ct, "ctx_t"))]
    loads += [(dst[:, :], a[src]) for dst, src in ((bq, "bq_x"), (bk, "bk_x"), (bv, "bv_x"))]
    return (wq, wk, wv, bq, bk, bv, ct), loads


def sigmoid_cross(nc, a, weights, landed, LOADS, X, XT):
    SCALE = 1.0 / float(np.sqrt(a["wq_x"].shape[1] // 2))
    HALVES = S // CH
    with ExitStack() as ctx:
        m = Mem(nc, ctx)
        wq, wk, wv, bq, bk, bv, ct = weights
        ones = m.sb("ones_x", [1, CTX])
        kt = m.sb("kt_x", [P, B * CTX])
        kstage = m.sb("kstage_x", [P, CTX])
        v = m.sb("v_x", [CTX, B, D])
        qt = m.sb("qt_x", [P, DEPTH, CH])
        z = m.sb("z_x", [CTX, DEPTH, CH])
        warm = m.sb("warm_x", [P, 1])
        pk = m.ps("pk_x", [P, CH])
        pq = m.ps("pq_x", [P, CH])
        pz = m.ps("pz_x", [P, DEPTH, CH])
        po = m.ps("po_x", [P, 2, 2, D])
        ones_ready, pk_ready, pk_out = m.sem("ones_x"), m.sem("pk_ready_x"), m.sem("pk_out_x")
        k_staged, q_ready, q_out = m.sem("k_staged_x"), m.sem("q_ready_x"), m.sem("q_out_x")
        z_ready, z_out, o_ready, added = m.sem("z_ready_x"), m.sem("z_out_x"), m.sem("o_ready_x"), m.sem("added_x")
        block = ctx.enter_context(nc.Block())

        @block.tensor
        def _(pe):
            pe.wait_ge(landed, 16 * LOADS)
            pe.wait_ge(ones_ready, 1)
            for k in range(DT):
                mm = pe.matmul(pk[:, 0:B * CTX], wk[:, k, :], ct[:, k, :], start=(k == 0), stop=(k == DT - 1))
            mm.then_inc(pk_ready, 1)
            for b in range(B):
                dst = po[0:CTX, b // 2, b % 2, :]
                pe.matmul(dst, ones[:, :], bv[:, :], start=True, stop=False)
                for k in range(DT):
                    mm = pe.matmul(dst, ct[:, k, b * CTX:(b + 1) * CTX], wv[:, k, :], start=False, stop=(k == DT - 1))
            mm.then_inc(pk_ready, 1)
            pe.wait_ge(pk_out, 3)
            with pe.Fori(0, B) as b:
                for s in range(HALVES):
                    c = b * HALVES + s
                    pe.wait_ge(q_out, c + 1)
                    for k in range(DT):
                        mm = pe.matmul(pq[:, :], wq[:, k, :], XT[:, k, ds(c * CH, CH)], start=(k == 0), stop=(k == DT - 1))
                    mm.then_inc(q_ready, 1)
                    if s == 0:
                        pe.wait_ge(k_staged, b + 1)
                    pe.wait_ge(q_out, c + 2)
                    mm = pe.matmul(pz[0:CTX, s, :], kstage[:, :], qt[:, s, :], start=True, stop=True)
                    mm.then_inc(z_ready, 1)
                    pe.wait_ge(z_out, c + 1)
                    for t in range(TPC):
                        if t % 2 == 0:
                            pe.wait_ge(added, c * 2 + t // 2 + 1)
                        mm = pe.matmul(po[:, t // 2, t % 2, :], z[:, s, t * P:(t + 1) * P],
                                       v[:, ds(b, 1), :].rearrange("p o d -> p (o d)"), start=True, stop=True)
                        if t % 2 == 1:
                            mm.then_inc(o_ready, 1)

        @block.scalar
        def _(act):
            act.wait_ge(landed, 16 * LOADS)
            act.wait_ge(pk_ready, 1)
            act.activation(kt[:, :], pk[:, 0:B * CTX], ACT.Identity, bias=bk[:, 0:1]).then_inc(pk_out, 1)
            act.wait_ge(pk_ready, 2)
            act.copy(v[:, 0:2, :], po[0:CTX, 0, :, :]).then_inc(pk_out, 1)
            act.copy(v[:, 2:4, :], po[0:CTX, 1, :, :]).then_inc(pk_out, 1)
            act.activation(warm[:, :], ct[:, 0, 0:1], ACT.Sigmoid)
            with act.Fori(0, B) as b:
                for s in range(HALVES):
                    act.wait_ge(z_ready, b * HALVES + s + 1)
                    act.activation(z[:, s, :], pz[0:CTX, s, :], ACT.Sigmoid, scale=SCALE).then_inc(z_out, 1)

        @block.vector
        def _(dve):
            dve.memset(ones[:, :], 1.0).then_inc(ones_ready, 1)
            dve.sem_inc(q_out, 1)
            dve.sem_inc(added, 2)
            dve.wait_ge(pk_out, 3)
            with dve.Fori(0, B) as b:
                for s in range(HALVES):
                    c = b * HALVES + s
                    if s == 0:
                        dve.wait_ge(added, b * HALVES * 2 + 1)
                        dve.tensor_copy(kstage[:, :], kt[:, ds(b * CTX, CTX)]).then_inc(k_staged, 1)
                    dve.wait_ge(q_ready, c + 1)
                    dve.tensor_scalar(qt[:, s, :], pq[:, :], bq[:, 0:1], None, ALU.add).then_inc(q_out, 1)
                    for t in range(2):
                        dve.wait_ge(o_ready, c * 2 + t + 1)
                        x = X[:, ds(c * TPC + 2 * t, 2), :]
                        dve.tensor_tensor(x, po[:, t, :, :], x, ALU.add).then_inc(added, 1)


def mlp_weights(m, a):
    FT = FF // P
    wg = m.sb("wg", [P, DT, FF])
    wu = m.sb("wu", [P, DT, FF])
    wd = m.sb("wd", [P, FT, D])
    bg = m.sb("bg", [P, FT])
    bu = m.sb("bu", [P, FT])
    bd = m.sb("bd", [1, D])
    loads = [(dst[:, :, :], a[src].rearrange("(k p) f -> p k f", p=P)) for dst, src in ((wg, "wg"), (wu, "wu"), (wd, "wd"))]
    loads += [(dst[:, :], a[src]) for dst, src in ((bg, "bg"), (bu, "bu"), (bd, "bd"))]
    return (wg, wu, wd, bg, bu, bd), loads


def gated_mlp(nc, weights, landed, LOADS, X, XT):
    FT = FF // P
    with ExitStack() as ctx:
        m = Mem(nc, ctx)
        wg, wu, wd, bg, bu, bd = weights
        ones = m.sb("ones_m", [1, P])
        sg = m.sb("sg", [P, DEPTH, CH])
        h = m.sb("h_m", [P, DEPTH, FT, CH])
        warm = m.sb("warm_m", [P, 1])
        pg = m.ps("pg", [P, DEPTH, CH])
        pu = m.ps("pu", [P, DEPTH, CH])
        po = m.ps("po_m", [P, 2, 2, D])
        ones_ready = m.sem("ones_ready_m")
        g_ready, u_ready, sg_ready, h_ready = m.sem("g_ready"), m.sem("u_ready"), m.sem("sg_ready"), m.sem("h_ready_m")
        o_ready, added = m.sem("o_ready_m"), m.sem("added_m")
        block = ctx.enter_context(nc.Block())

        @block.tensor
        def _(pe):
            pe.wait_ge(landed, 16 * LOADS)
            pe.wait_ge(ones_ready, 1)
            with pe.Fori(0, NC // DEPTH) as j:
                for s in range(DEPTH):
                    c = j * DEPTH + s
                    for f in range(FT):
                        n = c * FT + f
                        pe.wait_ge(h_ready, n + 1)
                        for w, dst, done in ((wg, pg, g_ready), (wu, pu, u_ready)):
                            for k in range(DT):
                                mm = pe.matmul(dst[:, f % DEPTH, :], w[:, k, f * P:(f + 1) * P], XT[:, k, ds(c * CH, CH)],
                                               start=(k == 0), stop=(k == DT - 1))
                            mm.then_inc(done, 1)
                    pe.wait_ge(h_ready, (c + 1) * FT + DEPTH)
                    for t in range(TPC):
                        if t % 2 == 0:
                            pe.wait_ge(added, c * 2 + t // 2 + 1)
                        pe.matmul(po[:, t // 2, t % 2, :], ones[:, :], bd[:, :], start=True, stop=False)
                        for f in range(FT):
                            mm = pe.matmul(po[:, t // 2, t % 2, :], h[:, s, f, t * P:(t + 1) * P], wd[:, f, :],
                                           start=False, stop=(f == FT - 1))
                        if t % 2 == 1:
                            mm.then_inc(o_ready, 1)

        @block.scalar
        def _(act):
            act.wait_ge(landed, 16 * LOADS)
            act.activation(warm[:, :], bg[:, 0:1], ACT.Silu)
            with act.Fori(0, NC) as c:
                for f in range(FT):
                    n = c * FT + f
                    act.wait_ge(g_ready, n + 1)
                    act.wait_ge(h_ready, n + 1)
                    act.activation(sg[:, f % DEPTH, :], pg[:, f % DEPTH, :], ACT.Silu, bias=bg[:, f:f + 1]).then_inc(sg_ready, 1)

        @block.vector
        def _(dve):
            dve.memset(ones[:, :], 1.0).then_inc(ones_ready, 1)
            dve.sem_inc(h_ready, DEPTH)
            dve.sem_inc(added, 2)
            dve.wait_ge(landed, 16 * LOADS)
            with dve.Fori(0, NC // DEPTH) as j:
                for s in range(DEPTH):
                    c = j * DEPTH + s
                    for f in range(FT):
                        n = c * FT + f
                        dve.wait_ge(u_ready, n + 1)
                        dve.wait_ge(sg_ready, n + 1)
                        dve.scalar_tensor_tensor(h[:, s, f, :], pu[:, f % DEPTH, :], bu[:, f:f + 1], sg[:, f % DEPTH, :],
                                                 ALU.add, ALU.mult).then_inc(h_ready, 1)
                    for t in range(2):
                        dve.wait_ge(o_ready, c * 2 + t + 1)
                        x = X[:, ds(c * TPC + 2 * t, 2), :]
                        dve.tensor_tensor(x, po[:, t, :, :], x, ALU.add).then_inc(added, 1)


def peer_gates(nc, a, XT, sim, thr, shift):
    SIM = 2 * NH * NK
    with ExitStack() as ctx:
        m = Mem(nc, ctx)
        wq_t = m.sb("wq_t", [P, SIM // P, D])
        keys = m.sb("keys", [P, SIM // P, 2 * NK])
        wsim = m.sb("wsim", [P, DT, SIM])
        xs = m.sb("xs_g", [P, DEPTH, DT, P])
        best = m.sb("best", [P, DEPTH, 2 * NH, TOPK])
        sums = m.sb("sums", [P, DEPTH, NH, TOPK * TOPK])
        picked = m.sb("picked", [P, DEPTH, NH, TOPK])
        picks = m.sb("picks", [P, NT, NH, TOPK])
        z = m.sb("z_g", [P, NT, NH])
        logz = m.sb("logz", [P, NT, NH])
        pw = m.ps("pw_g", [P, DT, SIM])
        psim = m.ps("psim", [P, DEPTH, SIM])
        landed, pw_ready, w_ready = m.sem("landed_g"), m.sem("pw_ready_g"), m.sem("w_ready_g")
        xs_ready, sim_ready, sim_kept = m.sem("xs_ready_g"), m.sem("sim_ready"), m.sem("sim_kept")
        best_ready, sums_ready, passed = m.sem("best_ready"), m.sem("sums_ready"), m.sem("passed_g")
        picked_ready, picks_kept = m.sem("picked_ready"), m.sem("picks_kept")
        tail, exp_ready, log_ready = m.sem("tail_g"), m.sem("exp_ready_g"), m.sem("log_ready_g")
        block = ctx.enter_context(nc.Block())

        @block.sync
        def _(sp):
            sp.dma_start(wq_t[:, :, :], a["peer_wq_t"].rearrange("(k p) f -> p k f", p=P)).then_inc(landed, 16)
            sp.dma_start(keys[:, :, :], a["peer_keys"].rearrange("(k p) f -> p k f", p=P)).then_inc(landed, 16)

        @block.tensor
        def _(pe):
            pe.wait_ge(landed, 32)
            for k in range(DT):
                for g in range(SIM // P):
                    mm = pe.matmul(pw[:, k, g * P:(g + 1) * P], wq_t[:, g, k * P:(k + 1) * P], keys[:, g, :],
                                   start=True, stop=True)
            mm.then_inc(pw_ready, 1)
            pe.wait_ge(w_ready, 1)
            with pe.Fori(0, NT // DEPTH) as j:
                for s in range(DEPTH):
                    i = j * DEPTH + s
                    pe.wait_ge(xs_ready, i + 1)
                    pe.wait_ge(best_ready, i + 1)
                    pe.wait_ge(sim_kept, i + 1)
                    for k in range(DT):
                        mm = pe.matmul(psim[:, s, :], xs[:, s, k, :], wsim[:, k, :], start=(k == 0), stop=(k == DT - 1))
                    mm.then_inc(sim_ready, 1)

        @block.gpsimd
        def _(pool):
            with pool.Fori(0, NT // DEPTH) as j:
                for s in range(DEPTH):
                    i = j * DEPTH + s
                    pool.wait_ge(sim_kept, i + 1)
                    pool.tensor_copy(xs[:, s, :, :], XT[:, :, ds(i * P, P)]).then_inc(xs_ready, 1)

        @block.scalar
        def _(act):
            act.wait_ge(pw_ready, 1)
            act.copy(wsim[:, :, :], pw[:, :, :]).then_inc(w_ready, 1)
            act.sem_inc(sim_kept, DEPTH)
            with act.Fori(0, NT // DEPTH) as j:
                for s in range(DEPTH):
                    i = j * DEPTH + s
                    act.wait_ge(best_ready, i + 1 + DEPTH)
                    act.copy(sim[:, ds(i, 1), :], psim[:, s, :].unsqueeze(1)).then_inc(sim_kept, 1)
            act.wait_ge(tail, 1)
            act.activation(picks[:, :, :, :], picks[:, :, :, :], ACT.Exp).then_inc(exp_ready, 1)
            act.wait_ge(tail, 2)
            act.activation(logz[:, :, :], z[:, :, :], ACT.Ln).then_inc(log_ready, 1)

        @block.vector
        def _(dve):
            dve.sem_inc(best_ready, DEPTH)
            with dve.Fori(0, NT // DEPTH) as j:
                for s in range(DEPTH):
                    i = j * DEPTH + s
                    dve.wait_ge(sim_ready, i + 1)
                    dve.sem_inc(passed, 1)
                    for g in range(2 * NH):
                        last = dve.max(best[:, s, g, :], psim[:, s, g * NK:(g + 1) * NK])
                    last.then_inc(best_ready, 1)
                    dve.wait_ge(best_ready, i + 1 + DEPTH)
                    for h in range(NH):
                        last = dve.tensor_tensor(
                            sums[:, s, h, :].rearrange("p (x y) -> p x y", x=TOPK),
                            best[:, s, h, :].unsqueeze(2).to_broadcast([P, TOPK, TOPK]),
                            best[:, s, NH + h, :].unsqueeze(1).to_broadcast([P, TOPK, TOPK]), ALU.add)
                    last.then_inc(sums_ready, 1)
                    dve.wait_ge(sums_ready, i + 1)
                    dve.sem_inc(passed, 1)
                    for h in range(NH):
                        last = dve.max(picked[:, s, h, :], sums[:, s, h, :])
                    last.then_inc(picked_ready, 1)
                    dve.wait_ge(picked_ready, i + 1)
                    dve.tensor_copy(picks[:, ds(i, 1), :, :].rearrange("p o h k -> p (o h k)"),
                                    picked[:, s, :, :].rearrange("p h k -> p (h k)")).then_inc(picks_kept, 1)
            dve.wait_ge(picks_kept, NT)
            dve.tensor_copy(thr[:, :, :], picks[:, :, :, TOPK - 1])
            dve.tensor_copy(shift[:, :, :], picks[:, :, :, 0]).then_inc(picks_kept, 1)
            dve.wait_ge(picks_kept, NT + 1)
            p3 = picks[:, :, :, :].rearrange("p t h k -> p (t h) k")
            dve.tensor_tensor(p3, p3, shift[:, :, :].rearrange("p t h -> p (t h)").unsqueeze(2).to_broadcast([P, NT * NH, TOPK]),
                              ALU.subtract).then_inc(tail, 1)
            dve.wait_ge(exp_ready, 1)
            dve.tensor_reduce(z[:, :, :].rearrange("p t h -> p (t h)"), p3, AX.X, ALU.add).then_inc(tail, 1)
            dve.wait_ge(log_ready, 1)
            dve.scalar_tensor_tensor(shift[:, :, :], shift[:, :, :], -1.0, logz[:, :, :], ALU.mult, ALU.subtract)


def peer_experts(nc, a, X, XT, sim, thr, shift, ident):
    ET = FF // P
    with ExitStack() as ctx:
        m = Mem(nc, ctx)
        down = m.sb("down_t", [P, DT, FF])
        up = m.sb("up", [P, ET, D])
        both = m.sb("both", [P, DEPTH, FF])
        expd = m.sb("expd", [P, DEPTH, FF])
        gate = m.sb("gate", [P, DEPTH, FF])
        gates = m.sb("gates", [P, DEPTH, FF])
        taken = m.sb("taken", [P, DEPTH])
        rest = m.sb("rest_e", [P, DEPTH])
        act_t = m.sb("act_t", [P, DEPTH, ET, P])
        weighted = m.sb("weighted", [P, ET, P])
        warm = m.sb("warm_e", [P, 1])
        pg = m.ps("pgt", [P, ET, P])
        pw = m.ps("pw_e", [P, ET, P])
        po = m.ps("po_e", [P, DEPTH, CH])
        landed, both_ready, exp_ready = m.sem("landed_e"), m.sem("both_ready"), m.sem("exp_ready_e")
        gate_ready, steps = m.sem("gate_ready"), m.sem("gate_steps")
        gates_ready, turned, w_ready = m.sem("gates_ready"), m.sem("gates_turned"), m.sem("w_ready_e")
        act_ready, weighted_ready = m.sem("act_ready"), m.sem("weighted_ready")
        o_ready, added = m.sem("o_ready_e"), m.sem("added_e")
        STEPS = NH - 1 + 1
        block = ctx.enter_context(nc.Block())

        @block.sync
        def _(sp):
            sp.dma_start(down[:, :, :], a["down_t"].rearrange("(k p) f -> p k f", p=P)).then_inc(landed, 16)
            sp.dma_start(up[:, :, :], a["up"].rearrange("(k p) f -> p k f", p=P)).then_inc(landed, 16)

        @block.gpsimd
        def _(pool):
            with pool.Fori(0, NT) as i:
                for h in range(NH):
                    n = i * NH + h
                    pool.wait_ge(gate_ready, n + 1)
                    xk = sim[:, ds(i, 1), h * NK:h * NK + NX].rearrange("p o k -> p (o k)")
                    yk = sim[:, ds(i, 1), (NH + h) * NK:(NH + h + 1) * NK].rearrange("p o k -> p (o k)")
                    pool.tensor_tensor(both[:, h % DEPTH, :].rearrange("p (x y) -> p x y", x=NX),
                                       xk.unsqueeze(2).to_broadcast([P, NX, NK]),
                                       yk.unsqueeze(1).to_broadcast([P, NX, NK]), ALU.add).then_inc(both_ready, 1)

        @block.scalar
        def _(act):
            act.wait_ge(landed, 32)
            act.activation(warm[:, :], down[:, 0, 0:1], ACT.Exp)
            act.sem_inc(act_ready, 1)
            with act.Fori(0, NT // DEPTH) as j:
                for s in range(DEPTH):
                    i = j * DEPTH + s
                    for h in range(NH):
                        n = i * NH + h
                        act.wait_ge(both_ready, n + 1)
                        act.wait_ge(gate_ready, n + 1)
                        act.activation(expd[:, h % DEPTH, :], both[:, h % DEPTH, :], ACT.Exp,
                                       bias=shift[:, ds(i, 1), h]).then_inc(exp_ready, 1)
                    act.wait_ge(w_ready, i + 1)
                    act.wait_ge(weighted_ready, i + 1)
                    act.activation(act_t[:, s, :, :], pw[:, :, :], ACT.Silu).then_inc(act_ready, 1)

        @block.vector
        def _(dve):
            def open_gates(i, s):
                chain = Chain(dve, steps, i * STEPS)
                for h in range(NH):
                    n = i * NH + h
                    dve.wait_ge(exp_ready, n + 1)
                    if h == 0:
                        dve.wait_ge(turned, i + 1)
                    dve.scalar_tensor_tensor(gates[:, s, :] if h == 0 else gate[:, h % DEPTH, :], both[:, h % DEPTH, :],
                                             thr[:, ds(i, 1), h], expd[:, h % DEPTH, :],
                                             ALU.is_ge, ALU.mult).then_inc(gate_ready, 1)
                    dve.wait_ge(gate_ready, n + 1 + DEPTH)
                    if h:
                        chain.link(dve.scalar_tensor_tensor(gates[:, s, :], gates[:, s, :], 1.0, gate[:, h % DEPTH, :],
                                                            ALU.mult, ALU.add,
                                                            accum_out=taken[:, s:s + 1] if h == NH - 1 else None))
                chain.link(dve.tensor_scalar(rest[:, s:s + 1], taken[:, s:s + 1], -1.0, float(NH), ALU.mult, ALU.add))
                dve.tensor_tensor(gates[:, s, FF - 1:FF], gates[:, s, FF - 1:FF], rest[:, s:s + 1],
                                  ALU.add).then_inc(gates_ready, 1)

            def weigh(i, s):
                dve.wait_ge(turned, i + 1 + DEPTH)
                dve.wait_ge(act_ready, i + 2)
                dve.wait_ge(o_ready, i + 1)
                dve.tensor_tensor(weighted[:, :, :], pg[:, :, :], act_t[:, s, :, :], ALU.mult).then_inc(weighted_ready, 1)

            def add(i, s):
                dve.wait_ge(o_ready, i + 2)
                x = X[:, ds(i, 1), :].rearrange("p o d -> p (o d)")
                dve.tensor_tensor(x, po[:, s, 0:D], x, ALU.add).then_inc(added, 1)

            dve.sem_inc(gate_ready, DEPTH)
            dve.sem_inc(weighted_ready, DEPTH)
            dve.sem_inc(added, DEPTH)
            open_gates(0, 0)
            weigh(0, 0)
            open_gates(1, 1)
            with dve.Fori(0, NT // DEPTH - 1) as j:
                for s in range(DEPTH):
                    i = j * DEPTH + s
                    weigh(i + 1, 1 - s)
                    add(i, s)
                    open_gates(i + 2, s)
            weigh(NT - 1, 1)
            add(NT - 2, 0)
            add(NT - 1, 1)

        @block.tensor
        def _(pe):
            def project(i):
                pe.wait_ge(act_ready, i + 1)
                for e in range(ET):
                    for k in range(DT):
                        mm = pe.matmul(pw[:, e, :], down[:, k, e * P:(e + 1) * P], XT[:, k, ds(i * P, P)],
                                       start=(k == 0), stop=(k == DT - 1))
                mm.then_inc(w_ready, 1)

            def turn(i, s):
                pe.wait_ge(gates_ready, i + 1)
                pe.wait_ge(weighted_ready, i + DEPTH)
                for e in range(ET):
                    mm = pe.transpose(pg[:, e, :], gates[:, s, e * P:(e + 1) * P], ident[:, :])
                mm.then_inc(turned, 1)

            def combine(i, s):
                pe.wait_ge(weighted_ready, i + 1 + DEPTH)
                pe.wait_ge(added, i + 1)
                for e in range(ET):
                    mm = pe.matmul(po[:, s, 0:D], weighted[:, e, :], up[:, e, :], start=(e == 0), stop=(e == ET - 1))
                mm.then_inc(o_ready, 1)

            pe.sem_inc(turned, DEPTH)
            pe.sem_inc(o_ready, 1)
            pe.wait_ge(landed, 32)
            project(0)
            turn(0, 0)
            with pe.Fori(0, NT // DEPTH - 1) as j:
                for s in range(DEPTH):
                    i = j * DEPTH + s
                    project(i + 1)
                    combine(i, s)
                    turn(i + 1, 1 - s)
            project(NT - 1)
            combine(NT - 2, 0)
            turn(NT - 1, 1)
            combine(NT - 1, 1)


def key_products(nc, a, XT, grams, vsum):
    QT = S // P
    with ExitStack() as ctx:
        m = Mem(nc, ctx)
        wkv = m.sb("wkv", [P, DT, 2 * D])
        mask = m.sb("mask", [P, P])
        ones = m.sb("ones_k", [P, 1])
        nb = m.sb("nb", [P, DT])
        xs = m.sb("xs_k", [P, DEPTH, DT, P])
        kv = m.sb("kv", [P, DEPTH, 2 * D])
        warm = m.sb("warm_k", [P, 1])
        pkv = m.ps("pkv", [P, DEPTH, 2 * D])
        pg = m.ps("pgram", [P, DT, 2 * D])
        pv = m.ps("pvsum", [P, DT, CH])
        landed, ones_ready = m.sem("landed_k"), m.sem("ones_ready_k")
        xs_ready, kv_ready, kv_out = m.sem("xs_ready_k"), m.sem("kv_ready"), m.sem("kv_out")
        gram_ready, gram_kept = m.sem("gram_ready"), m.sem("gram_kept")
        block = ctx.enter_context(nc.Block())

        @block.sync
        def _(sp):
            sp.dma_start(wkv[:, :, :], a["wkv1"].rearrange("(k p) f -> p k f", p=P)).then_inc(landed, 16)
            sp.dma_start(mask[:, :], a["mask"]).then_inc(landed, 16)
            sp.dma_start(nb[:, :], a["norm_b"]).then_inc(landed, 16)

        @block.scalar
        def _(act):
            act.wait_ge(landed, 48)
            act.sem_inc(kv_out, DEPTH)
            act.activation(warm[:, :], mask[:, 0:1], ACT.Identity)
            with act.Fori(0, B) as b:
                for t in range(QT):
                    act.wait_ge(kv_ready, b * QT + t + 1)
                    act.copy(kv[:, t % DEPTH, :], pkv[:, t % DEPTH, :]).then_inc(kv_out, 1)

        @block.tensor
        def _(pe):
            pe.wait_ge(landed, 48)
            pe.wait_ge(ones_ready, 1)
            with pe.Fori(0, B) as b:
                pe.wait_ge(gram_kept, b + 1)
                for t in range(QT + 1):
                    if t < QT:
                        pe.wait_ge(xs_ready, b * QT + t + 1)
                        pe.wait_ge(kv_out, b * QT + t + 1)
                        for k in range(DT):
                            mm = pe.matmul(pkv[:, t % DEPTH, :], xs[:, t % DEPTH, k, :], wkv[:, k, :],
                                           start=(k == 0), stop=(k == DT - 1))
                        mm.then_inc(kv_ready, 1)
                    if t:
                        u = t - 1
                        pe.wait_ge(kv_out, b * QT + u + 1 + DEPTH)
                        tile = kv[:, u % DEPTH, :].rearrange("p (o k f) -> p o k f", o=2, k=DT)
                        for k in range(DT):
                            pe.matmul(pg[:, k, 0:2 * P], tile[:, 0, k, :], tile[:, :, k, :],
                                      start=(u == 0), stop=(u == QT - 1))
                            mm = pe.matmul(pv[:, k, 0:1], tile[:, 1, k, :], ones[:, :],
                                           start=(u == 0), stop=(u == QT - 1))
                mm.then_inc(gram_ready, 1)

        @block.vector
        def _(dve):
            dve.memset(ones[:, :], 1.0).then_inc(ones_ready, 1)
            dve.sem_inc(gram_kept, 1)
            dve.wait_ge(landed, 48)
            with dve.Fori(0, B) as b:
                for t in range(QT):
                    dve.wait_ge(kv_ready, b * QT + t) if t else dve.wait_ge(gram_kept, b + 1)
                    dve.tensor_copy(xs[:, t % DEPTH, :, :], XT[:, :, ds(b * S + t * P, P)]).then_inc(xs_ready, 1)
                dve.wait_ge(gram_ready, b + 1)
                for k in range(DT):
                    dve.tensor_tensor(grams[:, ds(b * DT + k, 1), :, :].rearrange("p o g f -> p (o g) f"),
                                      pg[:, k, 0:2 * P].rearrange("p (g f) -> p g f", g=2),
                                      mask[:, :].unsqueeze(1).to_broadcast([P, 2, P]), ALU.mult)
                    last = dve.tensor_scalar(vsum[:, ds(b * DT + k, 1)], pv[:, k, 0:1], nb[:, k:k + 1], None, ALU.mult)
                last.then_inc(gram_kept, 1)


def normed_attention(nc, a, X, XT, grams, vsum):
    EPS = 1e-12
    HALVES = S // CH
    with ExitStack() as ctx:
        m = Mem(nc, ctx)
        wq = m.sb("wq1", [P, DT, D])
        wo = m.sb("wo1", [P, DT, D])
        bo = m.sb("bo1", [1, D])
        ng = m.sb("ng", [P, DT])
        mask = m.sb("mask_n", [P, P])
        ones = m.sb("ones_n", [1, P])
        gm = m.sb("gm", [P, DT, 2, P])
        vb = m.sb("vb", [P, DT])
        qt = m.sb("qt1", [P, DT, CH])
        prod = m.sb("prod", [P, DT, CH])
        norm = m.sb("norm1", [P, DT, CH])
        floor = m.sb("floor1", [P, DT, CH])
        inv = m.sb("inv1", [P, DT, CH])
        scaled = m.sb("scaled1", [P, DT, CH])
        o = m.sb("o1", [P, DT, CH])
        warm = m.sb("warm_n", [P, 1])
        pq = m.ps("pq1", [P, DT, CH])
        pn = m.ps("pn1", [P, DT, CH])
        pm = m.ps("pm1", [P, DT, CH])
        py = m.ps("py1", [P, 2, 2, D])
        landed, ones_ready, gm_ready = m.sem("landed_n"), m.sem("ones_ready_n"), m.sem("gm_ready")
        q_ready, q_out, g_ready, prod_ready = m.sem("q_ready_n"), m.sem("q_out_n"), m.sem("g_ready_n"), m.sem("prod_ready")
        n_ready, norm_ready, m_ready = m.sem("n_ready"), m.sem("norm_ready"), m.sem("m_ready")
        inv_steps, scaled_ready, o_ready = m.sem("inv_steps"), m.sem("scaled_ready"), m.sem("o_ready_n")
        y_ready, added = m.sem("y_ready_n"), m.sem("added_n")
        block = ctx.enter_context(nc.Block())

        def chunks(eng, chunk):
            with eng.Fori(0, B - 1) as b:
                for s in range(HALVES):
                    chunk(b, s, True)
            for s in range(HALVES):
                chunk(B - 1, s, s < HALVES - 1)

        @block.sync
        def _(sp):
            sp.dma_start(wq[:, :, :], a["wq1"].rearrange("(k p) f -> p k f", p=P)).then_inc(landed, 16)
            sp.dma_start(wo[:, :, :], a["wo1"].rearrange("(k p) f -> p k f", p=P)).then_inc(landed, 16)
            for dst, src in ((bo, "bo1"), (ng, "norm_g"), (mask, "mask")):
                sp.dma_start(dst[:, :], a[src]).then_inc(landed, 16)

        @block.tensor
        def _(pe):
            pe.sem_inc(y_ready, 2)
            pe.wait_ge(landed, 80)
            pe.wait_ge(ones_ready, 1)

            def project(c):
                for k in range(DT):
                    for kk in range(DT):
                        mm = pe.matmul(pq[:, k, :], wq[:, kk, k * P:(k + 1) * P], XT[:, kk, ds(c * CH, CH)],
                                       start=(kk == 0), stop=(kk == DT - 1))
                    mm.then_inc(q_ready, 1)

            def chunk(b, s, more):
                c = b * HALVES + s
                if s == 0:
                    pe.wait_ge(gm_ready, b + 1)
                for k in range(DT):
                    n = c * DT + k
                    pe.wait_ge(q_out, n + 1)
                    pe.wait_ge(scaled_ready, n + 1)
                    pe.matmul(pm[:, k, :], gm[:, k, 0, :], qt[:, k, :], start=True, stop=True).then_inc(g_ready, 1)
                for k in range(DT):
                    n = c * DT + k
                    pe.wait_ge(prod_ready, n + 1)
                    pe.matmul(pn[:, k, :], mask[:, :], prod[:, k, :], start=True, stop=True).then_inc(n_ready, 1)
                    pe.matmul(pm[:, k, :], gm[:, k, 1, :], qt[:, k, :], start=True, stop=True).then_inc(m_ready, 1)
                if more:
                    project(c + 1)
                pe.wait_ge(o_ready, (c + 1) * DT)
                for t in range(TPC):
                    if t % 2 == 0:
                        pe.wait_ge(added, c * 2 + t // 2 + 1)
                    dst = py[:, t // 2, t % 2, :]
                    pe.matmul(dst, ones[:, :], bo[:, :], start=True, stop=False)
                    for k in range(DT):
                        mm = pe.matmul(dst, o[:, k, t * P:(t + 1) * P], wo[:, k, :], start=False, stop=(k == DT - 1))
                    if t % 2 == 1:
                        mm.then_inc(y_ready, 1)

            project(0)
            chunks(pe, chunk)

        @block.scalar
        def _(act):
            act.wait_ge(landed, 80)
            act.activation(warm[:, :], ng[:, 0:1], ACT.Sqrt)

            def keep_q(c, k):
                act.wait_ge(q_ready, c * DT + k + 1)
                act.copy(qt[:, k, :], pq[:, k, :]).then_inc(q_out, 1)

            def chunk(b, s, more):
                c = b * HALVES + s
                for k in range(DT):
                    n = c * DT + k
                    act.wait_ge(n_ready, n + 1)
                    act.wait_ge(scaled_ready, n + 1)
                    act.activation(norm[:, k, :], pn[:, k, :], ACT.Sqrt).then_inc(norm_ready, 1)
                if more:
                    for k in range(DT):
                        act.wait_ge(m_ready, c * DT + k + 1)
                        keep_q(c + 1, k)
                for k in range(DT):
                    n = c * DT + k
                    act.wait_ge(scaled_ready, n + 1 + DT)
                    act.wait_ge(y_ready, c * 2 + 2)
                    act.activation(o[:, k, :], scaled[:, k, :], ACT.Identity,
                                   bias=vb[:, k:k + 1]).then_inc(o_ready, 1)

            for k in range(DT):
                keep_q(0, k)
            chunks(act, chunk)

        @block.vector
        def _(dve):
            dve.memset(ones[:, :], 1.0).then_inc(ones_ready, 1)
            dve.sem_inc(scaled_ready, DT)
            dve.sem_inc(added, 2)
            dve.wait_ge(landed, 80)

            def sequence(b):
                dve.tensor_copy(vb[:, :], vsum[:, ds(b * DT, DT)])
                dve.tensor_copy(gm[:, :, :, :], grams[:, ds(b * DT, DT), :, :]).then_inc(gm_ready, 1)

            def multiply(c):
                for k in range(DT):
                    dve.wait_ge(g_ready, c * DT + k + 1)
                    dve.tensor_tensor(prod[:, k, :], pm[:, k, :], qt[:, k, :], ALU.mult).then_inc(prod_ready, 1)

            def chunk(b, s, more):
                c = b * HALVES + s
                for k in range(DT):
                    n = c * DT + k
                    dve.wait_ge(norm_ready, n + 1)
                    dve.tensor_scalar(floor[:, k, :], norm[:, k, :], EPS, None, ALU.max).then_inc(inv_steps, 1)
                    dve.wait_ge(inv_steps, n * 2 + 1)
                    dve.reciprocal(inv[:, k, :], floor[:, k, :]).then_inc(inv_steps, 1)
                    dve.wait_ge(inv_steps, n * 2 + 2)
                    dve.wait_ge(m_ready, n + 1)
                    dve.scalar_tensor_tensor(scaled[:, k, :], pm[:, k, :], ng[:, k:k + 1], inv[:, k, :],
                                             ALU.mult, ALU.mult).then_inc(scaled_ready, 1)
                if more:
                    if s == HALVES - 1:
                        dve.wait_ge(o_ready, (c + 1) * DT)
                        sequence(b + 1)
                    multiply(c + 1)
                for t in range(2):
                    dve.wait_ge(y_ready, c * 2 + t + 1 + 2)
                    x = X[:, ds(c * TPC + 2 * t, 2), :]
                    dve.tensor_tensor(x, py[:, t, :, :], x, ALU.add).then_inc(added, 1)

            sequence(0)
            multiply(0)
            chunks(dve, chunk)


def circular_filter(nc, a, X, Z):
    PAIRS_ = KB // 2
    with ExitStack() as ctx:
        m = Mem(nc, ctx)
        fwd = m.sb("fwd", [P, 4, P])
        fw = m.sb("fw", [P, 3, P])
        inv = m.sb("inv_f", [P, 2, P])
        taps = m.sb("taps", [P, D])
        ct = m.sb("ct_f", [P, DT, B, CTX])
        kpw = m.sb("kpw", [P, DT, D])
        kpb = m.sb("kpb", [1, D])
        ones = m.sb("ones_f", [1, P])
        csum = m.sb("csum", [P, DT, B])
        cmean = m.sb("cmean", [P, DT, B, P])
        kmod = m.sb("kmod", [P, B, D])
        spec = m.sb("spec", [P, 3, B, D])
        part = m.sb("part_f", [P, DEPTH, 4, 2, D])
        yf = m.sb("yf", [P, DEPTH, 2, 2, D])
        px = m.ps("px_f", [P, DEPTH, 2, 2, D])
        py = m.ps("py_f", [P, DEPTH, 2, D])
        pk = m.ps("pk_f", [P, 2, 2, D])
        landed, ones_ready, steps = m.sem("landed_f"), m.sem("ones_ready_f"), m.sem("steps_f")
        mean_ready, k_ready, k_out, w_ready, spec_ready = (m.sem("mean_ready"), m.sem("k_ready_f"), m.sem("k_out_f"),
                                                           m.sem("w_ready_f"), m.sem("spec_ready"))
        x_ready, part_ready, yf_ready = m.sem("x_ready_f"), m.sem("part_ready"), m.sem("yf_ready")
        y_ready, z_ready = m.sem("y_ready_f"), m.sem("z_ready_f")
        block = ctx.enter_context(nc.Block())

        @block.sync
        def _(sp):
            for dst, src in ((fwd, "dft_fwd"), (fw, "dft_taps"), (inv, "dft_inv")):
                sp.dma_start(dst[:, :, :], a[src].rearrange("m p f -> p m f")).then_inc(landed, 16)
            sp.dma_start(ct[:, :, :, :].rearrange("p k b c -> p k (b c)"),
                         a["ctx_t"].rearrange("(k p) f -> p k f", p=P)).then_inc(landed, 16)
            sp.dma_start(kpw[:, :, :], a["kp_w_t"].rearrange("(k p) f -> p k f", p=P)).then_inc(landed, 16)
            sp.dma_start(taps[:, :], a["taps_t"]).then_inc(landed, 16)
            sp.dma_start(kpb[:, :], a["kp_b"]).then_inc(landed, 16)

        @block.tensor
        def _(pe):
            pe.wait_ge(landed, 16 * 7)
            pe.wait_ge(ones_ready, 1)
            pe.wait_ge(mean_ready, 1)
            for b in range(B):
                dst = pk[:, b // 2, b % 2, :]
                pe.matmul(dst, ones[:, :], kpb[:, :], start=True, stop=False)
                for k in range(DT):
                    mm = pe.matmul(dst, cmean[:, k, b, :], kpw[:, k, :], start=False, stop=(k == DT - 1))
            mm.then_inc(k_ready, 1)
            pe.wait_ge(k_out, 1)
            for w in range(3):
                mm = pe.matmul(pk[:, w // 2, w % 2, :], fw[:, w, :], taps[:, :], start=True, stop=True)
            mm.then_inc(w_ready, 1)
            with pe.Fori(0, B) as b:
                for q in range(PAIRS_ + 1):
                    if q < PAIRS_:
                        n = b * PAIRS_ + q
                        pe.wait_ge(part_ready, n + 1)
                        for o in range(2):
                            dst = px[:, q % DEPTH, o, :, :]
                            pe.matmul(dst, fwd[:, 2 * o + 1, :], X[:, ds(b * KB + 2 * q, 2), :],
                                      start=True, stop=False, skip_group_check=True)
                            if q:
                                mm = pe.matmul(dst, fwd[:, 2 * o, :], X[:, ds(b * KB + 2 * q - 1, 2), :],
                                               start=False, stop=True, skip_group_check=True)
                            else:
                                pe.matmul(dst[:, 0, :], fwd[:, 2 * o, :],
                                          X[:, ds(b * KB + KB - 1, 1), :].rearrange("p o d -> p (o d)"),
                                          start=False, stop=False, skip_group_check=True)
                                mm = pe.matmul(dst[:, 1, :], fwd[:, 2 * o, :],
                                               X[:, ds(b * KB, 1), :].rearrange("p o d -> p (o d)"),
                                               start=False, stop=True, skip_group_check=True)
                        mm.then_inc(x_ready, 1)
                    if q:
                        n = b * PAIRS_ + q - 1
                        s = (q - 1) % DEPTH
                        pe.wait_ge(yf_ready, n + 1 + DEPTH)
                        pe.wait_ge(z_ready, n + 1)
                        for o in range(2):
                            mm = pe.matmul(py[:, s, :, :], inv[:, o, :], yf[:, s, o, :, :], start=(o == 0), stop=(o == 1))
                        mm.then_inc(y_ready, 1)

        @block.scalar
        def _(act):
            act.wait_ge(k_ready, 1)
            act.copy(kmod[:, :, :].rearrange("p b d -> p (b d)"), pk[:, :, :, :].rearrange("p a c d -> p (a c d)")
                     ).then_inc(k_out, 1)

        @block.vector
        def _(dve):
            chain = Chain(dve, steps)
            dve.memset(ones[:, :], 1.0).then_inc(ones_ready, 1)
            dve.sem_inc(part_ready, DEPTH)
            dve.sem_inc(z_ready, DEPTH)
            dve.wait_ge(landed, 16 * 7)
            chain.link(dve.tensor_reduce(csum[:, :, :], ct[:, :, :, :], AX.X, ALU.add))
            chain.link(dve.tensor_scalar(csum[:, :, :], csum[:, :, :], 1.0 / CTX, None, ALU.mult))
            dve.tensor_copy(cmean[:, :, :, :], csum[:, :, :].unsqueeze(3).to_broadcast([P, DT, B, P])
                            ).then_inc(mean_ready, 1)
            dve.wait_ge(w_ready, 1)
            for w in range(3):
                for b in range(B):
                    last = dve.tensor_tensor(spec[:, w, b, :], pk[:, w // 2, w % 2, :], kmod[:, b, :], ALU.mult)
            last.then_inc(spec_ready, 1)
            dve.wait_ge(spec_ready, 1)
            with dve.Fori(0, B) as b:
                for q in range(PAIRS_ + 1):
                    if q < PAIRS_:
                        n = b * PAIRS_ + q
                        s = q % DEPTH
                        dve.wait_ge(x_ready, n + 1)
                        dve.wait_ge(yf_ready, n + 1)
                        for i, (o, w) in enumerate(((0, 0), (1, 1), (0, 1), (1, 2))):
                            last = dve.tensor_tensor(
                                part[:, s, i, :, :], px[:, s, o, :, :],
                                spec[:, w, ds(b, 1), :].to_broadcast([P, 2, D]), ALU.mult)
                        last.then_inc(part_ready, 1)
                    if q:
                        n = b * PAIRS_ + q - 1
                        dve.wait_ge(y_ready, n + 1)
                        blocks = ds(b * KB + 2 * (q - 1), 2)
                        dve.tensor_tensor(Z[:, blocks, :], py[:, (q - 1) % DEPTH, :, :], X[:, blocks, :],
                                          ALU.add).then_inc(z_ready, 1)

        @block.gpsimd
        def _(pool):
            pool.sem_inc(yf_ready, DEPTH)
            with pool.Fori(0, B) as b:
                for q in range(PAIRS_):
                    n = b * PAIRS_ + q
                    s = q % DEPTH
                    pool.wait_ge(part_ready, n + 1 + DEPTH)
                    if q >= DEPTH:
                        pool.wait_ge(y_ready, n + 1 - DEPTH)
                    pool.tensor_tensor(yf[:, s, 0, :, :], part[:, s, 0, :, :], part[:, s, 1, :, :], ALU.subtract)
                    pool.tensor_tensor(yf[:, s, 1, :, :], part[:, s, 2, :, :], part[:, s, 3, :, :],
                                       ALU.add).then_inc(yf_ready, 1)


def kronecker_weights(m, a):
    W1, W2 = 32, 64
    bu = m.sb("bu_t", [P, E * W2])
    au = m.sb("au_t", [P, E * W2])
    bad = m.sb("bad_t", [P, E * 2 * W1])
    ru = m.sb("ru", [P, 4 * DT, E])
    rd = m.sb("rd", [P, W2 // 2, E])
    bias_u = m.sb("bias_u", [W2, W2])
    bias_d = m.sb("bias_d", [W1, W1])
    scale_u = m.sb("scale_u", [W2, 1])
    scale_d = m.sb("scale_d", [W1, 1])
    loads = [(bu[0:W1, :], a["b_up"]), (au[0:W1, :], a["a_up"]), (bad[0:W2, :], a["ba_down"]),
             (ru[:, :, :], a["route_up"].rearrange("(k p) e -> p k e", p=P)), (rd[:, :, :], a["route_down"]),
             (bias_u[:, :], a["bias_up"]), (bias_d[:, :], a["bias_down"]),
             (scale_u[:, :], a["scale_up"].to_broadcast([W2, 1])), (scale_d[:, :], a["scale_down"].to_broadcast([W1, 1]))]
    return (bu, au, bad, ru, rd, bias_u, bias_d, scale_u, scale_d), loads, [t[:, :] for t in (bu, au, bad)]


def kronecker_experts(nc, weights, landed, LOADS, X, XT, spare, ident):
    R = P
    G = 8
    GB = 8
    W1, W2 = 32, 64
    PASSES = R // (G * GB)
    GROUPS = R // G
    K2 = 2
    LAYERS = 2
    FB = D // W1
    TOK = 4
    with ExitStack() as ctx:
        m = Mem(nc, ctx)
        bu, au, bad, ru, rd, bias_u, bias_d, scale_u, scale_d = weights
        ones = m.sb("ones_s", [P, P])
        xs = m.sb("xs_s", [P, DT, CH])
        xn = m.sb("xn", [W1, R, W1])
        h = spare[:, :, :].rearrange("p t d -> p (t d)")[:, 0:R * W2 // 2].rearrange("p (r o) -> p r o", o=W2 // 2)
        y = spare[0:W1, :, :].rearrange("p t d -> p (t d)")[:, R * W2 // 2:].rearrange("p (r o) -> p r o", o=W1)
        scores = m.sb("scores_s", [E, R])
        best = m.sb("best_s", [P, LAYERS, 8])
        place = m.sb("place_s", [P, LAYERS, 8], U32)
        start_f = m.sb("start_f", [P, LAYERS, K2])
        start_i = m.sb("start_i", [P, LAYERS, K2], I32)
        starts = m.sb("starts", [1, LAYERS, R, K2], I32)
        gap = m.sb("gap", [P, LAYERS, K2])
        gate = m.sb("gate_s", [P, LAYERS, K2])
        spread = m.sb("spread", [P, LAYERS, K2, R])
        gates = m.sb("gates_s", [P, LAYERS, K2, R])
        stage = m.sb("stage_s", [P, DEPTH, G, W2])
        mid = m.sb("mid_s", [P, DEPTH, G, K2, W2])
        pre = m.sb("pre_s", [W2, DEPTH, G, W2])
        warm = m.sb("warm_s", [P, 1])
        p_route = m.ps("p_route", [P, LAYERS, CH])
        p_mid = m.ps("p_mid", [P, DEPTH, G * K2 * W2])
        p_out = m.ps("p_out", [P, DEPTH, G * W2])
        p_turn = p_out
        zeroed = m.sem("zeroed_s")
        xs_ready, xn_ready = m.sem("xs_ready_s"), m.sem("xn_ready_s")
        route_ready, route_steps, starts_made, starts_landed = (m.sem("route_ready"), m.sem("route_steps"),
                                                                m.sem("starts_made"), m.sem("starts_landed"))
        scores_ready, scores_out = m.sem("scores_ready_s"), m.sem("scores_out_s")
        gap_ready, gate_ready, spread_ready = m.sem("gap_ready"), m.sem("gate_ready_s"), m.sem("spread_ready")
        spread_turned, gates_ready = m.sem("spread_turned"), m.sem("gates_ready_s")
        staged, mid_ready, mid_out = m.sem("staged_s"), m.sem("mid_ready_s"), m.sem("mid_out_s")
        out_ready, out_read, h_ready = m.sem("out_ready_s"), m.sem("out_read_s"), m.sem("h_ready_s")
        turn_ready, added = m.sem("turn_ready"), m.sem("added_s")
        up_routed = m.sem("up_routed_s")
        passed, pe_passed, act_passed = m.sem("passed_s"), m.sem("pe_passed_s"), m.sem("act_passed_s")
        STEPS = 2 * LAYERS + 1
        block = ctx.enter_context(nc.Block())

        def inner(c, layer, eng, ahead, front, back):
            def at(p, i):
                return (i, (c * LAYERS + layer) * GROUPS + p * GB + i, p * (GB * G) + i * G,
                        c * GROUPS + p * GB + i)

            for i in range(ahead):
                front(*at(0, i))
            with eng.Fori(0, PASSES - 1) as p:
                for i in range(GB):
                    front(*at(p, i + ahead))
                    back(*at(p, i))
            for i in range(GB):
                if i + ahead < GB:
                    front(*at(PASSES - 1, i + ahead))
                back(*at(PASSES - 1, i))

        @block.sync
        def _(sp):
            def send(v):
                sp.wait_ge(starts_made, v + 1)
                for layer in range(LAYERS):
                    sp.dma_start(starts[:, layer, :, :], start_i[:, layer, :]).then_inc(starts_landed, 16)

            send(0)
            with sp.Fori(0, NC) as c:
                send(c + 1)

        @block.tensor
        def _(pe):
            pe.sem_inc(turn_ready, DEPTH)
            pe.sem_inc(mid_ready, DEPTH)
            pe.wait_ge(landed, 16 * LOADS)
            pe.wait_ge(zeroed, 1)

            def route_up(c):
                pe.wait_ge(xs_ready, c + 1)
                for k in range(TOK * DT):
                    mm = pe.matmul(p_route[:, 0, 0:E], xs[:, k % DT, k // DT::TOK], ru[:, k, :],
                                   start=(k == 0), stop=(k == TOK * DT - 1))
                mm.then_inc(up_routed, 1)

            def spread_gates(v):
                pe.wait_ge(spread_ready, v + 1)
                pe.matmul(p_route[:, 0, :], ones[:, :], spread[:, :, :, :].rearrange("p l k r -> p (l k r)"),
                          start=True, stop=True).then_inc(spread_turned, 1)

            route_up(0)
            pe.matmul(p_route[:, 1, 0:E], ones[:, :], ru[:, 0, :], start=True, stop=True).then_inc(route_ready, 1)
            spread_gates(0)
            with pe.Fori(0, NC) as c:
                for layer in range(LAYERS):
                    n_in, n_out = ((W1, W2), (W2, W1))[layer]
                    if layer:
                        pe.wait_ge(gates_ready, c + 1)
                        pe.sem_inc(pe_passed, 1)
                        route_up(c + 1)
                        pe.wait_ge(h_ready, (c + 1) * GROUPS + DEPTH)
                        for o in range(W2 // 2):
                            mm = pe.matmul(p_route[0:E, 1, 0:R], rd[:, o, :], h[:, :, o], start=(o == 0), stop=(o == W2 // 2 - 1))
                        mm.then_inc(scores_ready, 1)
                        pe.wait_ge(scores_out, c + 1)
                        pe.sem_inc(pe_passed, 1)
                        pe.transpose(p_route[:, 1, 0:E], scores[:, :], ident[0:E, 0:E]).then_inc(route_ready, 1)
                        spread_gates(c + 1)
                    pe.wait_ge(starts_landed, (c + layer + 1) * 16 * LAYERS + 1)
                    if layer == 0:
                        pe.wait_ge(added, c * TPC + DEPTH)
                    pe.sem_inc(pe_passed, 1)
                    regs = {}

                    def load(i, row):
                        _, regs[i] = nc.values_load_multi_w_load_instructions(
                            starts[0:1, layer, ds(row, G), :].rearrange("o r k -> o (r k)"), min_val=0,
                            max_val=(E - 1) * W2, engines=[mybir.EngineType.PE],
                            skip_runtime_bounds_check_because="places among the experts, times their width")

                    def first(i, n, row, up_n):
                        load(i, row)
                        pe.wait_ge(staged, n + 1)
                        pe.wait_ge(mid_out, n + 1)
                        table = (bu, bad)[layer]
                        for g in range(G):
                            for k in range(K2):
                                col = (g * K2 + k) * W2
                                mm = pe.matmul(p_mid[0:n_in, i % DEPTH, col:col + W2], stage[:, i % DEPTH, g, 0:n_in],
                                               table[:, ds(regs[i][g * K2 + k], W2)], start=True, stop=True)
                        mm.then_inc(mid_ready, 1)

                    def second(i, n, row, up_n):
                        if i == 0:
                            load(i, row)
                        pe.wait_ge(mid_out, n + 1 + DEPTH)
                        pe.wait_ge(out_read, n + 1)
                        table = (au[:, :], bad[:, W1:E * W2])[layer]
                        for g in range(G):
                            for k in range(K2):
                                mm = pe.matmul(p_out[0:n_out, i % DEPTH, g * n_out:(g + 1) * n_out],
                                               mid[:, i % DEPTH, g, k, 0:n_out],
                                               table[:, ds(regs[i][g * K2 + k], n_out)],
                                               start=(k == 0), stop=(k == K2 - 1))
                        mm.then_inc(out_ready, 1)

                    inner(c, layer, pe, 1, first, second)
                pe.wait_ge(out_read, (c + 1) * LAYERS * GROUPS + DEPTH)
                for t in range(TPC):
                    pe.wait_ge(added, c * TPC + t + 1)
                    pe.sem_inc(pe_passed, 1)
                    for f in range(FB):
                        tok = y[:, t * W1:(t + 1) * W1, :].rearrange("p r o -> p (r o)")[:, f::FB]
                        mm = pe.transpose(p_turn[:, t % DEPTH, f * W1:(f + 1) * W1], tok, ident[0:W1, 0:W1])
                    mm.then_inc(turn_ready, 1)

        @block.vector
        def _(dve):
            dve.memset(stage[:, :, :, :], 0.0)
            dve.memset(mid[:, :, :, :, :], 0.0)
            dve.memset(ones[:, :], 1.0).then_inc(zeroed, 1)
            dve.sem_inc(mid_out, DEPTH)
            dve.sem_inc(added, DEPTH)
            dve.sem_inc(starts_landed, 1)
            dve.wait_ge(landed, 16 * LOADS)
            dve.wait_ge(zeroed, 1)

            def take_inputs(c):
                for f in range(FB):
                    q = f % (FB // DT)
                    last = dve.tensor_copy(xn[:, :, f::FB],
                                           XT[q * W1:(q + 1) * W1, f // (FB // DT), ds(c % NC * CH, CH)]
                                           .rearrange("p (r t) -> p r t", t=TOK))
                last.then_inc(xn_ready, 1)

            def route(v):
                chain = Chain(dve, route_steps, v * STEPS)
                dve.wait_ge(up_routed, v + 1)
                dve.wait_ge(route_ready, v + 1)
                for layer in range(LAYERS):
                    dve.sem_inc(passed, 1)
                    chain.link(dve.max(best[:, layer, :], p_route[:, layer, 0:E]))
                    dve.sem_inc(passed, 1)
                    chain.link(dve.max_index(place[:, layer, :], best[:, layer, :], p_route[:, layer, 0:E]))
                dve.tensor_tensor(gap[:, :, 0:1], best[:, :, 0:1], best[:, :, 1:2], ALU.subtract)
                dve.tensor_tensor(gap[:, :, 1:2], best[:, :, 1:2], best[:, :, 0:1], ALU.subtract).then_inc(gap_ready, 1)
                chain.link(dve.tensor_scalar(start_f[:, :, :], place[:, :, 0:K2], float(W2), None, ALU.mult))
                dve.wait_ge(starts_landed, v * 16 * LAYERS + 1)
                dve.tensor_copy(start_i[:, :, :], start_f[:, :, :]).then_inc(starts_made, 1)
                dve.wait_ge(gate_ready, v + 1)
                for layer in range(LAYERS):
                    for k in range(K2):
                        last = dve.tensor_scalar(spread[:, layer, k, :], ident[:, :], gate[:, layer, k:k + 1], None, ALU.mult)
                last.then_inc(spread_ready, 1)
                dve.wait_ge(spread_turned, v + 1)
                dve.tensor_copy(gates[:, :, :, :].rearrange("p l k r -> p (l k r)"), p_route[:, 0, :]
                                ).then_inc(gates_ready, 1)
                dve.wait_ge(gates_ready, v + 1)
                dve.sem_inc(passed, 1)

            take_inputs(0)
            route(0)
            with dve.Fori(0, NC) as c:
                for layer in range(LAYERS):
                    n_in, n_out = ((W1, W2), (W2, W1))[layer]
                    if layer:
                        dve.wait_ge(h_ready, (c + 1) * GROUPS + DEPTH)
                        take_inputs(c + 1)
                        dve.wait_ge(scores_ready, c + 1)
                        dve.tensor_copy(scores[:, :], p_route[0:E, 1, 0:R]).then_inc(scores_out, 1)
                        route(c + 1)

                    def gated(i, n, row, up_n):
                        dve.wait_ge(mid_ready, n + 1 + DEPTH)
                        for k in range(K2):
                            last = dve.tensor_tensor(
                                mid[0:n_in, i % DEPTH, :, k, 0:n_out],
                                p_mid[0:n_in, i % DEPTH, 0:G * K2 * W2].rearrange(
                                    "p (g k o) -> p g k o", g=G, k=K2)[:, :, k, 0:n_out],
                                gates[0:n_in, layer, k, ds(row, G)].unsqueeze(2).to_broadcast([n_in, G, n_out]), ALU.mult)
                        last.then_inc(mid_out, 1)

                    def biased(i, n, row, up_n):
                        dve.wait_ge(out_ready, n + 1)
                        src = p_out[0:n_out, i % DEPTH, 0:G * n_out].rearrange("p (g o) -> p g o", g=G)
                        if layer == 0:
                            dve.wait_ge(h_ready, up_n + 1)
                            dve.scalar_tensor_tensor(pre[:, i % DEPTH, :, :], src, scale_u[:, 0:1],
                                                     bias_u[:, :].unsqueeze(1).to_broadcast([W2, G, W2]),
                                                     ALU.mult, ALU.add).then_inc(out_read, 1)
                        else:
                            dve.scalar_tensor_tensor(y[:, ds(row, G), :], src, scale_d[:, 0:1],
                                                     bias_d[:, :].unsqueeze(1).to_broadcast([W1, G, W1]),
                                                     ALU.mult, ALU.add).then_inc(out_read, 1)

                    inner(c, layer, dve, 1, gated, biased)
                for t in range(TPC):
                    dve.wait_ge(turn_ready, c * TPC + t + 1 + DEPTH)
                    x = X[:, ds(c * TPC + t, 1), :].rearrange("p o d -> p (o d)")
                    dve.tensor_tensor(x, p_turn[:, t % DEPTH, 0:D], x, ALU.add).then_inc(added, 1)

        @block.scalar
        def _(act):
            act.sem_inc(out_read, DEPTH)
            act.sem_inc(h_ready, DEPTH)
            act.wait_ge(landed, 16 * LOADS)
            act.wait_ge(zeroed, 1)

            def take_tokens(c):
                act.copy(xs[:, :, :], XT[:, :, ds(c % NC * CH, CH)]).then_inc(xs_ready, 1)

            def make_gates(v):
                act.wait_ge(gap_ready, v + 1)
                act.activation(gate[:, :, :], gap[:, :, :], ACT.Sigmoid).then_inc(gate_ready, 1)

            take_tokens(0)
            make_gates(0)
            with act.Fori(0, NC) as c:
                for layer in range(LAYERS):
                    n_in, n_out = ((W1, W2), (W2, W1))[layer]
                    if layer == 0:
                        act.wait_ge(xn_ready, c + 1)
                        act.wait_ge(up_routed, c + 1)
                        act.sem_inc(act_passed, 1)
                        take_tokens(c + 1)
                        act.activation(warm[:, :], gap[:, 0, 0:1], ACT.Gelu)
                    else:
                        act.wait_ge(h_ready, (c + 1) * GROUPS + DEPTH)
                        make_gates(c + 1)

                    def staging(i, n, row, up_n):
                        act.wait_ge(mid_ready, n + 1)
                        if layer == 0:
                            last = act.copy(stage[0:W1, i % DEPTH, :, 0:W1], xn[:, ds(row, G), :])
                        else:
                            for odd in range(2):
                                last = act.copy(stage[0:W2, i % DEPTH, :, odd::2],
                                                h[odd * W2:(odd + 1) * W2, ds(row, G), :])
                        last.then_inc(staged, 1)

                    def activated(i, n, row, up_n):
                        if layer == 0:
                            act.wait_ge(out_read, n + 1 + DEPTH)
                            for odd in range(2):
                                last = act.activation(h[odd * W2:(odd + 1) * W2, ds(row, G), :],
                                                      pre[:, i % DEPTH, :, odd::2], ACT.Gelu)
                            last.then_inc(h_ready, 1)

                    inner(c, layer, act, DEPTH, staging, activated)



def program(nc, a, out):
    with ExitStack() as ctx:
        m = Mem(nc, ctx)
        X = m.sb("X", [P, NT, D])
        XT = m.sb("XT", [P, DT, N])
        ident = m.sb("ident", [P, P])
        load_tokens(nc, a["x"], X, a["ident"], ident, XT)
        with ExitStack() as c2:
            heads = c2.enter_context(nc.sbuf_tensor("heads", [P, B * NG, S // P, HG * HD], F32))
            q_parts = nc.dram_tensor("q_parts", (3, B * D, S), BF16).ap()
            k_parts = nc.dram_tensor("k_parts", (3, B * D, S), BF16).ap()
            v_rows = nc.dram_tensor("v_rows", (B * NG, S, HG * 2 * HD), F32).ap()
            attention_project(nc, a, XT, q_parts, k_parts, v_rows)
            attention(nc, a, q_parts, k_parts, v_rows, heads, ident)
            attention_output(nc, a, X, heads, ident)
        with ExitStack() as c2:
            w = Mem(nc, c2)
            weights, loads = cross_weights(w, a)
            landed = w.sem("landed_x")
            layer_norm(nc, "_0a", X, XT, ident, loads, landed)
            sigmoid_cross(nc, a, weights, landed, len(loads), X, XT)
        with ExitStack() as c2:
            w = Mem(nc, c2)
            weights, loads = mlp_weights(w, a)
            landed = w.sem("landed_m")
            layer_norm(nc, "_0x", X, XT, ident, loads, landed)
            gated_mlp(nc, weights, landed, len(loads), X, XT)
        with ExitStack() as c2:
            sim = c2.enter_context(nc.sbuf_tensor("sim", [P, NT, 2 * NH * NK], F32))
            thr = c2.enter_context(nc.sbuf_tensor("thr", [P, NT, NH], F32))
            shift = c2.enter_context(nc.sbuf_tensor("shift", [P, NT, NH], F32))
            peer_gates(nc, a, XT, sim, thr, shift)
            peer_experts(nc, a, X, XT, sim, thr, shift, ident)
        layer_norm(nc, "_0f", X, XT, ident)
        with ExitStack() as c2:
            grams = c2.enter_context(nc.sbuf_tensor("grams", [P, B * DT, 2, P], F32))
            vsum = c2.enter_context(nc.sbuf_tensor("vsum", [P, B * DT], F32))
            key_products(nc, a, XT, grams, vsum)
            normed_attention(nc, a, X, XT, grams, vsum)
        layer_norm(nc, "_1a", X, None, ident)
        Z = m.sb("Z", [P, NT, D])
        circular_filter(nc, a, X, Z)
        with ExitStack() as c2:
            w = Mem(nc, c2)
            weights, loads, blank = kronecker_weights(w, a)
            landed = w.sem("landed_s")
            layer_norm(nc, "_1x", Z, XT, ident, loads, landed, blank)
            kronecker_experts(nc, weights, landed, len(loads), Z, XT, X, ident)
        layer_norm(nc, "_1f", Z, None, ident)
        X = Z
        store_tokens(nc, X, out)


def kernel(**inputs):
    import concourse.bacc as _bacc
    from concourse.bass_utils import run_bass_kernel_spmd as _run

    arrays = {k: np.ascontiguousarray(v) for k, v in lay_out(inputs).items()}
    nc = _bacc.Bacc("TRN2", target_bir_lowering=False, num_devices=1)
    aps = {k: nc.dram_tensor("in_" + k, v.shape, mybir.dt.from_np(v.dtype), kind="ExternalInput").ap()
           for k, v in arrays.items()}
    out = nc.dram_tensor("out_0", (B, S, D), F32, kind="ExternalOutput").ap()
    program(nc, aps, out)
    r = _run(nc, [{"in_" + k: v for k, v in arrays.items()}], core_ids=[0])
    return r.results[0]["out_0"]


def fourier():
    L = 2 * P
    n, k = np.arange(L)[:, None], np.arange(P)[None, :]
    angle = 2 * np.pi * ((n * k) % L) / L
    last = np.where(n % 2 == 0, 1.0, -1.0)
    cos, sin = np.cos(angle), -np.sin(angle)
    sin_last = sin.copy()
    sin_last[:, :1] = last
    cos_last = cos.copy()
    cos_last[:, :1] = last
    back = np.full((P, 1), 2.0 / L)
    back[0] = 1.0 / L
    fwd = np.stack([cos[:P], cos[P:], sin_last[:P], sin_last[P:]])
    return {
        "dft_fwd": fwd.astype(np.float32),
        "dft_taps": np.stack([cos[:P], sin[:P], cos_last[:P]]).astype(np.float32),
        "dft_inv": np.stack([back * cos[P:].T, back * sin_last[P:].T]).astype(np.float32),
    }


def lay_out(inputs):
    def heads_last(w):
        return np.transpose(w, (1, 0, 2)).reshape(w.shape[1], -1)

    def table(w):
        return np.transpose(w, (2, 0, 1)).reshape(w.shape[2], -1)

    def padded(w, axis):
        shape = list(w.shape)
        shape[axis] = P
        full = np.zeros(shape, w.dtype)
        full[tuple(slice(0, n) for n in w.shape)] = w
        return full

    def peer_keys(keys):
        heads, count, halves, n = keys.shape
        full = np.zeros((halves * heads, n, 2, count), keys.dtype)
        for half in range(halves):
            for h in range(heads):
                g = half * heads + h
                full[g, :, g % 2, :] = keys[h, :, half, :].T
        return full.reshape(halves * heads * n, 2 * count)

    i = {k: np.asarray(v) for k, v in inputs.items()}
    return {
        "x": i["x"],
        "ident": np.eye(P, dtype=np.float32),
        "wq0": heads_last(i["L0_attn_W_query"]),
        "wk0": heads_last(i["L0_attn_W_key"]),
        "wv0": heads_last(i["L0_attn_W_val"]),
        "wo0": i["L0_attn_W_out"].reshape(D, D),
        "ctx_t": np.transpose(i["ctx_1024"], (2, 0, 1)).reshape(D, B * CTX),
        "wq_x": padded(i["L0_xattn_Wq"].T, 1),
        "wk_x": padded(i["L0_xattn_Wk"].T, 1),
        "wv_x": i["L0_xattn_Wv"].T,
        "bq_x": padded(i["L0_xattn_bq"][:, None], 0),
        "bk_x": padded(i["L0_xattn_bk"][:, None], 0),
        "bv_x": i["L0_xattn_bv"][None, :],
        "wg": i["L0_ffn_Wg"],
        "wu": i["L0_ffn_Wu"],
        "wd": i["L0_ffn_Wd"],
        "bg": i["L0_ffn_bg"].reshape(FF // P, P).T,
        "bu": i["L0_ffn_bu"].reshape(FF // P, P).T,
        "bd": i["L0_ffn_bd"][None, :],
        "peer_wq_t": i["L0_ffn_Wq"].T,
        "peer_keys": peer_keys(i["L0_ffn_keys"]),
        "down_t": i["L0_ffn_down_embed"].T,
        "up": i["L0_ffn_up_embed"],
        "wkv1": i["L1_attn_w_qkv"][D:, :].T,
        "wq1": i["L1_attn_w_qkv"][:D, :].T,
        "wo1": i["L1_attn_w_out"].T,
        "bo1": i["L1_attn_b_out"][None, :],
        "norm_g": np.repeat(i["L1_attn_norm_g"].reshape(H0), HD).reshape(DT, P).T,
        "norm_b": np.repeat(i["L1_attn_norm_b"].reshape(H0), HD).reshape(DT, P).T,
        "mask": np.kron(np.eye(P // HD), np.ones((HD, HD))).astype(np.float32),
        "taps_t": i["L1_xattn_weight"].T,
        "kp_w_t": i["L1_xattn_kp_w"].T,
        "kp_b": i["L1_xattn_kp_b"][None, :],
        **fourier(),
        "b_up": table(i["L1_ffn_B_up"]),
        "a_up": table(i["L1_ffn_A_up"]),
        "ba_down": table(np.concatenate([i["L1_ffn_B_down"], i["L1_ffn_A_down"]], 1)),
        "route_up": i["L1_ffn_W_up"].T,
        "route_down": np.transpose(i["L1_ffn_W_down"].reshape(E, 32, 2, 64), (2, 3, 1, 0)).reshape(P, 32, E),
        "bias_up": i["L1_ffn_bias_up"].reshape(64, 64).T,
        "bias_down": i["L1_ffn_bias_down"].reshape(32, 32).T,
        "scale_up": i["L1_ffn_scale_up"][None, :],
        "scale_down": i["L1_ffn_scale_down"][None, :],
    }
```
